# Optimizing a Trainium2 kernel written in Bass

```python
import numpy as np
import jax
import jax.numpy as jnp

def _softmax(x, axis=-1):
    return jax.nn.softmax(x, axis=axis)

def _gelu(x):
    return jax.nn.gelu(x, approximate=True)

def _silu(x):
    return jax.nn.silu(x)

def _sigmoid(x):
    return jax.nn.sigmoid(x)

def _layernorm(x, axis=-1, eps=1e-05):
    m = jnp.mean(x, axis=axis, keepdims=True)
    v = jnp.var(x, axis=axis, keepdims=True)
    return (x - m) / jnp.sqrt(v + eps)

def _scatter_add(tgt, idx, src, axis=0):
    return tgt.at[idx].add(src)

def _segment_sum(src, seg, n):
    return jax.ops.segment_sum(src, seg, n)
kernel_name = 'mk_recurrent_d2_jaxref_r8_44003b'

def setup_inputs(seed: int=0):
    np.random.seed(seed)
    _w = jnp.asarray

    def _L0_attn_setup():
        import jax, jax.numpy as jnp
        import numpy as np
        B, L, D_OUT, D_HIDDEN = (16, 512, 128, 64)
        MAX_PHASE = 6.28
        R_MIN, R_MAX = (0.9, 0.999)

        def _binop(q_i, q_j):
            A_i, b_i = q_i
            A_j, b_j = q_j
            return (A_j * A_i, A_j * b_i + b_j)

        def _reference_tuple_inner(x, theta_log, nu_log, gamma_log, B_re, B_im, C_re, C_im, D):
            diag_lambda = jnp.exp(-jnp.exp(nu_log) + 1j * jnp.exp(theta_log))
            B_norm = (B_re + 1j * B_im) * jnp.exp(gamma_log)[:, None]
            C = C_re + 1j * C_im
            Bu = jnp.einsum('hd,bld->blh', B_norm, x.astype(B_norm.dtype))
            Lam = jnp.broadcast_to(diag_lambda, Bu.shape)
            _, h = jax.lax.associative_scan(_binop, (Lam, Bu), axis=1)
            y = jnp.einsum('oh,blh->blo', C, h).real + D * x
            return (y, h[:, -1])
        key = jax.random.key(seed)
        ks = jax.random.split(key, 8)
        x = jax.random.normal(ks[0], (B, L, D_OUT), dtype=jnp.float32)
        u_th = jax.random.uniform(ks[1], (D_HIDDEN,), dtype=jnp.float32)
        theta_log = jnp.log(MAX_PHASE * u_th)
        u_nu = jax.random.uniform(ks[2], (D_HIDDEN,), dtype=jnp.float32)
        nu_log = jnp.log(-0.5 * jnp.log(u_nu * (R_MAX ** 2 - R_MIN ** 2) + R_MIN ** 2))
        diag_lambda = jnp.exp(-jnp.exp(nu_log) + 1j * jnp.exp(theta_log))
        gamma_log = jnp.log(jnp.sqrt(1.0 - jnp.abs(diag_lambda) ** 2))
        b_norm = jnp.sqrt(2.0 * D_OUT)
        c_norm = jnp.sqrt(float(D_HIDDEN))
        B_re = jax.random.normal(ks[3], (D_HIDDEN, D_OUT), dtype=jnp.float32) / b_norm
        B_im = jax.random.normal(ks[4], (D_HIDDEN, D_OUT), dtype=jnp.float32) / b_norm
        C_re = jax.random.normal(ks[5], (D_OUT, D_HIDDEN), dtype=jnp.float32) / c_norm
        C_im = jax.random.normal(ks[6], (D_OUT, D_HIDDEN), dtype=jnp.float32) / c_norm
        D = jax.random.normal(ks[7], (D_OUT,), dtype=jnp.float32)
        return {'x': x, 'theta_log': theta_log, 'nu_log': nu_log, 'gamma_log': gamma_log, 'B_re': B_re, 'B_im': B_im, 'C_re': C_re, 'C_im': C_im, 'D': D}
    _L0_attn_in = _L0_attn_setup()

    def _L0_ffn_setup():
        import jax, jax.numpy as jnp
        import numpy as np
        NUM_HEADS = 16
        TOP_K = 2
        key = jax.random.key(seed)
        ks = jax.random.split(key, 5)
        B, S, D, E = (4, 256, 128, 8)
        scale = 0.02
        return {'x': jax.random.normal(ks[0], (B, S, D), dtype=jnp.float32), 'W_qkv': jax.random.normal(ks[1], (D, 3 * D), dtype=jnp.float32) * scale, 'b_qkv': jnp.zeros((3 * D,), dtype=jnp.float32), 'W_gate': jax.random.normal(ks[2], (D, E), dtype=jnp.float32) * scale, 'b_gate': jnp.zeros((E,), dtype=jnp.float32), 'W_experts': jax.random.normal(ks[3], (E, D, D), dtype=jnp.float32) * scale, 'b_experts': jnp.zeros((E, D), dtype=jnp.float32)}
    _L0_ffn_in = _L0_ffn_setup()

    def _L1_attn_setup():
        import jax, jax.numpy as jnp
        import numpy as np
        import math
        DIM = 128
        HEADS = 16
        HEAD_DIM = 64
        WINDOW = 32
        GLOBAL = 64
        B, S = (1, 512)

        def _sparse_mask(seq_len, window, global_tokens):
            i = jnp.arange(seq_len)[:, None]
            j = jnp.arange(seq_len)[None, :]
            half = window // 2
            local = (j >= i - half) & (j <= i + half)
            glob = (j < global_tokens) | (i < global_tokens)
            causal = j <= i
            return ((local | glob) & causal)[None, None, :, :]
        key = jax.random.key(seed)
        k1, k2, k3 = jax.random.split(key, 3)
        x = jax.random.normal(k1, (B, S, DIM), dtype=jnp.float32)
        w_qkv = jax.random.normal(k2, (DIM, 3 * HEADS * HEAD_DIM), dtype=jnp.float32) * (1.0 / math.sqrt(DIM))
        w_out = jax.random.normal(k3, (HEADS * HEAD_DIM, DIM), dtype=jnp.float32) * (1.0 / math.sqrt(HEADS * HEAD_DIM))
        return {'x': x, 'w_qkv': w_qkv, 'w_out': w_out}
    _L1_attn_in = _L1_attn_setup()

    def _L1_ffn_setup():
        import jax, jax.numpy as jnp
        import numpy as np
        HIDDEN = 128
        INTER = 512
        key = jax.random.key(seed)
        k1, k2, k3, k4, k5 = jax.random.split(key, 5)
        hidden_states = jax.random.normal(k1, (4, 256, HIDDEN), dtype=jnp.float32)
        W1 = jax.random.normal(k2, (HIDDEN, INTER), dtype=jnp.float32) * (1.0 / np.sqrt(HIDDEN))
        b1 = jax.random.normal(k3, (INTER,), dtype=jnp.float32) * 0.02
        W2 = jax.random.normal(k4, (INTER, HIDDEN), dtype=jnp.float32) * (1.0 / np.sqrt(INTER))
        b2 = jax.random.normal(k5, (HIDDEN,), dtype=jnp.float32) * 0.02
        return {'hidden_states': hidden_states, 'W1': W1, 'b1': b1, 'W2': W2, 'b2': b2}
    _L1_ffn_in = _L1_ffn_setup()
    _d = {'L0_attn_x': _L0_attn_in['x'], 'L0_attn_theta_log': _L0_attn_in['theta_log'], 'L0_attn_nu_log': _L0_attn_in['nu_log'], 'L0_attn_gamma_log': _L0_attn_in['gamma_log'], 'L0_attn_B_re': _L0_attn_in['B_re'], 'L0_attn_B_im': _L0_attn_in['B_im'], 'L0_attn_C_re': _L0_attn_in['C_re'], 'L0_attn_C_im': _L0_attn_in['C_im'], 'L0_attn_D': _L0_attn_in['D'], 'L0_ffn_W_qkv': _L0_ffn_in['W_qkv'], 'L0_ffn_b_qkv': _L0_ffn_in['b_qkv'], 'L0_ffn_W_gate': _L0_ffn_in['W_gate'], 'L0_ffn_b_gate': _L0_ffn_in['b_gate'], 'L0_ffn_W_experts': _L0_ffn_in['W_experts'], 'L0_ffn_b_experts': _L0_ffn_in['b_experts'], 'L1_attn_w_qkv': _L1_attn_in['w_qkv'], 'L1_attn_w_out': _L1_attn_in['w_out'], 'L1_ffn_W1': _L1_ffn_in['W1'], 'L1_ffn_b1': _L1_ffn_in['b1'], 'L1_ffn_W2': _L1_ffn_in['W2'], 'L1_ffn_b2': _L1_ffn_in['b2']}
    _x0 = _d['L0_attn_x']
    _d['L0_attn_x'] = jax.random.normal(jax.random.fold_in(jax.random.key(seed), 1), (1, 2048, 128), dtype=_x0.dtype)
    del _x0
    return _d

def reference(L0_attn_x, L0_attn_theta_log, L0_attn_nu_log, L0_attn_gamma_log, L0_attn_B_re, L0_attn_B_im, L0_attn_C_re, L0_attn_C_im, L0_attn_D, L0_ffn_W_qkv, L0_ffn_b_qkv, L0_ffn_W_gate, L0_ffn_b_gate, L0_ffn_W_experts, L0_ffn_b_experts, L1_attn_w_qkv, L1_attn_w_out, L1_ffn_W1, L1_ffn_b1, L1_ffn_W2, L1_ffn_b2):

    def _L0_attn_ref(x, theta_log, nu_log, gamma_log, B_re, B_im, C_re, C_im, D):
        import jax, jax.numpy as jnp
        import numpy as np
        B, L, D_OUT, D_HIDDEN = (16, 512, 128, 64)
        MAX_PHASE = 6.28
        R_MIN, R_MAX = (0.9, 0.999)

        def _binop(q_i, q_j):
            A_i, b_i = q_i
            A_j, b_j = q_j
            return (A_j * A_i, A_j * b_i + b_j)

        def _reference_tuple_inner(x, theta_log, nu_log, gamma_log, B_re, B_im, C_re, C_im, D):
            diag_lambda = jnp.exp(-jnp.exp(nu_log) + 1j * jnp.exp(theta_log))
            B_norm = (B_re + 1j * B_im) * jnp.exp(gamma_log)[:, None]
            C = C_re + 1j * C_im
            Bu = jnp.einsum('hd,bld->blh', B_norm, x.astype(B_norm.dtype))
            Lam = jnp.broadcast_to(diag_lambda, Bu.shape)
            _, h = jax.lax.associative_scan(_binop, (Lam, Bu), axis=1)
            y = jnp.einsum('oh,blh->blo', C, h).real + D * x
            return (y, h[:, -1])
        return _reference_tuple_inner(x, theta_log, nu_log, gamma_log, B_re, B_im, C_re, C_im, D)[0]

    def _L0_ffn_ref(x, W_qkv, b_qkv, W_gate, b_gate, W_experts, b_experts):
        import jax, jax.numpy as jnp
        import numpy as np
        NUM_HEADS = 16
        TOP_K = 2
        B, S, D = x.shape
        H = NUM_HEADS
        hd = D // H
        E = W_gate.shape[-1]
        qkv = (x @ W_qkv + b_qkv).reshape(B, S, 3, H, hd)
        q, k, v = (qkv[:, :, 0], qkv[:, :, 1], qkv[:, :, 2])
        attn = jnp.einsum('bqhd,bkhd->bhqk', q, k) / jnp.sqrt(jnp.asarray(hd, x.dtype))
        attn = jax.nn.softmax(attn, axis=-1)
        attn_out = jnp.einsum('bhqk,bkhd->bqhd', attn, v).reshape(B, S, D)
        gate = jax.nn.softmax(x @ W_gate + b_gate, axis=-1)
        top_g, top_i = jax.lax.top_k(gate, TOP_K)
        combine = jnp.sum(jax.nn.one_hot(top_i, E, dtype=x.dtype) * top_g[..., None], axis=2)
        expert_out = jnp.einsum('bsd,edf->bsef', x, W_experts) + b_experts
        moe_out = jnp.einsum('bsef,bse->bsf', expert_out, combine)
        return attn_out + moe_out

    def _L1_attn_ref(x, w_qkv, w_out):
        import jax, jax.numpy as jnp
        import numpy as np
        import math
        DIM = 128
        HEADS = 16
        HEAD_DIM = 64
        WINDOW = 32
        GLOBAL = 64
        B, S = (1, 512)

        def _sparse_mask(seq_len, window, global_tokens):
            i = jnp.arange(seq_len)[:, None]
            j = jnp.arange(seq_len)[None, :]
            half = window // 2
            local = (j >= i - half) & (j <= i + half)
            glob = (j < global_tokens) | (i < global_tokens)
            causal = j <= i
            return ((local | glob) & causal)[None, None, :, :]
        b, s, _ = x.shape
        scale = 1.0 / math.sqrt(HEAD_DIM)
        qkv = x @ w_qkv
        qkv = qkv.reshape(b, s, 3, HEADS, HEAD_DIM)
        q, k, v = jnp.transpose(qkv, (2, 0, 3, 1, 4))
        mask = _sparse_mask(s, WINDOW, GLOBAL)
        scores = jnp.einsum('bhid,bhjd->bhij', q, k) * scale
        scores = jnp.where(mask, scores, -jnp.inf)
        attn = jax.nn.softmax(scores, axis=-1)
        out = jnp.einsum('bhij,bhjd->bhid', attn, v)
        out = jnp.transpose(out, (0, 2, 1, 3)).reshape(b, s, HEADS * HEAD_DIM)
        return out @ w_out

    def _L1_ffn_ref(hidden_states, W1, b1, W2, b2):
        import jax, jax.numpy as jnp
        import numpy as np
        HIDDEN = 128
        INTER = 512
        h = jax.nn.relu(jnp.einsum('bsh,hi->bsi', hidden_states, W1) + b1)
        return jnp.einsum('bsi,ih->bsh', h, W2) + b2
    x = L0_attn_x
    xn = _layernorm(x, axis=-1)
    s = _L0_attn_ref(xn, L0_attn_theta_log, L0_attn_nu_log, L0_attn_gamma_log, L0_attn_B_re, L0_attn_B_im, L0_attn_C_re, L0_attn_C_im, L0_attn_D)
    g = _silu(_L0_ffn_ref(xn, L0_ffn_W_qkv, L0_ffn_b_qkv, L0_ffn_W_gate, L0_ffn_b_gate, L0_ffn_W_experts, L0_ffn_b_experts))
    x = x + s * g
    xn = _layernorm(x, axis=-1)
    s = _L1_attn_ref(xn, L1_attn_w_qkv, L1_attn_w_out)
    g = _silu(_L1_ffn_ref(xn, L1_ffn_W1, L1_ffn_b1, L1_ffn_W2, L1_ffn_b2))
    x = x + s * g
    return x

_drawn_inputs = setup_inputs


def setup_inputs(seed=0):
    import zlib

    import numpy as np

    out = dict(_drawn_inputs(seed))
    spreads = {'L0_ffn_b_qkv': (0.0, 0.1),
     'L0_ffn_b_gate': (0.0, 0.413),
     'L0_ffn_b_experts': (0.0, 0.496)}
    factors = {'L0_ffn_W_qkv': 8.0, 'L1_ffn_b1': 43.512, 'L1_ffn_b2': 28.415}
    for name, (base, spread) in spreads.items():
        noise = np.random.default_rng([zlib.crc32(name.encode()), seed]).standard_normal(out[name].shape)
        drawn = base * np.exp(spread * noise) if base else spread * noise
        out[name] = jnp.asarray(drawn.astype(out[name].dtype))
    for name, factor in factors.items():
        out[name] = (out[name] * factor).astype(out[name].dtype)
    return out
```

```python
import concourse.bass as bass
from concourse import mybir
from contextlib import ExitStack


def recurrent_moe_sparse_attention_kernel(
    nc, x, theta_log, nu_log, gamma_log, B_re, B_im, C_re, C_im, D_skip,
    W_qkv0, b_qkv0, W_gate, b_gate, W_experts, b_experts,
    W_qkv1, W_out1, W1, b1, W2, b2, out,
):
    fp32 = mybir.dt.float32
    bf16 = mybir.dt.bfloat16
    i32 = mybir.dt.int32
    ALU = mybir.AluOpType
    ACT = mybir.ActivationFunctionType
    AX = mybir.AxisListType
    ds = bass.ds

    P = 128
    S, D = x.shape[1], x.shape[2]
    NT = S // P
    CH = 512
    NC = S // CH
    TPC = CH // P
    EPS = 1e-5
    HID = theta_log.shape[0]
    NE = W_gate.shape[1]
    H0 = 16
    HD0 = D // H0
    G0 = 4
    NG0 = H0 // G0
    NB = NC * NG0
    SC0 = float(HD0) ** -0.5
    NPROD = 6
    KR = NPROD * HD0
    H1 = 16
    HD1 = W_out1.shape[0] // H1
    NP1 = H1 // 2
    SC1 = float(HD1) ** -0.5
    HALF = 16
    GLOB = 64
    WIN = P + HALF
    KW = WIN + GLOB
    TAIL = KW - P
    NI = W1.shape[1] // P
    NEG = -1.0e30
    BIG = 3.0e38
    TWO_PI_HI = 6.28125
    TWO_PI_LO = 0.0019353071795864769
    PI_2 = 1.5707963267948966

    ctx = ExitStack()
    with ctx:
        def sb(name, shape, dt=fp32):
            return ctx.enter_context(nc.sbuf_tensor(name, shape, dt))

        def sem(name):
            return ctx.enter_context(nc.semaphore(name))

        x_sb = sb("x_sb", [P, NT, D])
        xT = sb("xT", [P, S])
        layer0 = sb("layer0", [P, 3, S])
        y_sb, attn_sb, v_sb = [layer0[:, n, :].rearrange("p (t d) -> p t d", d=D) for n in range(3)]
        gate_sb = sb("gate_sb", [P, NT, D])
        ident = sb("ident", [P, P])
        ones_row = sb("ones_row", [1, P])
        w1qkv_sb = sb("w1qkv_sb", [P, 3, H1 * HD1])
        wout_sb = sb("wout_sb", [P, NP1, D])
        W1_sb = sb("W1_sb", [P, NI * P])
        W2_sb = sb("W2_sb", [P, NI, D])
        b1_sb = sb("b1_sb", [P, NI])
        b2_sb = sb("b2_sb", [1, D])
        stats = sb("stats", [P, NT, 6])
        mv = sb("mv", [P, NT, 2])
        var_eps = sb("var_eps", [P, NT])
        std = sb("std", [P, NT])
        rstd = sb("rstd", [P, NT])
        masks = sb("masks", [P, KW])
        mask0 = sb("mask0", [P, P])

        ARENA = 24576
        arena = sb("arena", [P, ARENA])

        def cut(at, words):
            assert at + words <= ARENA
            return arena[:, at:at + words]

        xn_sb = cut(0, S).rearrange("p (t d) -> p t d", d=D)
        cos_t, sin_t, rot_x, state, st_cos, st_sin = [cut(S * (n + 1), S) for n in range(6)]
        partsQ = cut(7 * S, 3 * S // 2).bitcast(bf16).rearrange("p (a n) -> p a n", a=3)
        partsK = cut(7 * S + 3 * S // 2, 3 * S // 2).bitcast(bf16).rearrange("p (a n) -> p a n", a=3)
        qk32 = cut(10 * S, 2 * CH).rearrange("p (a n) -> p a n", a=2)
        rest = cut(10 * S + 2 * CH, 2 * CH).rearrange("p (a n) -> p a n", a=2)
        kmax = [cut(S * n, S).bitcast(bf16).rearrange("p (t n) -> p t n", t=2) for n in range(2)]
        kexp = [cut(S * (2 + n), S).bitcast(bf16).rearrange("p (t n) -> p t n", t=2) for n in range(2)]
        qmax = [cut(4 * S + CH * n, CH).bitcast(bf16).rearrange("p (t n) -> p t n", t=2) for n in range(2)]
        qexp = [cut(4 * S + CH * (2 + n), CH).bitcast(bf16).rearrange("p (t n) -> p t n", t=2)
                for n in range(2)]
        probs = [cut(5 * S + 2 * CH * n, 2 * CH).rearrange("p (g n) -> p g n", g=2) for n in range(4)]
        vst = [cut(7 * S + S * n, S).rearrange("p (t j d) -> p t j d", j=G0, d=32) for n in range(2)]
        outT0 = [cut(9 * S + CH * n, CH) for n in range(2)]
        outT1 = cut(0, NP1 * S).rearrange("p (h n) -> p h n", h=NP1)
        hT = cut(0, NI * S).rearrange("p (i n) -> p i n", i=NI)
        qT = cut(8 * S, S)
        kT = cut(9 * S, S)
        v1 = cut(10 * S, S).rearrange("p (t d) -> p t d", d=P)
        v2 = cut(11 * S, S).rearrange("p (t d) -> p t d", d=P)

        prm = sb("prm", [P, 3])
        eprm = sb("eprm", [P, 3])
        r_col = sb("r_col", [P, 1])
        ang = sb("ang", [P, 8])
        ang_i = sb("ang_i", [P, 1], i32)
        pw = sb("pw", [P, 12, 4])
        rot_tmp = sb("rot_tmp", [P, S // 2])
        B_sb = sb("B_sb", [P, 2, D])
        C_sb = sb("C_sb", [P, 2, 2 * HID])
        BT = sb("BT", [P, 2, P])
        CT = sb("CT", [P, 2, D])
        D_col = sb("D_col", [P, 1])
        D_diag = sb("D_diag", [P, P])
        w0_sb = sb("w0_sb", [P, 3, D])
        bqk_col = sb("bqk_col", [P, 2])
        bv_row = sb("bv_row", [1, D])
        wg_sb = sb("wg_sb", [P, NE])
        bg_row = sb("bg_row", [1, NE])
        we_sb = sb("we_sb", [P, NE, D])
        be_sb = sb("be_sb", [NE, D])
        logits = sb("logits", [P, NT, NE])
        gmax = sb("gmax", [P, NT])
        gsum = sb("gsum", [P, NT])
        gates = sb("gates", [P, NT, NE])
        beats = cut(11 * S, NT * NE * NE).rearrange("p (t e j) -> p t e j", e=NE, j=NE)
        ties = cut(11 * S + NT * NE * NE, NT * NE * NE).rearrange("p (t e j) -> p t e j", e=NE, j=NE)
        lower = sb("lower", [P, NE, NE])
        combT = sb("combT", [NE, S])
        tile_max = sb("tile_max", [P, 2 * TPC * 2, NC])
        neg_max = sb("neg_max", [P, 2 * TPC * 2])
        max_rows = sb("max_rows", [2 * TPC * 2, 2, P], bf16)
        rden0 = sb("rden0", [P, TPC * G0])
        xtail = sb("xtail", [P, NT, TAIL])
        wst = sb("wst", [P, 3, P])
        NSLOT = 8
        p1 = layer0[:, :, :].rearrange("p a n -> p (a n)")[:, 0:NSLOT * 2 * KW]\
            .rearrange("p (s g n) -> p s g n", g=2, n=KW)
        nmax1 = sb("nmax1", [P, NSLOT, 2])
        rsum1 = sb("rsum1", [P, NSLOT, 2])
        rinv1 = sb("rinv1", [P, NSLOT, 2])
        pT = layer0[:, 2, :].rearrange("p (s n) -> p s n", n=CH)
        tmp = rot_tmp[:, :].rearrange("p (s n) -> p s n", n=CH)

        ps = ctx.enter_context(nc.psum_tensor("ps", [P, 8, CH], fp32))

        q_parts = nc.dram_tensor("q_parts", [NPROD, P, S], bf16, kind="Internal").ap()
        k_parts = nc.dram_tensor("k_parts", [NPROD, P, S], bf16, kind="Internal").ap()
        Q_PART = [0, 0, 0, 1, 1, 2]
        K_PART = [0, 1, 2, 0, 1, 0]

        x_loaded = sem("x_loaded")
        rec_loaded = sem("rec_loaded")
        att_loaded = sem("att_loaded")
        moe_loaded = sem("moe_loaded")
        l1_loaded = sem("l1_loaded")
        consts_made = sem("consts_made")
        stats_done = sem("stats_done")
        std_done = sem("std_done")
        xn_done = sem("xn_done")
        prm_done = sem("prm_done")
        angle_steps = sem("angle_steps")
        sin_done = sem("sin_done")
        filled = sem("filled")
        act_drained = sem("act_drained")
        dve_drained = sem("dve_drained")
        parts_done = sem("parts_done")
        parts_steps = sem("parts_steps")
        hi_done = sem("hi_done")
        table_steps = sem("table_steps")
        rot_done = sem("rot_done")
        rot_steps = sem("rot_steps")
        scan_done = sem("scan_done")
        back_done = sem("back_done")
        diag_done = sem("diag_done")
        gate_steps = sem("gate_steps")
        gexp_in = sem("gexp_in")
        gexp_done = sem("gexp_done")
        comb_done = sem("comb_done")
        moe_steps = sem("moe_steps")
        parts_stored = sem("parts_stored")

        jobs = [("xT", c, "act") for c in range(NC)]
        jobs += [("BT", 0, "act"), ("CT", 0, "act")]
        jobs += [(k, c, "act") for k in ("q", "k") for c in range(NC)]
        jobs += [("logits", 0, "dve")]
        jobs += [("v", c, "act") for c in range(NC)]
        jobs += [(k, c, "dve") for c in range(NC) for k in ("u", "w")]
        jobs += [("combT", c, "act") for c in range(NC)]
        jobs += [("bias", c, "act") for c in range(NC)]
        jobs += [("experts", n, "dve") for n in range(2 * NT)]
        jobs += [("y", c, "act") for c in range(NC)]
        nth = {}
        seen = {"act": 0, "dve": 0}
        for n, (kind, c, eng) in enumerate(jobs):
            seen[eng] += 1
            nth[kind, c] = (n, seen[eng])
        drained = {"act": act_drained, "dve": dve_drained}

        def bank(kind, c):
            return ps[:, nth[kind, c][0] % 8, :]

        with nc.Block() as block:
            @block.sync
            def _(sp):
                sp.dma_start(x_sb[:, :, :], x[0].rearrange("(t p) d -> p t d", p=P)).then_inc(x_loaded, 16)
                sp.dma_start(w0_sb[:, :, :], W_qkv0.rearrange("k (s n) -> k s n", s=3)).then_inc(att_loaded, 16)
                sp.dma_start(bqk_col[:, 0:1], b_qkv0[0:D].rearrange("(p a) -> p a", a=1)).then_inc(att_loaded, 16)
                sp.dma_start(bqk_col[:, 1:2], b_qkv0[D:2 * D].rearrange("(p a) -> p a", a=1)).then_inc(att_loaded, 16)
                sp.dma_start(bv_row[:, :], b_qkv0[2 * D:3 * D].rearrange("(a n) -> a n", a=1)).then_inc(att_loaded, 16)
                sp.dma_start(wg_sb[:, :], W_gate).then_inc(moe_loaded, 16)
                sp.dma_start(bg_row[:, :], b_gate.rearrange("(a n) -> a n", a=1)).then_inc(moe_loaded, 16)
                sp.dma_start(we_sb[:, :, :], W_experts.rearrange("e d f -> d e f")).then_inc(moe_loaded, 16)
                sp.dma_start(be_sb[:, :], b_experts).then_inc(moe_loaded, 16)
                sp.dma_start(w1qkv_sb[:, :, :], W_qkv1.rearrange("k (s n) -> k s n", s=3)).then_inc(l1_loaded, 16)
                sp.dma_start(wout_sb[:, :, :], W_out1.rearrange("(h p) n -> p h n", p=P)).then_inc(l1_loaded, 16)
                sp.dma_start(W1_sb[:, :], W1).then_inc(l1_loaded, 16)
                sp.dma_start(W2_sb[:, :, :], W2.rearrange("(p i) n -> p i n", p=P)).then_inc(l1_loaded, 16)
                sp.dma_start(b1_sb[:, :], b1.rearrange("(p i) -> p i", p=P)).then_inc(l1_loaded, 16)
                sp.dma_start(b2_sb[:, :], b2.rearrange("(a n) -> a n", a=1)).then_inc(l1_loaded, 16)
                for n, (parts, order, dram) in enumerate(((partsQ, Q_PART, q_parts), (partsK, K_PART, k_parts))):
                    sp.wait_ge(parts_done, NC * (n + 1))
                    for r in range(NPROD):
                        sp.dma_start(dram[r], parts[:, order[r], :]).then_inc(parts_stored, 16)
                sp.wait_ge(parts_stored, 2 * NPROD * 16)
                sp.wait_ge(l1_loaded, 6 * 16)

            @block.gpsimd
            def _(pool):
                pool.memset(ident[:, :], 0.0).then_inc(consts_made, 1)
                pool.memset(ones_row[:, :], 1.0).then_inc(consts_made, 1)
                pool.memset(lower[:, :, :], 1.0).then_inc(consts_made, 1)
                pool.memset(masks[:, :], 0.0).then_inc(consts_made, 1)
                pool.memset(mask0[:, :], 0.0).then_inc(consts_made, 1)
                pool.wait_ge(consts_made, 5)
                pool.affine_select(out=ident[:, :], in_=ident[:, :], compare_op=ALU.not_equal, fill=1.0,
                                   base=0, pattern=[[-1, P]], channel_multiplier=1).then_inc(consts_made, 1)
                pool.affine_select(out=lower[:, :, :], in_=lower[:, :, :], compare_op=ALU.is_gt, fill=0.0,
                                   base=0, pattern=[[1, NE], [-1, NE]], channel_multiplier=0).then_inc(consts_made, 1)
                pool.affine_select(out=masks[:, 0:WIN], in_=masks[:, 0:WIN], compare_op=ALU.is_ge, fill=NEG,
                                   base=0, pattern=[[1, WIN]], channel_multiplier=-1).then_inc(consts_made, 1)
                pool.affine_select(out=mask0[:, GLOB:P], in_=mask0[:, GLOB:P], compare_op=ALU.is_ge, fill=NEG,
                                   base=HALF + GLOB, pattern=[[1, P - GLOB]], channel_multiplier=-1).then_inc(consts_made, 1)
                pool.wait_ge(consts_made, 9)
                pool.affine_select(out=masks[:, 0:WIN], in_=masks[:, 0:WIN], compare_op=ALU.is_ge, fill=NEG,
                                   base=HALF, pattern=[[-1, WIN]], channel_multiplier=1).then_inc(consts_made, 1)
                pool.affine_select(out=mask0[:, :], in_=mask0[:, :], compare_op=ALU.is_ge, fill=NEG,
                                   base=0, pattern=[[-1, P]], channel_multiplier=1).then_inc(consts_made, 1)
                pool.wait_ge(scan_done, 1)
                pool.tensor_tensor(st_cos, state, cos_t, ALU.mult).then_inc(back_done, 1)
                pool.tensor_tensor(st_sin, state, sin_t, ALU.mult).then_inc(back_done, 1)

            @block.scalar
            def _(act):
                for h in range(2):
                    half = slice(HID * h, HID * (h + 1))
                    act.dma_start(prm[half, 0:1], theta_log.rearrange("(p a) -> p a", a=1)).then_inc(rec_loaded, 16)
                    act.dma_start(prm[half, 1:2], nu_log.rearrange("(p a) -> p a", a=1)).then_inc(rec_loaded, 16)
                    act.dma_start(prm[half, 2:3], gamma_log.rearrange("(p a) -> p a", a=1)).then_inc(rec_loaded, 16)
                    act.dma_start(B_sb[half, h, :], B_re).then_inc(rec_loaded, 16)
                    act.dma_start(B_sb[half, 1 - h, :], B_im).then_inc(rec_loaded, 16)
                act.dma_start(C_sb[:, 0, 0:HID], C_re).then_inc(rec_loaded, 16)
                act.dma_start(C_sb[:, 0, HID:], C_im).then_inc(rec_loaded, 16)
                act.dma_start(C_sb[:, 1, 0:HID], C_im).then_inc(rec_loaded, 16)
                act.dma_start(C_sb[:, 1, HID:], C_re).then_inc(rec_loaded, 16)
                act.dma_start(D_col[:, :], D_skip.rearrange("(p a) -> p a", a=1)).then_inc(rec_loaded, 16)
                act.wait_ge(rec_loaded, 15 * 16)
                act.activation(eprm[:, :], prm[:, :], ACT.Exp).then_inc(prm_done, 1)
                act.wait_ge(prm_done, 1)
                act.activation(r_col[:, :], eprm[:, 1:2], ACT.Exp, scale=-1.0).then_inc(prm_done, 1)
                act.wait_ge(stats_done, 2 * NT + 1)
                act.activation(std[:, :], var_eps[:, :], ACT.Sqrt).then_inc(std_done, 1)
                act.wait_ge(angle_steps, 7)
                act.activation(ang[:, 4:6], ang[:, 2:4], ACT.Sin).then_inc(sin_done, 1)

                def drain(kind, c, dst, **how):
                    n, k = nth[kind, c]
                    act.wait_ge(filled, n + 1)
                    act.activation(dst, how.pop("src", bank(kind, c)), how.pop("func", ACT.Copy), **how)\
                       .then_inc(act_drained, 1)

                for c in range(NC):
                    drain("xT", c, xT[:, CH * c:CH * (c + 1)])
                drain("BT", 0, BT[:, :, :], src=bank("BT", 0)[:, 0:2 * P].rearrange("p (a n) -> p a n", a=2))
                drain("CT", 0, CT[:, :, :], src=bank("CT", 0)[:, 0:2 * P].rearrange("p (a n) -> p a n", a=2))
                act.wait_ge(att_loaded, 4 * 16)
                for n, (kind, parts) in enumerate((("q", partsQ), ("k", partsK))):
                    for c in range(NC):
                        m = NC * n + c
                        if m >= 2:
                            act.wait_ge(parts_done, m - 1)
                        act.wait_ge(filled, nth[kind, c][0] + 1)
                        act.activation(parts[:, 0, CH * c:CH * (c + 1)], bank(kind, c), ACT.Identity,
                                       bias=bqk_col[:, n:n + 1]).then_inc(hi_done, 1)
                        drain(kind, c, qk32[:, m % 2, :], func=ACT.Identity, bias=bqk_col[:, n:n + 1])
                for c in range(NC):
                    drain("v", c, v_sb[:, TPC * c:TPC * (c + 1), :],
                          src=bank("v", c).rearrange("p (t d) -> p t d", d=D))
                act.wait_ge(gexp_in, 1)
                act.activation(gates[:, :, :], logits[:, :, :], ACT.Exp).then_inc(gexp_done, 1)
                for c in range(NC):
                    drain("combT", c, combT[:, CH * c:CH * (c + 1)], src=bank("combT", c)[0:NE, :])
                for c in range(NC):
                    drain("bias", c, gate_sb[:, TPC * c:TPC * (c + 1), :],
                          src=bank("bias", c).rearrange("p (t d) -> p t d", d=D))
                for c in range(NC):
                    drain("y", c, y_sb[:, TPC * c:TPC * (c + 1), :],
                          src=bank("y", c).rearrange("p (t d) -> p t d", d=D))

            @block.tensor
            def _(pe):
                def begin(kind, c):
                    n = nth[kind, c][0]
                    if n >= 8:
                        k, cc, eng = jobs[n - 8]
                        pe.wait_ge(drained[eng], nth[k, cc][1])
                    return bank(kind, c)

                pe.wait_ge(consts_made, 6)
                for c in range(NC):
                    to = begin("xT", c)
                    for t in range(TPC):
                        pe.wait_ge(xn_done, TPC * c + t + 1)
                        mm = pe.transpose(to[:, P * t:P * (t + 1)], xn_sb[:, TPC * c + t, :], ident[:, :])
                    mm.then_inc(filled, 1)
                pe.wait_ge(diag_done, 6)
                to = begin("BT", 0)
                for a in range(2):
                    mm = pe.transpose(to[:, P * a:P * (a + 1)], B_sb[:, a, :], ident[:, :])
                mm.then_inc(filled, 1)
                to = begin("CT", 0)
                for a in range(2):
                    mm = pe.transpose(to[:, P * a:P * (a + 1)], C_sb[:, a, :], ident[:, :])
                mm.then_inc(filled, 1)
                pe.wait_ge(att_loaded, 4 * 16)
                for n, kind in enumerate(("q", "k")):
                    for c in range(NC):
                        pe.wait_ge(act_drained, nth["xT", c][1])
                        pe.matmul(begin(kind, c), w0_sb[:, n, :], xT[:, CH * c:CH * (c + 1)],
                                  start=True, stop=True).then_inc(filled, 1)
                pe.wait_ge(moe_loaded, 4 * 16)
                to = begin("logits", 0)
                for t in range(NT):
                    pe.matmul(to[:, NE * t:NE * (t + 1)], xT[:, P * t:P * (t + 1)], wg_sb[:, :],
                              start=True, stop=False)
                    mm = pe.matmul(to[:, NE * t:NE * (t + 1)], ones_row[:, :], bg_row[:, :],
                                   start=False, stop=True)
                mm.then_inc(filled, 1)
                for c in range(NC):
                    to = begin("v", c)
                    for t in range(TPC):
                        cols = slice(P * t, P * (t + 1))
                        pe.matmul(to[:, cols], xT[:, CH * c + P * t:CH * c + P * (t + 1)], w0_sb[:, 2, :],
                                  start=True, stop=False)
                        mm = pe.matmul(to[:, cols], ones_row[:, :], bv_row[:, :], start=False, stop=True)
                    mm.then_inc(filled, 1)
                pe.wait_ge(act_drained, nth["BT", 0][1])
                for c in range(NC):
                    for a, kind in enumerate(("u", "w")):
                        pe.matmul(begin(kind, c), BT[:, a, :], xT[:, CH * c:CH * (c + 1)],
                                  start=True, stop=True).then_inc(filled, 1)
                pe.wait_ge(comb_done, 1)
                for c in range(NC):
                    to = begin("combT", c)
                    for t in range(TPC):
                        mm = pe.transpose(to[0:NE, P * t:P * (t + 1)], gates[:, TPC * c + t, :], ident[:, :])
                    mm.then_inc(filled, 1)
                for c in range(NC):
                    pe.wait_ge(act_drained, nth["combT", c][1])
                    to = begin("bias", c)
                    for t in range(TPC):
                        mm = pe.matmul(to[:, P * t:P * (t + 1)], combT[:, CH * c + P * t:CH * c + P * (t + 1)],
                                       be_sb[:, :], start=True, stop=True)
                    mm.then_inc(filled, 1)
                for n in range(2 * NT):
                    pe.matmul(begin("experts", n), xT[:, P * (n // 2):P * (n // 2 + 1)],
                              we_sb[:, NE // 2 * (n % 2):NE // 2 * (n % 2 + 1), :].rearrange("p e f -> p (e f)"),
                              start=True, stop=True).then_inc(filled, 1)
                pe.wait_ge(act_drained, nth["CT", 0][1])
                pe.wait_ge(back_done, 2)
                for c in range(NC):
                    to = begin("y", c)
                    for t in range(TPC):
                        tok = slice(CH * c + P * t, CH * c + P * (t + 1))
                        cols = slice(P * t, P * (t + 1))
                        pe.matmul(to[:, cols], st_cos[:, tok], CT[:, 0, :], start=True, stop=False)
                        pe.matmul(to[:, cols], st_sin[:, tok], CT[:, 1, :], start=False, stop=False)
                        mm = pe.matmul(to[:, cols], xT[:, tok], D_diag[:, :], start=False, stop=True)
                    mm.then_inc(filled, 1)

            @block.vector
            def _(dve):
                dve.wait_ge(x_loaded, 16)
                for t in range(NT):
                    dve.bn_stats(stats[:, t, :], x_sb[:, t, :]).then_inc(stats_done, 1)
                dve.wait_ge(stats_done, NT)
                for t in range(NT):
                    dve.bn_aggr(mv[:, t, :], stats[:, t, :]).then_inc(stats_done, 1)
                dve.wait_ge(stats_done, 2 * NT)
                dve.tensor_scalar(var_eps[:, :], mv[:, :, 1], EPS, None, ALU.add).then_inc(stats_done, 1)
                dve.wait_ge(prm_done, 2)
                th = eprm[:, 0:1]
                dve.tensor_scalar(ang_i[:, :], th, 1.0 / (TWO_PI_HI + TWO_PI_LO), None, ALU.mult)\
                   .then_inc(angle_steps, 1)
                dve.wait_ge(angle_steps, 1)
                dve.tensor_copy(ang[:, 0:1], ang_i[:, :]).then_inc(angle_steps, 1)
                dve.wait_ge(angle_steps, 2)
                dve.scalar_tensor_tensor(out=ang[:, 1:2], in0=ang[:, 0:1], scalar=-TWO_PI_HI, in1=th,
                                         op0=ALU.mult, op1=ALU.add).then_inc(angle_steps, 1)
                dve.wait_ge(angle_steps, 3)
                dve.scalar_tensor_tensor(out=ang[:, 6:7], in0=ang[:, 0:1], scalar=-TWO_PI_LO, in1=ang[:, 1:2],
                                         op0=ALU.mult, op1=ALU.add).then_inc(angle_steps, 1)
                dve.wait_ge(angle_steps, 4)
                dve.tensor_scalar(ang[:, 2:3], ang[:, 6:7], 0.5, None, ALU.mult).then_inc(angle_steps, 1)
                dve.wait_ge(angle_steps, 5)
                dve.scalar_tensor_tensor(out=ang[:, 7:8], in0=ang[:, 2:3], scalar=-1.0, in1=ang[:, 2:3],
                                         op0=ALU.mult, op1=ALU.max).then_inc(angle_steps, 1)
                dve.wait_ge(angle_steps, 6)
                dve.tensor_scalar(ang[:, 3:4], ang[:, 7:8], -1.0, PI_2, ALU.mult, ALU.add).then_inc(angle_steps, 1)
                dve.wait_ge(std_done, 1)
                dve.reciprocal(rstd[:, :], std[:, :]).then_inc(stats_done, 1)
                dve.wait_ge(stats_done, 2 * NT + 2)
                for t in range(NT):
                    dve.tensor_scalar(xn_sb[:, t, :], x_sb[:, t, :], mv[:, t, 0:1], rstd[:, t:t + 1],
                                      ALU.subtract, ALU.mult).then_inc(xn_done, 1)
                gam = eprm[:, 2:3]
                lo, hi = slice(0, HID), slice(HID, 2 * HID)
                dve.tensor_scalar(B_sb[:, 0, :], B_sb[:, 0, :], gam, None, ALU.mult).then_inc(diag_done, 1)
                dve.tensor_scalar(B_sb[lo, 1, :], B_sb[lo, 1, :], gam[lo], None, ALU.mult).then_inc(diag_done, 1)
                dve.tensor_scalar(B_sb[hi, 1, :], B_sb[hi, 1, :], gam[hi], -1.0, ALU.mult, ALU.mult)\
                   .then_inc(diag_done, 1)
                dve.tensor_scalar(C_sb[:, 0, HID:], C_sb[:, 0, HID:], -1.0, None, ALU.mult).then_inc(diag_done, 1)
                dve.tensor_scalar(C_sb[:, 1, :], C_sb[:, 1, :], -1.0, None, ALU.mult).then_inc(diag_done, 1)
                dve.wait_ge(consts_made, 11)
                dve.tensor_scalar(D_diag[:, :], ident[:, :], D_col[:, 0:1], None, ALU.mult).then_inc(diag_done, 1)
                steps = 0
                for m in range(2 * NC):
                    parts, c = (partsQ, partsK)[m // NC], m % NC
                    cols = slice(CH * c, CH * (c + 1))
                    kind = ("q", "k")[m // NC]
                    dve.wait_ge(act_drained, nth[kind, c][1])
                    dve.wait_ge(hi_done, m + 1)
                    dve.tensor_tensor(rest[:, m % 2, :], qk32[:, m % 2, :], parts[:, 0, cols], ALU.subtract)\
                       .then_inc(parts_steps, 1)
                    dve.wait_ge(parts_steps, 2 * m + 1)
                    dve.tensor_copy(parts[:, 1, cols], rest[:, m % 2, :]).then_inc(parts_steps, 1)
                    dve.wait_ge(parts_steps, 2 * m + 2)
                    dve.tensor_tensor(parts[:, 2, cols], rest[:, m % 2, :], parts[:, 1, cols], ALU.subtract)\
                       .then_inc(parts_done, 1)
                gs = 0
                def gstep(ins):
                    nonlocal gs
                    gs += 1
                    ins.then_inc(gate_steps, 1)
                    dve.wait_ge(gate_steps, gs)
                dve.wait_ge(filled, nth["logits", 0][0] + 1)
                src = bank("logits", 0)[:, 0:NT * NE].rearrange("p (t e) -> p t e", e=NE)
                gstep(dve.tensor_reduce(gmax[:, :], src, AX.X, ALU.max))
                dve.tensor_tensor(logits[:, :, :], src, gmax[:, :].unsqueeze(2).broadcast_to([P, NT, NE]),
                                  ALU.subtract).then_inc(dve_drained, 1)
                dve.wait_ge(dve_drained, nth["logits", 0][1])
                dve.sem_inc(gexp_in, 1)
                ts = 0
                def tstep(ins):
                    nonlocal ts
                    ts += 1
                    ins.then_inc(table_steps, 1)
                    return ts
                dve.wait_ge(sin_done, 1)
                sh, chh = ang[:, 4:5], ang[:, 5:6]

                def double(level, s, c):
                    n = tstep(dve.tensor_tensor(pw[:, level, 2:3], s, s, ALU.mult))
                    dve.wait_ge(table_steps, n)
                    tstep(dve.tensor_scalar(pw[:, level, 0:1], pw[:, level, 2:3], -2.0, 1.0, ALU.mult, ALU.add))
                    n = tstep(dve.scalar_tensor_tensor(out=pw[:, level, 1:2], in0=s, scalar=2.0, in1=c,
                                                       op0=ALU.mult, op1=ALU.mult))
                    dve.wait_ge(table_steps, n)

                double(0, sh, chh)
                tstep(dve.memset(cos_t[:, 0:1], 1.0))
                n = tstep(dve.memset(sin_t[:, 0:1], 0.0))
                dve.wait_ge(table_steps, n)
                size, level = 1, 0
                while size < S:
                    c1, s1 = pw[:, level, 0:1], pw[:, level, 1:2]
                    a, b = slice(0, size), slice(size, 2 * size)
                    n = tstep(dve.tensor_scalar(rot_tmp[:, a], sin_t[:, a], s1, None, ALU.mult))
                    dve.wait_ge(table_steps, n)
                    n = tstep(dve.scalar_tensor_tensor(out=cos_t[:, b], in0=cos_t[:, a], scalar=c1,
                                                       in1=rot_tmp[:, a], op0=ALU.mult, op1=ALU.subtract))
                    dve.wait_ge(table_steps, n)
                    n = tstep(dve.tensor_scalar(rot_tmp[:, a], cos_t[:, a], s1, None, ALU.mult))
                    dve.wait_ge(table_steps, n)
                    n = tstep(dve.scalar_tensor_tensor(out=sin_t[:, b], in0=sin_t[:, a], scalar=c1,
                                                       in1=rot_tmp[:, a], op0=ALU.mult, op1=ALU.add))
                    dve.wait_ge(table_steps, n)
                    if 2 * size < S:
                        double(level + 1, s1, c1)
                    size, level = 2 * size, level + 1
                for c in range(NC):
                    cols = slice(CH * c, CH * (c + 1))
                    dve.wait_ge(filled, nth["w", c][0] + 1)
                    dve.tensor_tensor(rot_x[:, cols], bank("u", c), cos_t[:, cols], ALU.mult).then_inc(dve_drained, 1)
                    dve.tensor_tensor(rot_tmp[:, 0:CH], bank("w", c), sin_t[:, cols], ALU.mult).then_inc(dve_drained, 1)
                    dve.wait_ge(dve_drained, nth["w", c][1])
                    dve.tensor_tensor(rot_x[:, cols], rot_x[:, cols], rot_tmp[:, 0:CH], ALU.add).then_inc(rot_done, 1)
                    dve.wait_ge(rot_done, c + 1)
                dve.tensor_tensor_scan(state, r_col[:, 0:1].broadcast_to([P, S]), rot_x, 0.0, ALU.mult, ALU.add)\
                   .then_inc(scan_done, 1)
                dve.wait_ge(gexp_done, 1)
                gstep(dve.tensor_reduce(gsum[:, :], gates[:, :, :], AX.X, ALU.add))
                gstep(dve.reciprocal(gmax[:, :], gsum[:, :]))
                gstep(dve.tensor_tensor(gates[:, :, :], gates[:, :, :], gmax[:, :].unsqueeze(2).broadcast_to([P, NT, NE]),
                                        ALU.mult))
                mine = gates[:, :, :].unsqueeze(3).broadcast_to([P, NT, NE, NE])
                other = gates[:, :, :].unsqueeze(2).broadcast_to([P, NT, NE, NE])
                gstep(dve.tensor_tensor(beats[:, :, :, :], other, mine, ALU.is_gt))
                gstep(dve.tensor_tensor(ties[:, :, :, :], other, mine, ALU.is_equal))
                gstep(dve.tensor_tensor(ties[:, :, :, :].rearrange("p t e j -> p t (e j)"),
                                        ties[:, :, :, :].rearrange("p t e j -> p t (e j)"),
                                        lower[:, :, :].rearrange("p e j -> p (e j)").unsqueeze(1).broadcast_to([P, NT, NE * NE]),
                                        ALU.mult))
                gstep(dve.tensor_tensor(beats[:, :, :, :], beats[:, :, :, :], ties[:, :, :, :], ALU.add))
                gstep(dve.tensor_reduce(logits[:, :, :], beats[:, :, :, :], AX.X, ALU.add))
                dve.scalar_tensor_tensor(out=gates[:, :, :], in0=logits[:, :, :], scalar=2.0, in1=gates[:, :, :],
                                         op0=ALU.is_lt, op1=ALU.mult).then_inc(comb_done, 1)
                dve.wait_ge(comb_done, 1)
                ms = 0
                for n in range(2 * NT):
                    t = n // 2
                    dve.wait_ge(act_drained, nth["bias", t // TPC][1])
                    dve.wait_ge(filled, nth["experts", n][0] + 1)
                    for k in range(NE // 2):
                        e = NE // 2 * (n % 2) + k
                        if ms:
                            dve.wait_ge(moe_steps, ms)
                        ins = dve.scalar_tensor_tensor(
                            out=gate_sb[:, t, :], in0=bank("experts", n)[:, P * k:P * (k + 1)],
                            scalar=gates[:, t, e:e + 1], in1=gate_sb[:, t, :], op0=ALU.mult, op1=ALU.add)
                        if k == NE // 2 - 1:
                            ins.then_inc(dve_drained, 1)
                            dve.wait_ge(dve_drained, nth["experts", n][1])
                        else:
                            ins.then_inc(moe_steps, 1)
                            ms += 1

        NMAX = 2 * 2 * TPC * NC
        NEXP = 2 * NT
        MAX_STEPS = NT - 2
        scores_ready = sem("scores_ready")
        probs_ready = sem("probs_ready")
        probs_used = sem("probs_used")
        max_ready = sem("max_ready")
        max_reduced = sem("max_reduced")
        mops_loaded = [sem("mops_loaded0"), sem("mops_loaded1")]
        eops_loaded = [sem("eops_loaded0"), sem("eops_loaded1")]
        ones_set = sem("ones_set")
        v_staged = sem("v_staged")
        max_joined = sem("max_joined")
        max_turned = sem("max_turned")
        max_hi = sem("max_hi")
        max_split = sem("max_split")
        out_drained = sem("out_drained")
        out_turned = sem("out_turned")
        out_rden = sem("out_rden")
        out_normed = sem("out_normed")

        exp_ps = [ps[:, 2 * t:2 * t + 2, :] for t in range(2)]
        max_ps = [ps[:, 4 + n, :] for n in range(2)]
        av_ps = ps[:, 6, :]
        turn_ps = ps[:, 7, :]
        MCOLS = 2 * 2 * TPC

        def max_range(s):
            return range(NMAX * s // MAX_STEPS, NMAX * (s + 1) // MAX_STEPS) if s < MAX_STEPS else range(0)

        def max_tile(m):
            return m % 2, m // 2 % 2, m // (4 * NC), m // 4 % NC

        def for_blocks(eng, body):
            body(0, 0, 0)
            with eng.Fori(0, (NB - 2) // 2) as i:
                body(2 * i + 1, 1, i)
                body(2 * i + 2, 0, i + 1)
            body(NB - 1, 1, NB // 2 - 1)

        def static(b):
            return isinstance(b, int)

        with nc.Block() as block:
            @block.sync
            def _(sp):
                q_src = q_parts.rearrange("r (a x d) (c n) -> a x r d c n", x=G0, d=HD0, n=CH)
                k_src = k_parts.rearrange("r (a x d) n -> a x r d n", x=G0, d=HD0)

                def load(q_to, k_to, b, loaded):
                    b = b % NB if static(b) else b
                    for g in range(2):
                        rows = slice(64 * g, 64 * g + KR)
                        for t in range(2):
                            sp.dma_start(q_to[rows, t, :], q_src[ds(b % NG0, 1), 2 * t + g, :, :, ds(b // NG0 % NC, 1), :])\
                              .then_inc(loaded, 16)
                            sp.dma_start(k_to[rows, t, :], k_src[ds(b % NG0, 1), 2 * t + g, :, :, :]).then_inc(loaded, 16)

                def load_max_rows(par):
                    for g in range(2):
                        for a in range(2):
                            row = 64 * g + KR + a
                            sp.dma_start(qexp[par][row:row + 1, :, :].rearrange("p t (s q) -> p (t s) q", q=P),
                                         max_rows[2 * TPC * g:2 * TPC * (g + 1), a, :])\
                              .then_inc(eops_loaded[par], 16)

                def body(b, par, k):
                    if not static(b) or b < NB - 1:
                        sp.wait_ge(max_ready, NMAX * (b + 1))
                        load(qmax[par], kmax[par], b + 2, mops_loaded[par])
                        if not static(b) or b > 0:
                            sp.wait_ge(scores_ready, NEXP * b)
                        load(qexp[1 - par], kexp[1 - par], b + 1, eops_loaded[1 - par])
                        sp.wait_ge(max_split, b + 2)
                        load_max_rows(1 - par)

                load(qmax[0], kmax[0], 0, mops_loaded[0])
                load(qmax[1], kmax[1], 1, mops_loaded[1])
                sp.wait_ge(ones_set, 2)
                load(qexp[0], kexp[0], 0, eops_loaded[0])
                sp.wait_ge(max_split, 1)
                load_max_rows(0)
                for_blocks(sp, body)
                sp.wait_ge(mops_loaded[0], 128 * (NB // 2 + 1))
                sp.wait_ge(mops_loaded[1], 128 * (NB // 2))

            @block.gpsimd
            def _(pool):
                for n in range(2):
                    pool.memset(kexp[n], 1.0).then_inc(ones_set, 1)
                for n in range(2):
                    pool.memset(vst[n], 0.0).then_inc(ones_set, 1)
                pool.wait_ge(ones_set, 4)
                for n in range(2):
                    pool.memset(vst[n][:, :, :, HD0:HD0 + 1], 1.0).then_inc(ones_set, 1)

                def stage(b, par):
                    pool.tensor_copy(vst[par][:, :, :, 0:HD0],
                                     v_sb[:, :, ds(G0 * HD0 * (b % NG0), G0 * HD0)].rearrange("p t (j d) -> p t j d", d=HD0))\
                        .then_inc(v_staged, 1)

                def body(b, par, k):
                    if not static(b) or b < NB - 1:
                        if not static(b) or b > 0:
                            pool.wait_ge(probs_used, NT * b)
                        stage(b + 1, 1 - par)

                stage(0, 0)
                for_blocks(pool, body)

            @block.tensor
            def _(pe):
                def max_scores(b, par, ms):
                    for m in ms:
                        g, t, qs, kc = max_tile(m)
                        if not static(b) or b > 0 or m >= 2:
                            pe.wait_ge(max_reduced, NMAX * b + m - 1)
                        rows = slice(64 * g, 64 * g + KR)
                        pe.matmul(max_ps[m % 2], qmax[par][rows, t, P * qs:P * (qs + 1)],
                                  kmax[par][rows, t, CH * kc:CH * (kc + 1)], start=True, stop=True)\
                          .then_inc(max_ready, 1)

                def turn_max(b):
                    pe.wait_ge(max_joined, b + 1)
                    if not static(b) or b > 1:
                        pe.wait_ge(out_normed, b - 1)
                    pe.transpose(turn_ps[0:MCOLS, 0:P], neg_max[:, :], ident[:, :]).then_inc(max_turned, 1)

                def scores_T(b, par, s):
                    rows = [slice(64 * g, 64 * g + KR + 2) for g in range(2)]
                    for t in range(2):
                        if not static(b) or b > 0 or s > 0:
                            pe.wait_ge(probs_ready, NEXP * b + 2 * s + t - 1)
                        for g in range(2):
                            mm = pe.matmul(exp_ps[t][:, g, :], kexp[par][rows[g], t, P * s:P * (s + 1)],
                                           qexp[par][rows[g], t, :], start=True, stop=True)
                        mm.then_inc(scores_ready, 1)

                def values(b, par, s):
                    pe.wait_ge(probs_ready, NEXP * b + 2 * s + 2)
                    if s == 0:
                        pe.wait_ge(v_staged, b + 1)
                        if not static(b) or b > 0:
                            pe.wait_ge(out_drained, b)
                    for j in range(G0):
                        t, g = j // 2, j % 2
                        mm = pe.matmul(av_ps[32 * j:32 * (j + 1), :], vst[par][:, s, j, :],
                                       probs[2 * (s % 2) + t][:, g, :], start=(s == 0), stop=(s == NT - 1))
                    mm.then_inc(probs_used, 1)

                def turn_out(b, par):
                    pe.wait_ge(out_drained, b + 1)
                    if not static(b) or b < NB - 1:
                        pe.wait_ge(max_split, b + 2)
                    else:
                        pe.wait_ge(out_normed, b)
                    for qs in range(TPC):
                        mm = pe.transpose(turn_ps[:, P * qs:P * (qs + 1)], outT0[par][:, P * qs:P * (qs + 1)],
                                          ident[:, :])
                    mm.then_inc(out_turned, 1)

                def body(b, par, k):
                    more = not static(b) or b < NB - 1
                    later = not static(b) or b > 0
                    pe.wait_ge(eops_loaded[par], 12 * 16 * (k + 1))
                    for s in range(NT):
                        scores_T(b, par, s)
                        if more:
                            if s == 0:
                                pe.wait_ge(mops_loaded[1 - par], 8 * 16 * ((k if par == 0 else k + 1) + 1))
                            max_scores(b + 1, 1 - par, max_range(s))
                        if s > 0:
                            values(b, par, s - 1)
                        elif later:
                            values(b - 1, 1 - par, NT - 1)
                        if s == 2 and later:
                            turn_out(b - 1, 1 - par)
                        if s == MAX_STEPS and more:
                            turn_max(b + 1)

                pe.wait_ge(mops_loaded[0], 8 * 16)
                max_scores(0, 0, range(NMAX))
                turn_max(0)
                for_blocks(pe, body)
                values(NB - 1, 1, NT - 1)
                turn_out(NB - 1, 1)

            @block.scalar
            def _(act):
                def drain_out(b, par):
                    act.wait_ge(probs_used, NT * (b + 1))
                    act.activation(outT0[par], av_ps, ACT.Copy).then_inc(out_drained, 1)

                def body(b, par, k):
                    later = not static(b) or b > 0
                    for s in range(NT):
                        for t in range(2):
                            act.wait_ge(scores_ready, NEXP * b + 2 * s + t + 1)
                            if later or s >= 2:
                                act.wait_ge(probs_used, NT * b + s - 1)
                            act.activation(probs[2 * (s % 2) + t], exp_ps[t], ACT.Exp, scale=SC0)\
                               .then_inc(probs_ready, 1)
                        if s == 0 and later:
                            drain_out(b - 1, 1 - par)

                for_blocks(act, body)
                drain_out(NB - 1, 1)

            @block.vector
            def _(dve):
                def reduce_tiles(b, ms):
                    for m in ms:
                        g, t, qs, kc = max_tile(m)
                        dve.wait_ge(max_ready, NMAX * b + m + 1)
                        col = (2 * g + t) * TPC + qs
                        dve.tensor_reduce(tile_max[:, col, kc:kc + 1], max_ps[m % 2], AX.X, ALU.max)\
                           .then_inc(max_reduced, 1)

                def join_max(b):
                    dve.wait_ge(max_reduced, NMAX * (b + 1))
                    dve.tensor_reduce(neg_max[:, :], tile_max[:, :, :], AX.X, ALU.max, negate=True)\
                       .then_inc(max_joined, 1)

                def split_max(b):
                    dve.wait_ge(max_turned, b + 1)
                    dve.tensor_copy(max_rows[:, 0, :], turn_ps[0:MCOLS, 0:P]).then_inc(max_hi, 1)
                    dve.wait_ge(max_hi, b + 1)
                    dve.tensor_tensor(max_rows[:, 1, :], turn_ps[0:MCOLS, 0:P], max_rows[:, 0, :], ALU.subtract)\
                       .then_inc(max_split, 1)

                def norm_out(b):
                    dve.wait_ge(out_turned, b + 1)
                    sums = turn_ps.rearrange("p (a j d) -> p (a j) d", j=G0, d=32)
                    dve.reciprocal(rden0[:, :], sums[:, :, HD0]).then_inc(out_rden, 1)
                    dve.wait_ge(out_rden, b + 1)
                    dve.tensor_tensor(
                        attn_sb[:, ds(b // NG0 * TPC, TPC), ds(b % NG0 * (G0 * HD0), G0 * HD0)]
                        .rearrange("p a (j d) -> p a j d", d=HD0),
                        turn_ps.rearrange("p (a j d) -> p a j d", j=G0, d=32)[:, :, :, 0:HD0],
                        rden0[:, :].rearrange("p (a j) -> p a j", j=G0).unsqueeze(3).broadcast_to([P, TPC, G0, HD0]),
                        ALU.mult).then_inc(out_normed, 1)

                def body(b, par, k):
                    more = not static(b) or b < NB - 1
                    later = not static(b) or b > 0
                    for s in range(NT):
                        if more:
                            reduce_tiles(b + 1, max_range(s))
                        if s == 3 and later:
                            norm_out(b - 1)
                    if more:
                        join_max(b + 1)
                        split_max(b + 1)

                reduce_tiles(0, range(NMAX))
                join_max(0)
                split_max(0)
                for_blocks(dve, body)
                norm_out(NB - 1)

        z_sum = sem("z_sum")
        z_exp = sem("z_exp")
        gate0_steps = sem("gate0_steps")
        x1_done = sem("x1_done")
        stats1_done = sem("stats1_done")
        std1_done = sem("std1_done")
        xn1_done = sem("xn1_done")
        turned1 = sem("turned1")
        xT1_done = sem("xT1_done")
        tails_made = sem("tails_made")
        hid_ready = sem("hid_ready")
        hid_done = sem("hid_done")
        mlp_ready = sem("mlp_ready")
        mlp_exp = sem("mlp_exp")
        mlp_done = sem("mlp_done")
        mlp_steps = sem("mlp_steps")
        xn1 = cut(8 * S, S).rearrange("p (t d) -> p t d", d=D)
        ez = cut(9 * S, S)
        gz = cut(10 * S, S)

        def flat(a):
            return a[:, :, :].rearrange("p t d -> p (t d)")

        with nc.Block() as block:
            @block.vector
            def _(dve):
                def chunk(a, c):
                    return a[:, CH * c:CH * (c + 1)]
                z, y, g, xf = flat(attn_sb), flat(y_sb), flat(gate_sb), flat(x_sb)
                for c in range(NC):
                    dve.tensor_tensor(chunk(z, c), chunk(z, c), chunk(g, c), ALU.add).then_inc(z_sum, 1)
                n = 0
                for c in range(NC):
                    dve.wait_ge(z_exp, c + 1)
                    for m, ins in enumerate((
                        lambda: dve.tensor_scalar(chunk(ez, c), chunk(ez, c), 1.0, None, ALU.add),
                        lambda: dve.reciprocal(chunk(ez, c), chunk(ez, c)),
                        lambda: dve.tensor_tensor(chunk(gz, c), chunk(z, c), chunk(y, c), ALU.mult),
                        lambda: dve.tensor_tensor(chunk(gz, c), chunk(gz, c), chunk(ez, c), ALU.mult),
                    )):
                        ins().then_inc(gate0_steps, 1)
                        n += 1
                        dve.wait_ge(gate0_steps, n)
                    dve.tensor_tensor(chunk(xf, c), chunk(xf, c), chunk(gz, c), ALU.add).then_inc(x1_done, 1)
                    dve.wait_ge(x1_done, c + 1)
                    for t in range(TPC * c, TPC * (c + 1)):
                        dve.bn_stats(stats[:, t, :], x_sb[:, t, :]).then_inc(stats1_done, 1)
                dve.wait_ge(stats1_done, NT)
                for t in range(NT):
                    dve.bn_aggr(mv[:, t, :], stats[:, t, :]).then_inc(stats1_done, 1)
                dve.wait_ge(stats1_done, 2 * NT)
                dve.tensor_scalar(var_eps[:, :], mv[:, :, 1], EPS, None, ALU.add).then_inc(stats1_done, 1)
                dve.wait_ge(std1_done, 1)
                dve.reciprocal(rstd[:, :], std[:, :]).then_inc(stats1_done, 1)
                dve.wait_ge(stats1_done, 2 * NT + 2)
                for t in range(NT):
                    dve.tensor_scalar(xn1[:, t, :], x_sb[:, t, :], mv[:, t, 0:1], rstd[:, t:t + 1],
                                      ALU.subtract, ALU.mult).then_inc(xn1_done, 1)
                n = 0
                for c in range(NC):
                    dve.wait_ge(mlp_exp, c + 1)
                    dve.tensor_scalar(chunk(ez, c), chunk(ez, c), 1.0, None, ALU.add).then_inc(mlp_steps, 1)
                    dve.wait_ge(mlp_steps, 2 * c + 1)
                    dve.reciprocal(chunk(ez, c), chunk(ez, c)).then_inc(mlp_steps, 1)
                    dve.wait_ge(mlp_steps, 2 * c + 2)
                    dve.tensor_tensor(chunk(g, c), ps[:, c, :], chunk(ez, c), ALU.mult).then_inc(mlp_done, 1)

            @block.scalar
            def _(act):
                z = flat(attn_sb)
                for c in range(NC):
                    act.wait_ge(z_sum, c + 1)
                    act.activation(ez[:, CH * c:CH * (c + 1)], z[:, CH * c:CH * (c + 1)], ACT.Exp, scale=-1.0)\
                       .then_inc(z_exp, 1)
                act.wait_ge(stats1_done, 2 * NT + 1)
                act.activation(std[:, :], var_eps[:, :], ACT.Sqrt).then_inc(std1_done, 1)
                for c in range(NC):
                    act.wait_ge(turned1, c + 1)
                    act.activation(xT[:, CH * c:CH * (c + 1)], ps[:, c, :], ACT.Copy).then_inc(xT1_done, 1)
                for n in range(NI * NC):
                    i, c = n % NI, n // NI
                    act.wait_ge(hid_ready, n + 1)
                    act.activation(hT[:, i, CH * c:CH * (c + 1)], ps[:, 4 + n % 4, :], ACT.Relu,
                                   bias=b1_sb[:, i:i + 1]).then_inc(hid_done, 1)
                for c in range(NC):
                    act.wait_ge(mlp_ready, c + 1)
                    act.activation(ez[:, CH * c:CH * (c + 1)], ps[:, c, :], ACT.Exp, scale=-1.0).then_inc(mlp_exp, 1)

            @block.gpsimd
            def _(pool):
                for t in range(1, NT):
                    pool.wait_ge(xT1_done, t // TPC + 1)
                    pool.tensor_copy(xtail[:, t, 0:HALF], xT[:, P * (t + 1) - HALF:P * (t + 1)]).then_inc(tails_made, 1)
                    pool.tensor_copy(xtail[:, t, HALF:TAIL], xT[:, 0:GLOB]).then_inc(tails_made, 1)

            @block.tensor
            def _(pe):
                for c in range(NC):
                    for t in range(TPC):
                        pe.wait_ge(xn1_done, TPC * c + t + 1)
                        mm = pe.transpose(ps[:, c, P * t:P * (t + 1)], xn1[:, TPC * c + t, :], ident[:, :])
                    mm.then_inc(turned1, 1)
                for n in range(NI * NC):
                    i, c = n % NI, n // NI
                    pe.wait_ge(xT1_done, c + 1)
                    if n >= 4:
                        pe.wait_ge(hid_done, n - 3)
                    pe.matmul(ps[:, 4 + n % 4, :], W1_sb[:, i:NI * P:NI], xT[:, CH * c:CH * (c + 1)],
                              start=True, stop=True).then_inc(hid_ready, 1)
                for c in range(NC):
                    pe.wait_ge(hid_done, NI * (c + 1))
                    for t in range(TPC):
                        cols = slice(P * t, P * (t + 1))
                        for i in range(NI):
                            pe.matmul(ps[:, c, cols], hT[:, i, CH * c + P * t:CH * c + P * (t + 1)], W2_sb[:, i, :],
                                      start=(i == 0), stop=False)
                        mm = pe.matmul(ps[:, c, cols], ones_row[:, :], b2_sb[:, :], start=False, stop=True)
                    mm.then_inc(mlp_ready, 1)

        w_staged = sem("w_staged")
        qk_filled = sem("qk_filled")
        q_drained = sem("q_drained")
        k_drained = sem("k_drained")
        v_filled = sem("v_filled")
        v1_drained = sem("v1_drained")
        v2_drained = sem("v2_drained")
        s_filled = sem("s_filled")
        s_masked = sem("s_masked")
        mask_turns = sem("mask_turns")
        exped = sem("exped")
        recips = sem("recips")
        normed = sem("normed")
        pT_filled = sem("pT_filled")
        pT_drained = sem("pT_drained")
        av_done = sem("av_done")
        av_drained = sem("av_drained")
        T_LAG, AV_LAG, OUT_LAG = 3, 4, 5

        def width(qb):
            return KW if qb else P

        with nc.Block() as block:
            @block.gpsimd
            def _(pool):
                pool.tensor_copy(wst[:, :, :], w1qkv_sb[:, :, 0:P]).then_inc(w_staged, 1)
                with pool.Fori(0, NP1) as hp:
                    pool.wait_ge(v_filled, 2 * NC * (hp + 1))
                    pool.tensor_copy(wst[:, :, :], w1qkv_sb[:, :, ds(P * ((hp + 1) % NP1), P)]).then_inc(w_staged, 1)
                    for qb in range(NT):
                        pool.wait_ge(recips, NT * hp + qb + 1)
                        p = p1[:, qb % NSLOT, :, 0:width(qb)]
                        pool.tensor_tensor(p, p, rinv1[:, qb % NSLOT, :].unsqueeze(2).broadcast_to([P, 2, width(qb)]),
                                           ALU.mult).then_inc(normed, 1)

            @block.tensor
            def _(pe):
                with pe.Fori(0, NP1) as hp:
                    pe.wait_ge(w_staged, hp + 1)
                    for n in range(2 * NC):
                        c, which = n // 2, n % 2
                        if n >= 4:
                            pe.wait_ge(k_drained if which else q_drained, NC * hp + c - 1)
                        pe.matmul(ps[:, n % 4, :], wst[:, which, :], xT[:, CH * c:CH * (c + 1)],
                                  start=True, stop=True).then_inc(qk_filled, 1)
                    pe.wait_ge(av_drained, NC * hp + 1)
                    for n in range(2 * NC):
                        c, tail = n // 2, n % 2
                        if n >= 4:
                            pe.wait_ge(v2_drained if tail else v1_drained, NC * hp + c - 1)
                        for t in range(TPC * c, TPC * (c + 1)):
                            cols = slice(P * (t % TPC), P * (t % TPC + 1))
                            if not tail:
                                first = P * t - HALF if t else 0
                                mm = pe.matmul(ps[:, 4 + n % 4, cols], xT[:, first:first + P], wst[:, 2, :],
                                               start=True, stop=True)
                            elif t:
                                mm = pe.matmul(ps[0:TAIL, 4 + n % 4, cols], xtail[:, t, :], wst[:, 2, :],
                                               start=True, stop=True)
                        mm.then_inc(v_filled, 1)
                    pe.wait_ge(q_drained, NC * (hp + 1))
                    pe.wait_ge(k_drained, NC * (hp + 1))
                    for step in range(NT + AV_LAG):
                        qb = step
                        if qb < NT:
                            if qb >= 2:
                                pe.wait_ge(s_masked, 2 * NT * hp + 2 * (qb - 1))
                            q = [qT[64 * g:64 * (g + 1), P * qb:P * (qb + 1)] for g in range(2)]
                            k = [kT[64 * g:64 * (g + 1), :] for g in range(2)]
                            to = [ps[:, 2 * (qb % 2) + g, :] for g in range(2)]
                            first, wide = (P * qb - HALF, WIN) if qb else (0, P)
                            for g in range(2):
                                mm = pe.matmul(to[g][:, 0:wide], q[g], k[g][:, first:first + wide], start=True, stop=True)
                            if qb:
                                for g in range(2):
                                    mm = pe.matmul(to[g][:, WIN:KW], q[g], k[g][:, 0:GLOB], start=True, stop=True)
                            mm.then_inc(s_filled, 1)
                        qb = step - T_LAG
                        if 0 <= qb < NT:
                            pe.wait_ge(normed, NT * hp + qb + 1)
                            if qb >= 2:
                                pe.wait_ge(pT_drained, NT * hp + qb - 1)
                            elif qb == 0:
                                pe.wait_ge(v1_drained, NC * (hp + 1))
                                pe.wait_ge(v2_drained, NC * (hp + 1))
                            to = ps[:, 4 + qb % 2, :]
                            for g in range(2):
                                mm = pe.transpose(to[:, P * g:P * (g + 1)], p1[:, qb % NSLOT, g, 0:P], ident[:, :])
                            if qb:
                                for g in range(2):
                                    mm = pe.transpose(to[0:TAIL, P * (2 + g):P * (3 + g)],
                                                      p1[:, qb % NSLOT, g, P:KW], ident[:, :])
                            mm.then_inc(pT_filled, 1)
                        qb = step - AV_LAG
                        if 0 <= qb < NT:
                            pe.wait_ge(pT_drained, NT * hp + qb + 1)
                            if qb % TPC == 0 and qb // TPC >= 2:
                                pe.wait_ge(av_drained, NC * hp + qb // TPC)
                            to = ps[:, 6 + qb // TPC % 2, P * (qb % TPC):P * (qb % TPC + 1)]
                            for g in range(2):
                                mm = pe.matmul(to[64 * g:64 * (g + 1), :], v1[:, qb, 64 * g:64 * (g + 1)],
                                               pT[:, qb % 4, P * g:P * (g + 1)], start=True, stop=(qb == 0))
                            if qb:
                                for g in range(2):
                                    mm = pe.matmul(to[64 * g:64 * (g + 1), :], v2[0:TAIL, qb, 64 * g:64 * (g + 1)],
                                                   pT[0:TAIL, qb % 4, P * (2 + g):P * (3 + g)], start=False, stop=True)
                            mm.then_inc(av_done, 1)
                    pe.wait_ge(s_masked, 2 * NT * (hp + 1))
                    pe.wait_ge(pT_drained, NT * (hp + 1))

            @block.scalar
            def _(act):
                with act.Fori(0, NP1) as hp:
                    for c in range(NC):
                        act.wait_ge(qk_filled, 2 * NC * hp + 2 * c + 1)
                        act.activation(qT[:, CH * c:CH * (c + 1)], ps[:, 2 * c % 4, :], ACT.Copy).then_inc(q_drained, 1)
                    for c in range(NC):
                        act.wait_ge(v_filled, 2 * NC * hp + 2 * c + 1)
                        act.activation(v1[:, TPC * c:TPC * (c + 1), :],
                                       ps[:, 4 + 2 * c % 4, :].rearrange("p (t d) -> p t d", d=P), ACT.Copy)\
                           .then_inc(v1_drained, 1)
                    for step in range(NT + T_LAG):
                        qb = step
                        if qb < NT:
                            for g in range(2):
                                act.wait_ge(s_masked, 2 * NT * hp + 2 * qb + g + 1)
                                p = p1[:, qb % NSLOT, g, 0:width(qb)]
                                act.activation(p, p, ACT.Exp, scale=-1.0, bias=nmax1[:, qb % NSLOT, g:g + 1],
                                               accum_out=rsum1[:, qb % NSLOT, g:g + 1]).then_inc(exped, 1)
                        qb = step - T_LAG
                        if qb >= 0:
                            act.wait_ge(pT_filled, NT * hp + qb + 1)
                            frm = ps[:, 4 + qb % 2, :]
                            ins = act.activation(pT[:, qb % 4, 0:2 * P], frm[:, 0:2 * P], ACT.Copy)
                            if qb:
                                ins = act.activation(pT[0:TAIL, qb % 4, 2 * P:4 * P], frm[0:TAIL, 2 * P:4 * P], ACT.Copy)
                            ins.then_inc(pT_drained, 1)

            @block.vector
            def _(dve):
                dve.sem_inc(av_drained, 1)
                with dve.Fori(0, NP1) as hp:
                    for c in range(NC):
                        dve.wait_ge(qk_filled, 2 * NC * hp + 2 * c + 2)
                        dve.tensor_copy(kT[:, CH * c:CH * (c + 1)], ps[:, (2 * c + 1) % 4, :]).then_inc(k_drained, 1)
                    for c in range(NC):
                        dve.wait_ge(v_filled, 2 * NC * hp + 2 * c + 2)
                        t0 = 1 if c == 0 else 0
                        dve.tensor_copy(v2[0:TAIL, TPC * c + t0:TPC * (c + 1), :],
                                        ps[0:TAIL, 4 + (2 * c + 1) % 4, P * t0:].rearrange("p (t d) -> p t d", d=P))\
                           .then_inc(v2_drained, 1)
                    for step in range(NT + OUT_LAG):
                        qb = step
                        if qb < NT:
                            dve.wait_ge(s_filled, NT * hp + qb + 1)
                            if qb >= NSLOT:
                                dve.wait_ge(pT_filled, NT * hp + qb - NSLOT + 1)
                            dve.sem_inc(mask_turns, 1)
                            for g in range(2):
                                dve.tensor_tensor_reduce(
                                    p1[:, qb % NSLOT, g, 0:width(qb)], ps[:, 2 * (qb % 2) + g, 0:width(qb)],
                                    masks[:, :] if qb else mask0[:, :], -SC1, BIG, ALU.add, ALU.min,
                                    nmax1[:, qb % NSLOT, g:g + 1]).then_inc(s_masked, 1)
                        qb = step - 1
                        if 0 <= qb < NT:
                            dve.wait_ge(exped, 2 * NT * hp + 2 * (qb + 1))
                            dve.reciprocal(rinv1[:, qb % NSLOT, :], rsum1[:, qb % NSLOT, :]).then_inc(recips, 1)
                        qb = step - OUT_LAG
                        if qb >= 0 and qb % TPC == TPC - 1:
                            c = qb // TPC
                            dve.wait_ge(av_done, NT * hp + qb + 1)
                            dve.tensor_copy(outT1[:, ds(hp, 1), CH * c:CH * (c + 1)],
                                            ps[:, 6 + c % 2, :].unsqueeze(1)).then_inc(av_drained, 1)

        o_ready = sem("o_ready")
        o_gated = sem("o_gated")
        x2_done = sem("x2_done")
        stored = sem("stored")
        with nc.Block() as block:
            @block.tensor
            def _(pe):
                for c in range(NC):
                    for t in range(TPC):
                        for h in range(NP1):
                            mm = pe.matmul(ps[:, c, P * t:P * (t + 1)],
                                           outT1[:, h, CH * c + P * t:CH * c + P * (t + 1)], wout_sb[:, h, :],
                                           start=(h == 0), stop=(h == NP1 - 1))
                    mm.then_inc(o_ready, 1)

            @block.vector
            def _(dve):
                for c in range(NC):
                    cols = slice(CH * c, CH * (c + 1))
                    dve.wait_ge(o_ready, c + 1)
                    dve.tensor_tensor(tmp[:, c % 2, :], ps[:, c, :], flat(gate_sb)[:, cols], ALU.mult).then_inc(o_gated, 1)
                    dve.wait_ge(o_gated, c + 1)
                    dve.tensor_tensor(flat(x_sb)[:, cols], flat(x_sb)[:, cols], tmp[:, c % 2, :], ALU.add)\
                       .then_inc(x2_done, 1)

            @block.sync
            def _(sp):
                for c in range(NC):
                    sp.wait_ge(x2_done, c + 1)
                    sp.dma_start(out[0, CH * c:CH * (c + 1), :].rearrange("(t p) d -> p t d", p=P),
                                 x_sb[:, TPC * c:TPC * (c + 1), :]).then_inc(stored, 16)
                sp.wait_ge(stored, NC * 16)


_INS = ['L0_attn_x', 'L0_attn_theta_log', 'L0_attn_nu_log', 'L0_attn_gamma_log', 'L0_attn_B_re', 'L0_attn_B_im',
        'L0_attn_C_re', 'L0_attn_C_im', 'L0_attn_D', 'L0_ffn_W_qkv', 'L0_ffn_b_qkv', 'L0_ffn_W_gate',
        'L0_ffn_b_gate', 'L0_ffn_W_experts', 'L0_ffn_b_experts', 'L1_attn_w_qkv', 'L1_attn_w_out',
        'L1_ffn_W1', 'L1_ffn_b1', 'L1_ffn_W2', 'L1_ffn_b2']
_OUTS = [((1, 2048, 128), 'float32')]


def kernel(**inputs):
    import numpy as _np
    import concourse.bacc as _bacc
    from concourse import mybir as _mybir
    from concourse.bass_utils import run_bass_kernel_spmd as _run

    nc = _bacc.Bacc("TRN2", target_bir_lowering=False, num_devices=1)
    arrays, args = {}, []
    for name in _INS:
        a = _np.ascontiguousarray(inputs[name])
        arrays[f"in_{name}_dram"] = a
        args.append(nc.dram_tensor(f"in_{name}_dram", a.shape, _mybir.dt.from_np(a.dtype), kind="ExternalInput").ap())
    for i, (shape, dtype) in enumerate(_OUTS):
        dt = _mybir.dt.from_np(_np.dtype(dtype))
        args.append(nc.dram_tensor(f"out_{i}_dram", shape, dt, kind="ExternalOutput").ap())
    recurrent_moe_sparse_attention_kernel(nc, *args)
    r = _run(nc, [arrays], core_ids=[0])
    got = tuple(r.results[0][f"out_{i}_dram"] for i in range(len(_OUTS)))
    return got[0]
```

```python
import concourse.bass as bass
from concourse import mybir
from contextlib import ExitStack


def recurrent_moe_sparse_attention_kernel(
    nc, x, theta_log, nu_log, gamma_log, B_re, B_im, C_re, C_im, D_skip,
    W_qkv0, b_qkv0, W_gate, b_gate, W_experts, b_experts,
    W_qkv1, W_out1, W1, b1, W2, b2, out,
):
    fp32 = mybir.dt.float32
    bf16 = mybir.dt.bfloat16
    i32 = mybir.dt.int32
    ALU = mybir.AluOpType
    ACT = mybir.ActivationFunctionType
    AX = mybir.AxisListType
    ds = bass.ds

    P = 128
    S, D = x.shape[1], x.shape[2]
    NT = S // P
    CH = 512
    NC = S // CH
    TPC = CH // P
    EPS = 1e-5
    HID = theta_log.shape[0]
    NE = W_gate.shape[1]
    H0 = 16
    HD0 = D // H0
    G0 = 4
    NG0 = H0 // G0
    NB = NC * NG0
    SC0 = float(HD0) ** -0.5
    NPROD = 6
    KR = NPROD * HD0
    H1 = 16
    HD1 = W_out1.shape[0] // H1
    NP1 = H1 // 2
    SC1 = float(HD1) ** -0.5
    HALF = 16
    GLOB = 64
    WIN = P + HALF
    KW = WIN + GLOB
    TAIL = KW - P
    NI = W1.shape[1] // P
    NEG = -1.0e30
    BIG = 3.0e38
    TWO_PI_HI = 6.28125
    TWO_PI_LO = 0.0019353071795864769
    PI_2 = 1.5707963267948966

    ctx = ExitStack()
    with ctx:
        def sb(name, shape, dt=fp32):
            return ctx.enter_context(nc.sbuf_tensor(name, shape, dt))

        def sem(name):
            return ctx.enter_context(nc.semaphore(name))

        x_sb = sb("x_sb", [P, NT, D])
        xT = sb("xT", [P, S])
        layer0 = sb("layer0", [P, 3, S])
        y_sb, attn_sb, v_sb = [layer0[:, n, :].rearrange("p (t d) -> p t d", d=D) for n in range(3)]
        gate_sb = sb("gate_sb", [P, NT, D])
        ident = sb("ident", [P, P])
        ones_row = sb("ones_row", [1, P])
        w1qkv_sb = sb("w1qkv_sb", [P, 3, H1 * HD1])
        wout_sb = sb("wout_sb", [P, NP1, D])
        W1_sb = sb("W1_sb", [P, NI * P])
        W2_sb = sb("W2_sb", [P, NI, D])
        b1_sb = sb("b1_sb", [P, NI])
        b2_sb = sb("b2_sb", [1, D])
        stats = sb("stats", [P, NT, 6])
        mv = sb("mv", [P, NT, 2])
        var_eps = sb("var_eps", [P, NT])
        std = sb("std", [P, NT])
        rstd = sb("rstd", [P, NT])
        masks = sb("masks", [P, KW])
        mask0 = sb("mask0", [P, P])

        ARENA = 13 * S + 64 * 2
        arena = sb("arena", [P, ARENA])

        def cut(at, words):
            assert at + words <= ARENA
            return arena[:, at:at + words]

        xn_sb = cut(0, S).rearrange("p (t d) -> p t d", d=D)
        cos_t, sin_t, rot_x, state, st_cos, st_sin = [cut(S * (n + 1), S) for n in range(6)]
        partsQ = cut(7 * S, 3 * S // 2).bitcast(bf16).rearrange("p (a n) -> p a n", a=3)
        partsK = cut(7 * S + 3 * S // 2, 3 * S // 2).bitcast(bf16).rearrange("p (a n) -> p a n", a=3)
        qk32 = cut(10 * S, 2 * CH).rearrange("p (a n) -> p a n", a=2)
        rest = cut(10 * S + 2 * CH, 2 * CH).rearrange("p (a n) -> p a n", a=2)
        kmax = [cut(S * n, S).bitcast(bf16).rearrange("p (t n) -> p t n", t=2) for n in range(2)]
        kexp = [cut(S * (2 + n), S).bitcast(bf16).rearrange("p (t n) -> p t n", t=2) for n in range(2)]
        qmax, qexp = [[cut(4 * S + 2 * CH * n + S * m, 2 * CH).bitcast(bf16)
                       .rearrange("p (g t n) -> p g t n", g=2, t=2) for n in range(2)] for m in range(2)]
        probs = [cut(6 * S + 2 * CH * n, 2 * CH).rearrange("p (g n) -> p g n", g=2) for n in range(4)]
        vst = [cut(8 * S + S * n, S).rearrange("p (t j d) -> p t j d", j=G0, d=32) for n in range(2)]
        outT0 = [cut(10 * S + CH * n, CH) for n in range(2)]
        outT1 = cut(0, NP1 * S).rearrange("p (h n) -> p h n", h=NP1)
        hT = cut(0, NI * S).rearrange("p (i n) -> p i n", i=NI)
        qT = cut(8 * S, S)
        k_pad = cut(9 * S, 2 * S).rearrange("p (g n) -> p g n", g=2)
        v1 = cut(11 * S, S + P).rearrange("p (t d) -> p t d", d=P)
        v2 = cut(12 * S + P, S - P).rearrange("p (t d) -> p t d", d=P)

        prm = sb("prm", [P, 3])
        eprm = sb("eprm", [P, 3])
        r_col = sb("r_col", [P, 1])
        ang = sb("ang", [P, 8])
        ang_i = sb("ang_i", [P, 1], i32)
        pw = sb("pw", [P, 12, 4])
        rot_tmp = sb("rot_tmp", [P, S // 2])
        B_sb = sb("B_sb", [P, 2, D])
        C_sb = sb("C_sb", [P, 2, 2 * HID])
        BT = sb("BT", [P, 2, P])
        CT = sb("CT", [P, 2, D])
        D_col = sb("D_col", [P, 1])
        D_diag = sb("D_diag", [P, P])
        w0_sb = sb("w0_sb", [P, 3, D])
        bqk_col = sb("bqk_col", [P, 2])
        bv_row = sb("bv_row", [1, D])
        wg_sb = sb("wg_sb", [P, NE])
        bg_row = sb("bg_row", [1, NE])
        we_sb = sb("we_sb", [P, NE, D])
        be_sb = sb("be_sb", [NE, D])
        logits = sb("logits", [P, NT, NE])
        gmax = sb("gmax", [P, NT])
        gsum = sb("gsum", [P, NT])
        gates = sb("gates", [P, NT, NE])
        beats = cut(11 * S, NT * NE * NE).rearrange("p (t e j) -> p t e j", e=NE, j=NE)
        ties = cut(11 * S + NT * NE * NE, NT * NE * NE).rearrange("p (t e j) -> p t e j", e=NE, j=NE)
        lower = sb("lower", [P, NE, NE])
        combT = sb("combT", [NE, S])
        tile_max = sb("tile_max", [P, 2 * TPC * 2, NC])
        neg_max = sb("neg_max", [P, 2 * TPC * 2])
        max_rows = sb("max_rows", [2 * TPC * 2, 2, P], bf16)
        rden0 = sb("rden0", [P, TPC * G0])
        wst = sb("wst", [P, 3, P])
        NSLOT = 8
        p1 = layer0[:, :, :].rearrange("p a n -> p (a n)")[:, 0:NSLOT * 2 * KW]\
            .rearrange("p (s g n) -> p s g n", g=2, n=KW)
        nmax1 = sb("nmax1", [P, NSLOT, 2])
        rsum1 = sb("rsum1", [P, NSLOT, 2])
        rinv1 = sb("rinv1", [P, NSLOT, 2])
        pT = layer0[:, 2, :].rearrange("p (s n) -> p s n", n=CH)
        tmp = rot_tmp[:, :].rearrange("p (s n) -> p s n", n=CH)

        ps = ctx.enter_context(nc.psum_tensor("ps", [P, 8, CH], fp32))

        q_parts = nc.dram_tensor("q_parts", [NPROD, P, S], bf16, kind="Internal").ap()
        k_parts = nc.dram_tensor("k_parts", [NPROD, P, S], bf16, kind="Internal").ap()
        Q_PART = [0, 0, 0, 1, 1, 2]
        K_PART = [0, 1, 2, 0, 1, 0]

        x_loaded = sem("x_loaded")
        rec_loaded = sem("rec_loaded")
        att_loaded = sem("att_loaded")
        moe_loaded = sem("moe_loaded")
        l1_loaded = sem("l1_loaded")
        consts_made = sem("consts_made")
        stats_done = sem("stats_done")
        std_done = sem("std_done")
        xn_done = sem("xn_done")
        prm_done = sem("prm_done")
        angle_steps = sem("angle_steps")
        sin_done = sem("sin_done")
        filled = sem("filled")
        act_drained = sem("act_drained")
        dve_drained = sem("dve_drained")
        parts_done = sem("parts_done")
        parts_steps = sem("parts_steps")
        hi_done = sem("hi_done")
        table_steps = sem("table_steps")
        rot_done = sem("rot_done")
        rot_steps = sem("rot_steps")
        scan_done = sem("scan_done")
        back_done = sem("back_done")
        diag_done = sem("diag_done")
        gate_steps = sem("gate_steps")
        gexp_in = sem("gexp_in")
        gexp_done = sem("gexp_done")
        comb_done = sem("comb_done")
        moe_steps = sem("moe_steps")
        parts_stored = sem("parts_stored")

        jobs = [("xT", c, "act") for c in range(NC)]
        jobs += [("BT", 0, "act"), ("CT", 0, "act")]
        jobs += [(k, c, "act") for k in ("q", "k") for c in range(NC)]
        jobs += [("logits", 0, "dve")]
        jobs += [("v", c, "act") for c in range(NC)]
        jobs += [(k, c, "dve") for c in range(NC) for k in ("u", "w")]
        jobs += [("combT", c, "act") for c in range(NC)]
        jobs += [("bias", c, "act") for c in range(NC)]
        jobs += [("experts", n, "dve") for n in range(2 * NT)]
        jobs += [("y", c, "act") for c in range(NC)]
        nth = {}
        seen = {"act": 0, "dve": 0}
        for n, (kind, c, eng) in enumerate(jobs):
            seen[eng] += 1
            nth[kind, c] = (n, seen[eng])
        drained = {"act": act_drained, "dve": dve_drained}

        def bank(kind, c):
            return ps[:, nth[kind, c][0] % 8, :]

        with nc.Block() as block:
            @block.sync
            def _(sp):
                sp.dma_start(x_sb[:, :, :], x[0].rearrange("(t p) d -> p t d", p=P)).then_inc(x_loaded, 16)
                sp.dma_start(w0_sb[:, :, :], W_qkv0.rearrange("k (s n) -> k s n", s=3)).then_inc(att_loaded, 16)
                sp.dma_start(bqk_col[:, 0:1], b_qkv0[0:D].rearrange("(p a) -> p a", a=1)).then_inc(att_loaded, 16)
                sp.dma_start(bqk_col[:, 1:2], b_qkv0[D:2 * D].rearrange("(p a) -> p a", a=1)).then_inc(att_loaded, 16)
                sp.dma_start(bv_row[:, :], b_qkv0[2 * D:3 * D].rearrange("(a n) -> a n", a=1)).then_inc(att_loaded, 16)
                sp.dma_start(wg_sb[:, :], W_gate).then_inc(moe_loaded, 16)
                sp.dma_start(bg_row[:, :], b_gate.rearrange("(a n) -> a n", a=1)).then_inc(moe_loaded, 16)
                sp.dma_start(we_sb[:, :, :], W_experts.rearrange("e d f -> d e f")).then_inc(moe_loaded, 16)
                sp.dma_start(be_sb[:, :], b_experts).then_inc(moe_loaded, 16)
                sp.dma_start(w1qkv_sb[:, :, :], W_qkv1.rearrange("k (s n) -> k s n", s=3)).then_inc(l1_loaded, 16)
                sp.dma_start(wout_sb[:, :, :], W_out1.rearrange("(h p) n -> p h n", p=P)).then_inc(l1_loaded, 16)
                sp.dma_start(W1_sb[:, :], W1).then_inc(l1_loaded, 16)
                sp.dma_start(W2_sb[:, :, :], W2.rearrange("(p i) n -> p i n", p=P)).then_inc(l1_loaded, 16)
                sp.dma_start(b1_sb[:, :], b1.rearrange("(p i) -> p i", p=P)).then_inc(l1_loaded, 16)
                sp.dma_start(b2_sb[:, :], b2.rearrange("(a n) -> a n", a=1)).then_inc(l1_loaded, 16)
                for n, (parts, order, dram) in enumerate(((partsQ, Q_PART, q_parts), (partsK, K_PART, k_parts))):
                    sp.wait_ge(parts_done, NC * (n + 1))
                    for r in range(NPROD):
                        sp.dma_start(dram[r], parts[:, order[r], :]).then_inc(parts_stored, 16)
                sp.wait_ge(parts_stored, 2 * NPROD * 16)
                sp.wait_ge(l1_loaded, 6 * 16)

            @block.gpsimd
            def _(pool):
                pool.memset(ident[:, :], 0.0).then_inc(consts_made, 1)
                pool.memset(ones_row[:, :], 1.0).then_inc(consts_made, 1)
                pool.memset(lower[:, :, :], 1.0).then_inc(consts_made, 1)
                pool.memset(masks[:, :], 0.0).then_inc(consts_made, 1)
                pool.memset(mask0[:, :], 0.0).then_inc(consts_made, 1)
                pool.wait_ge(consts_made, 5)
                pool.affine_select(out=ident[:, :], in_=ident[:, :], compare_op=ALU.not_equal, fill=1.0,
                                   base=0, pattern=[[-1, P]], channel_multiplier=1).then_inc(consts_made, 1)
                pool.affine_select(out=lower[:, :, :], in_=lower[:, :, :], compare_op=ALU.is_gt, fill=0.0,
                                   base=0, pattern=[[1, NE], [-1, NE]], channel_multiplier=0).then_inc(consts_made, 1)
                pool.affine_select(out=masks[:, 0:WIN], in_=masks[:, 0:WIN], compare_op=ALU.is_ge, fill=NEG,
                                   base=0, pattern=[[1, WIN]], channel_multiplier=-1).then_inc(consts_made, 1)
                pool.affine_select(out=mask0[:, GLOB:P], in_=mask0[:, GLOB:P], compare_op=ALU.is_ge, fill=NEG,
                                   base=HALF + GLOB, pattern=[[1, P - GLOB]], channel_multiplier=-1).then_inc(consts_made, 1)
                pool.wait_ge(consts_made, 9)
                pool.affine_select(out=masks[:, 0:WIN], in_=masks[:, 0:WIN], compare_op=ALU.is_ge, fill=NEG,
                                   base=HALF, pattern=[[-1, WIN]], channel_multiplier=1).then_inc(consts_made, 1)
                pool.affine_select(out=mask0[:, :], in_=mask0[:, :], compare_op=ALU.is_ge, fill=NEG,
                                   base=0, pattern=[[-1, P]], channel_multiplier=1).then_inc(consts_made, 1)
                pool.wait_ge(scan_done, 1)
                pool.tensor_tensor(st_cos, state, cos_t, ALU.mult).then_inc(back_done, 1)
                pool.tensor_tensor(st_sin, state, sin_t, ALU.mult).then_inc(back_done, 1)

            @block.scalar
            def _(act):
                for h in range(2):
                    half = slice(HID * h, HID * (h + 1))
                    act.dma_start(prm[half, 0:1], theta_log.rearrange("(p a) -> p a", a=1)).then_inc(rec_loaded, 16)
                    act.dma_start(prm[half, 1:2], nu_log.rearrange("(p a) -> p a", a=1)).then_inc(rec_loaded, 16)
                    act.dma_start(prm[half, 2:3], gamma_log.rearrange("(p a) -> p a", a=1)).then_inc(rec_loaded, 16)
                    act.dma_start(B_sb[half, h, :], B_re).then_inc(rec_loaded, 16)
                    act.dma_start(B_sb[half, 1 - h, :], B_im).then_inc(rec_loaded, 16)
                act.dma_start(C_sb[:, 0, 0:HID], C_re).then_inc(rec_loaded, 16)
                act.dma_start(C_sb[:, 0, HID:], C_im).then_inc(rec_loaded, 16)
                act.dma_start(C_sb[:, 1, 0:HID], C_im).then_inc(rec_loaded, 16)
                act.dma_start(C_sb[:, 1, HID:], C_re).then_inc(rec_loaded, 16)
                act.dma_start(D_col[:, :], D_skip.rearrange("(p a) -> p a", a=1)).then_inc(rec_loaded, 16)
                act.wait_ge(rec_loaded, 15 * 16)
                act.activation(eprm[:, :], prm[:, :], ACT.Exp).then_inc(prm_done, 1)
                act.wait_ge(prm_done, 1)
                act.activation(r_col[:, :], eprm[:, 1:2], ACT.Exp, scale=-1.0).then_inc(prm_done, 1)
                act.wait_ge(stats_done, 2 * NT + 1)
                act.activation(std[:, :], var_eps[:, :], ACT.Sqrt).then_inc(std_done, 1)
                act.wait_ge(angle_steps, 7)
                act.activation(ang[:, 4:6], ang[:, 2:4], ACT.Sin).then_inc(sin_done, 1)

                def drain(kind, c, dst, **how):
                    n, k = nth[kind, c]
                    act.wait_ge(filled, n + 1)
                    act.activation(dst, how.pop("src", bank(kind, c)), how.pop("func", ACT.Copy), **how)\
                       .then_inc(act_drained, 1)

                for c in range(NC):
                    drain("xT", c, xT[:, CH * c:CH * (c + 1)])
                drain("BT", 0, BT[:, :, :], src=bank("BT", 0)[:, 0:2 * P].rearrange("p (a n) -> p a n", a=2))
                drain("CT", 0, CT[:, :, :], src=bank("CT", 0)[:, 0:2 * P].rearrange("p (a n) -> p a n", a=2))
                act.wait_ge(att_loaded, 4 * 16)
                for n, (kind, parts) in enumerate((("q", partsQ), ("k", partsK))):
                    for c in range(NC):
                        m = NC * n + c
                        if m >= 2:
                            act.wait_ge(parts_done, m - 1)
                        act.wait_ge(filled, nth[kind, c][0] + 1)
                        act.activation(parts[:, 0, CH * c:CH * (c + 1)], bank(kind, c), ACT.Identity,
                                       bias=bqk_col[:, n:n + 1]).then_inc(hi_done, 1)
                        drain(kind, c, qk32[:, m % 2, :], func=ACT.Identity, bias=bqk_col[:, n:n + 1])
                for c in range(NC):
                    drain("v", c, v_sb[:, TPC * c:TPC * (c + 1), :],
                          src=bank("v", c).rearrange("p (t d) -> p t d", d=D))
                act.wait_ge(gexp_in, 1)
                act.activation(gates[:, :, :], logits[:, :, :], ACT.Exp).then_inc(gexp_done, 1)
                for c in range(NC):
                    drain("combT", c, combT[:, CH * c:CH * (c + 1)], src=bank("combT", c)[0:NE, :])
                for c in range(NC):
                    drain("bias", c, gate_sb[:, TPC * c:TPC * (c + 1), :],
                          src=bank("bias", c).rearrange("p (t d) -> p t d", d=D))
                for c in range(NC):
                    drain("y", c, y_sb[:, TPC * c:TPC * (c + 1), :],
                          src=bank("y", c).rearrange("p (t d) -> p t d", d=D))

            @block.tensor
            def _(pe):
                def begin(kind, c):
                    n = nth[kind, c][0]
                    if n >= 8:
                        k, cc, eng = jobs[n - 8]
                        pe.wait_ge(drained[eng], nth[k, cc][1])
                    return bank(kind, c)

                pe.wait_ge(consts_made, 6)
                for c in range(NC):
                    to = begin("xT", c)
                    for t in range(TPC):
                        pe.wait_ge(xn_done, TPC * c + t + 1)
                        mm = pe.transpose(to[:, P * t:P * (t + 1)], xn_sb[:, TPC * c + t, :], ident[:, :])
                    mm.then_inc(filled, 1)
                pe.wait_ge(diag_done, 6)
                to = begin("BT", 0)
                for a in range(2):
                    mm = pe.transpose(to[:, P * a:P * (a + 1)], B_sb[:, a, :], ident[:, :])
                mm.then_inc(filled, 1)
                to = begin("CT", 0)
                for a in range(2):
                    mm = pe.transpose(to[:, P * a:P * (a + 1)], C_sb[:, a, :], ident[:, :])
                mm.then_inc(filled, 1)
                pe.wait_ge(att_loaded, 4 * 16)
                for n, kind in enumerate(("q", "k")):
                    for c in range(NC):
                        pe.wait_ge(act_drained, nth["xT", c][1])
                        pe.matmul(begin(kind, c), w0_sb[:, n, :], xT[:, CH * c:CH * (c + 1)],
                                  start=True, stop=True).then_inc(filled, 1)
                pe.wait_ge(moe_loaded, 4 * 16)
                to = begin("logits", 0)
                for t in range(NT):
                    pe.matmul(to[:, NE * t:NE * (t + 1)], xT[:, P * t:P * (t + 1)], wg_sb[:, :],
                              start=True, stop=False)
                    mm = pe.matmul(to[:, NE * t:NE * (t + 1)], ones_row[:, :], bg_row[:, :],
                                   start=False, stop=True)
                mm.then_inc(filled, 1)
                for c in range(NC):
                    to = begin("v", c)
                    for t in range(TPC):
                        cols = slice(P * t, P * (t + 1))
                        pe.matmul(to[:, cols], xT[:, CH * c + P * t:CH * c + P * (t + 1)], w0_sb[:, 2, :],
                                  start=True, stop=False)
                        mm = pe.matmul(to[:, cols], ones_row[:, :], bv_row[:, :], start=False, stop=True)
                    mm.then_inc(filled, 1)
                pe.wait_ge(act_drained, nth["BT", 0][1])
                for c in range(NC):
                    for a, kind in enumerate(("u", "w")):
                        pe.matmul(begin(kind, c), BT[:, a, :], xT[:, CH * c:CH * (c + 1)],
                                  start=True, stop=True).then_inc(filled, 1)
                pe.wait_ge(comb_done, 1)
                for c in range(NC):
                    to = begin("combT", c)
                    for t in range(TPC):
                        mm = pe.transpose(to[0:NE, P * t:P * (t + 1)], gates[:, TPC * c + t, :], ident[:, :])
                    mm.then_inc(filled, 1)
                for c in range(NC):
                    pe.wait_ge(act_drained, nth["combT", c][1])
                    to = begin("bias", c)
                    for t in range(TPC):
                        mm = pe.matmul(to[:, P * t:P * (t + 1)], combT[:, CH * c + P * t:CH * c + P * (t + 1)],
                                       be_sb[:, :], start=True, stop=True)
                    mm.then_inc(filled, 1)
                for n in range(2 * NT):
                    pe.matmul(begin("experts", n), xT[:, P * (n // 2):P * (n // 2 + 1)],
                              we_sb[:, NE // 2 * (n % 2):NE // 2 * (n % 2 + 1), :].rearrange("p e f -> p (e f)"),
                              start=True, stop=True).then_inc(filled, 1)
                pe.wait_ge(act_drained, nth["CT", 0][1])
                pe.wait_ge(back_done, 2)
                for c in range(NC):
                    to = begin("y", c)
                    for t in range(TPC):
                        tok = slice(CH * c + P * t, CH * c + P * (t + 1))
                        cols = slice(P * t, P * (t + 1))
                        pe.matmul(to[:, cols], st_cos[:, tok], CT[:, 0, :], start=True, stop=False)
                        pe.matmul(to[:, cols], st_sin[:, tok], CT[:, 1, :], start=False, stop=False)
                        mm = pe.matmul(to[:, cols], xT[:, tok], D_diag[:, :], start=False, stop=True)
                    mm.then_inc(filled, 1)

            @block.vector
            def _(dve):
                dve.wait_ge(x_loaded, 16)
                for t in range(NT):
                    dve.bn_stats(stats[:, t, :], x_sb[:, t, :]).then_inc(stats_done, 1)
                dve.wait_ge(stats_done, NT)
                for t in range(NT):
                    dve.bn_aggr(mv[:, t, :], stats[:, t, :]).then_inc(stats_done, 1)
                dve.wait_ge(stats_done, 2 * NT)
                dve.tensor_scalar(var_eps[:, :], mv[:, :, 1], EPS, None, ALU.add).then_inc(stats_done, 1)
                dve.wait_ge(prm_done, 2)
                th = eprm[:, 0:1]
                dve.tensor_scalar(ang_i[:, :], th, 1.0 / (TWO_PI_HI + TWO_PI_LO), None, ALU.mult)\
                   .then_inc(angle_steps, 1)
                dve.wait_ge(angle_steps, 1)
                dve.tensor_copy(ang[:, 0:1], ang_i[:, :]).then_inc(angle_steps, 1)
                dve.wait_ge(angle_steps, 2)
                dve.scalar_tensor_tensor(out=ang[:, 1:2], in0=ang[:, 0:1], scalar=-TWO_PI_HI, in1=th,
                                         op0=ALU.mult, op1=ALU.add).then_inc(angle_steps, 1)
                dve.wait_ge(angle_steps, 3)
                dve.scalar_tensor_tensor(out=ang[:, 6:7], in0=ang[:, 0:1], scalar=-TWO_PI_LO, in1=ang[:, 1:2],
                                         op0=ALU.mult, op1=ALU.add).then_inc(angle_steps, 1)
                dve.wait_ge(angle_steps, 4)
                dve.tensor_scalar(ang[:, 2:3], ang[:, 6:7], 0.5, None, ALU.mult).then_inc(angle_steps, 1)
                dve.wait_ge(angle_steps, 5)
                dve.scalar_tensor_tensor(out=ang[:, 7:8], in0=ang[:, 2:3], scalar=-1.0, in1=ang[:, 2:3],
                                         op0=ALU.mult, op1=ALU.max).then_inc(angle_steps, 1)
                dve.wait_ge(angle_steps, 6)
                dve.tensor_scalar(ang[:, 3:4], ang[:, 7:8], -1.0, PI_2, ALU.mult, ALU.add).then_inc(angle_steps, 1)
                dve.wait_ge(std_done, 1)
                dve.reciprocal(rstd[:, :], std[:, :]).then_inc(stats_done, 1)
                dve.wait_ge(stats_done, 2 * NT + 2)
                for t in range(NT):
                    dve.tensor_scalar(xn_sb[:, t, :], x_sb[:, t, :], mv[:, t, 0:1], rstd[:, t:t + 1],
                                      ALU.subtract, ALU.mult).then_inc(xn_done, 1)
                gam = eprm[:, 2:3]
                lo, hi = slice(0, HID), slice(HID, 2 * HID)
                dve.tensor_scalar(B_sb[:, 0, :], B_sb[:, 0, :], gam, None, ALU.mult).then_inc(diag_done, 1)
                dve.tensor_scalar(B_sb[lo, 1, :], B_sb[lo, 1, :], gam[lo], None, ALU.mult).then_inc(diag_done, 1)
                dve.tensor_scalar(B_sb[hi, 1, :], B_sb[hi, 1, :], gam[hi], -1.0, ALU.mult, ALU.mult)\
                   .then_inc(diag_done, 1)
                dve.tensor_scalar(C_sb[:, 0, HID:], C_sb[:, 0, HID:], -1.0, None, ALU.mult).then_inc(diag_done, 1)
                dve.tensor_scalar(C_sb[:, 1, :], C_sb[:, 1, :], -1.0, None, ALU.mult).then_inc(diag_done, 1)
                dve.wait_ge(consts_made, 11)
                dve.tensor_scalar(D_diag[:, :], ident[:, :], D_col[:, 0:1], None, ALU.mult).then_inc(diag_done, 1)
                steps = 0
                for m in range(2 * NC):
                    parts, c = (partsQ, partsK)[m // NC], m % NC
                    cols = slice(CH * c, CH * (c + 1))
                    kind = ("q", "k")[m // NC]
                    dve.wait_ge(act_drained, nth[kind, c][1])
                    dve.wait_ge(hi_done, m + 1)
                    dve.tensor_tensor(rest[:, m % 2, :], qk32[:, m % 2, :], parts[:, 0, cols], ALU.subtract)\
                       .then_inc(parts_steps, 1)
                    dve.wait_ge(parts_steps, 2 * m + 1)
                    dve.tensor_copy(parts[:, 1, cols], rest[:, m % 2, :]).then_inc(parts_steps, 1)
                    dve.wait_ge(parts_steps, 2 * m + 2)
                    dve.tensor_tensor(parts[:, 2, cols], rest[:, m % 2, :], parts[:, 1, cols], ALU.subtract)\
                       .then_inc(parts_done, 1)
                gs = 0
                def gstep(ins):
                    nonlocal gs
                    gs += 1
                    ins.then_inc(gate_steps, 1)
                    dve.wait_ge(gate_steps, gs)
                dve.wait_ge(filled, nth["logits", 0][0] + 1)
                src = bank("logits", 0)[:, 0:NT * NE].rearrange("p (t e) -> p t e", e=NE)
                gstep(dve.tensor_reduce(gmax[:, :], src, AX.X, ALU.max))
                dve.tensor_tensor(logits[:, :, :], src, gmax[:, :].unsqueeze(2).broadcast_to([P, NT, NE]),
                                  ALU.subtract).then_inc(dve_drained, 1)
                dve.wait_ge(dve_drained, nth["logits", 0][1])
                dve.sem_inc(gexp_in, 1)
                ts = 0
                def tstep(ins):
                    nonlocal ts
                    ts += 1
                    ins.then_inc(table_steps, 1)
                    return ts
                dve.wait_ge(sin_done, 1)
                sh, chh = ang[:, 4:5], ang[:, 5:6]

                def double(level, s, c):
                    n = tstep(dve.tensor_tensor(pw[:, level, 2:3], s, s, ALU.mult))
                    dve.wait_ge(table_steps, n)
                    tstep(dve.tensor_scalar(pw[:, level, 0:1], pw[:, level, 2:3], -2.0, 1.0, ALU.mult, ALU.add))
                    n = tstep(dve.scalar_tensor_tensor(out=pw[:, level, 1:2], in0=s, scalar=2.0, in1=c,
                                                       op0=ALU.mult, op1=ALU.mult))
                    dve.wait_ge(table_steps, n)

                double(0, sh, chh)
                tstep(dve.memset(cos_t[:, 0:1], 1.0))
                n = tstep(dve.memset(sin_t[:, 0:1], 0.0))
                dve.wait_ge(table_steps, n)
                size, level = 1, 0
                while size < S:
                    c1, s1 = pw[:, level, 0:1], pw[:, level, 1:2]
                    a, b = slice(0, size), slice(size, 2 * size)
                    n = tstep(dve.tensor_scalar(rot_tmp[:, a], sin_t[:, a], s1, None, ALU.mult))
                    dve.wait_ge(table_steps, n)
                    n = tstep(dve.scalar_tensor_tensor(out=cos_t[:, b], in0=cos_t[:, a], scalar=c1,
                                                       in1=rot_tmp[:, a], op0=ALU.mult, op1=ALU.subtract))
                    dve.wait_ge(table_steps, n)
                    n = tstep(dve.tensor_scalar(rot_tmp[:, a], cos_t[:, a], s1, None, ALU.mult))
                    dve.wait_ge(table_steps, n)
                    n = tstep(dve.scalar_tensor_tensor(out=sin_t[:, b], in0=sin_t[:, a], scalar=c1,
                                                       in1=rot_tmp[:, a], op0=ALU.mult, op1=ALU.add))
                    dve.wait_ge(table_steps, n)
                    if 2 * size < S:
                        double(level + 1, s1, c1)
                    size, level = 2 * size, level + 1
                for c in range(NC):
                    cols = slice(CH * c, CH * (c + 1))
                    dve.wait_ge(filled, nth["w", c][0] + 1)
                    dve.tensor_tensor(rot_x[:, cols], bank("u", c), cos_t[:, cols], ALU.mult).then_inc(dve_drained, 1)
                    dve.tensor_tensor(rot_tmp[:, 0:CH], bank("w", c), sin_t[:, cols], ALU.mult).then_inc(dve_drained, 1)
                    dve.wait_ge(dve_drained, nth["w", c][1])
                    dve.tensor_tensor(rot_x[:, cols], rot_x[:, cols], rot_tmp[:, 0:CH], ALU.add).then_inc(rot_done, 1)
                    dve.wait_ge(rot_done, c + 1)
                dve.tensor_tensor_scan(state, r_col[:, 0:1].broadcast_to([P, S]), rot_x, 0.0, ALU.mult, ALU.add)\
                   .then_inc(scan_done, 1)
                dve.wait_ge(gexp_done, 1)
                gstep(dve.tensor_reduce(gsum[:, :], gates[:, :, :], AX.X, ALU.add))
                gstep(dve.reciprocal(gmax[:, :], gsum[:, :]))
                gstep(dve.tensor_tensor(gates[:, :, :], gates[:, :, :], gmax[:, :].unsqueeze(2).broadcast_to([P, NT, NE]),
                                        ALU.mult))
                mine = gates[:, :, :].unsqueeze(3).broadcast_to([P, NT, NE, NE])
                other = gates[:, :, :].unsqueeze(2).broadcast_to([P, NT, NE, NE])
                gstep(dve.tensor_tensor(beats[:, :, :, :], other, mine, ALU.is_gt))
                gstep(dve.tensor_tensor(ties[:, :, :, :], other, mine, ALU.is_equal))
                gstep(dve.tensor_tensor(ties[:, :, :, :].rearrange("p t e j -> p t (e j)"),
                                        ties[:, :, :, :].rearrange("p t e j -> p t (e j)"),
                                        lower[:, :, :].rearrange("p e j -> p (e j)").unsqueeze(1).broadcast_to([P, NT, NE * NE]),
                                        ALU.mult))
                gstep(dve.tensor_tensor(beats[:, :, :, :], beats[:, :, :, :], ties[:, :, :, :], ALU.add))
                gstep(dve.tensor_reduce(logits[:, :, :], beats[:, :, :, :], AX.X, ALU.add))
                dve.scalar_tensor_tensor(out=gates[:, :, :], in0=logits[:, :, :], scalar=2.0, in1=gates[:, :, :],
                                         op0=ALU.is_lt, op1=ALU.mult).then_inc(comb_done, 1)
                dve.wait_ge(comb_done, 1)
                ms = 0
                for n in range(2 * NT):
                    t = n // 2
                    dve.wait_ge(act_drained, nth["bias", t // TPC][1])
                    dve.wait_ge(filled, nth["experts", n][0] + 1)
                    for k in range(NE // 2):
                        e = NE // 2 * (n % 2) + k
                        if ms:
                            dve.wait_ge(moe_steps, ms)
                        ins = dve.scalar_tensor_tensor(
                            out=gate_sb[:, t, :], in0=bank("experts", n)[:, P * k:P * (k + 1)],
                            scalar=gates[:, t, e:e + 1], in1=gate_sb[:, t, :], op0=ALU.mult, op1=ALU.add)
                        if k == NE // 2 - 1:
                            ins.then_inc(dve_drained, 1)
                            dve.wait_ge(dve_drained, nth["experts", n][1])
                        else:
                            ins.then_inc(moe_steps, 1)
                            ms += 1

        NMAX = 2 * 2 * TPC * NC
        NEXP = 2 * NT
        MAX_STEPS = NT - 2
        scores_ready = sem("scores_ready")
        probs_ready = sem("probs_ready")
        probs_used = sem("probs_used")
        ring_filled = sem("ring_filled")
        ring_drained = sem("ring_drained")
        mops_loaded = [sem("mops_loaded0"), sem("mops_loaded1")]
        eops_loaded = [sem("eops_loaded0"), sem("eops_loaded1")]
        rows_set = sem("rows_set")
        v_staged = sem("v_staged")
        max_joined = sem("max_joined")
        max_hi = sem("max_hi")
        out_drained = sem("out_drained")
        out_rden = sem("out_rden")

        exp_ps = [ps[:, 2 * t:2 * t + 2, :] for t in range(2)]
        av_ps = ps[:, 4, :]
        ring_ps = [ps[:, 5 + n, :] for n in range(3)]
        MCOLS = 2 * 2 * TPC

        def max_range(s):
            return range(NMAX * s // MAX_STEPS, NMAX * (s + 1) // MAX_STEPS) if s < MAX_STEPS else range(0)

        OUT_STEP = 2
        OUT_JOB = max_range(OUT_STEP).stop
        JOBS = NMAX + 2
        assert JOBS % len(ring_ps) == 0

        def max_job(m):
            return m + (m >= OUT_JOB)

        def ring(j):
            return ring_ps[j % len(ring_ps)]

        def max_tile(m):
            return m % 2, m // 2 % 2, m // (4 * NC), m // 4 % NC

        def for_blocks(eng, body):
            body(0, 0, 0)
            with eng.Fori(0, (NB - 2) // 2) as i:
                body(2 * i + 1, 1, i)
                body(2 * i + 2, 0, i + 1)
            body(NB - 1, 1, NB // 2 - 1)

        def static(b):
            return isinstance(b, int)

        with nc.Block() as block:
            @block.sync
            def _(sp):
                q_src = q_parts.rearrange("r (a x d) (c n) -> a x r d c n", x=G0, d=HD0, n=CH)
                k_src = k_parts.rearrange("r (a x d) n -> a x r d n", x=G0, d=HD0)

                def load(q_to, k_to, b, loaded):
                    b = b % NB if static(b) else b
                    for g in range(2):
                        rows = slice(64 * g, 64 * g + KR)
                        for t in range(2):
                            sp.dma_start(q_to[rows, g, t, :], q_src[ds(b % NG0, 1), 2 * t + g, :, :, ds(b // NG0 % NC, 1), :])\
                              .then_inc(loaded, 16)
                            sp.dma_start(k_to[rows, t, :], k_src[ds(b % NG0, 1), 2 * t + g, :, :, :]).then_inc(loaded, 16)

                def load_max_rows(par):
                    for g in range(2):
                        for a in range(2):
                            row = 64 * g + KR + a
                            sp.dma_start(qexp[par][row:row + 1, g, :, :].rearrange("p t (s q) -> p (t s) q", q=P),
                                         max_rows[2 * TPC * g:2 * TPC * (g + 1), a, :])\
                              .then_inc(eops_loaded[par], 16)

                def body(b, par, k):
                    if not static(b) or b < NB - 1:
                        sp.wait_ge(ring_filled, JOBS * (b + 1))
                        load(qmax[par], kmax[par], b + 2, mops_loaded[par])
                        if not static(b) or b > 0:
                            sp.wait_ge(scores_ready, NEXP * b)
                        load(qexp[1 - par], kexp[1 - par], b + 1, eops_loaded[1 - par])
                        sp.wait_ge(ring_drained, JOBS * (b + 2))
                        load_max_rows(1 - par)

                sp.wait_ge(rows_set, 4)
                load(qmax[0], kmax[0], 0, mops_loaded[0])
                sp.wait_ge(rows_set, 8)
                load(qmax[1], kmax[1], 1, mops_loaded[1])
                load(qexp[0], kexp[0], 0, eops_loaded[0])
                sp.wait_ge(ring_drained, JOBS)
                load_max_rows(0)
                for_blocks(sp, body)
                sp.wait_ge(mops_loaded[0], 128 * (NB // 2 + 1))
                sp.wait_ge(mops_loaded[1], 128 * (NB // 2))

            @block.gpsimd
            def _(pool):
                for n in range(2):
                    pool.memset(qmax[n], 0.0).then_inc(rows_set, 1)
                    pool.memset(kmax[n], 1.0).then_inc(rows_set, 1)
                    pool.memset(qexp[n], 0.0).then_inc(rows_set, 1)
                    pool.memset(kexp[n], 1.0).then_inc(rows_set, 1)
                for n in range(2):
                    pool.memset(vst[n], 0.0).then_inc(rows_set, 1)
                pool.wait_ge(rows_set, 10)
                for n in range(2):
                    pool.memset(vst[n][:, :, :, HD0:HD0 + 1], 1.0).then_inc(rows_set, 1)

                def stage(b, par):
                    pool.tensor_copy(vst[par][:, :, :, 0:HD0],
                                     v_sb[:, :, ds(G0 * HD0 * (b % NG0), G0 * HD0)].rearrange("p t (j d) -> p t j d", d=HD0))\
                        .then_inc(v_staged, 1)

                def body(b, par, k):
                    if not static(b) or b < NB - 1:
                        if not static(b) or b > 0:
                            pool.wait_ge(probs_used, NT * b)
                        stage(b + 1, 1 - par)

                stage(0, 0)
                for_blocks(pool, body)

            @block.tensor
            def _(pe):
                def ring_free(b, j):
                    if not static(b) or b > 0 or j >= len(ring_ps):
                        pe.wait_ge(ring_drained, JOBS * b + j - len(ring_ps) + 1)

                def max_scores(b, par, ms):
                    for m in ms:
                        g, t, qs, kc = max_tile(m)
                        ring_free(b, max_job(m))
                        pe.matmul(ring(max_job(m)), qmax[par][:, g, t, P * qs:P * (qs + 1)],
                                  kmax[par][:, t, CH * kc:CH * (kc + 1)], start=True, stop=True)\
                          .then_inc(ring_filled, 1)

                def turn_max(b):
                    pe.wait_ge(max_joined, b + 1)
                    ring_free(b, JOBS - 1)
                    pe.transpose(ring(JOBS - 1)[0:MCOLS, 0:P], neg_max[:, :], ident[:, :]).then_inc(ring_filled, 1)

                def scores_T(b, par, s, t):
                    if not static(b) or b > 0 or s > 0:
                        pe.wait_ge(probs_ready, NEXP * b + 2 * s + t - 1)
                    for g in range(2):
                        mm = pe.matmul(exp_ps[t][:, g, :], kexp[par][:, t, P * s:P * (s + 1)],
                                       qexp[par][:, g, t, :], start=True, stop=True)
                    mm.then_inc(scores_ready, 1)

                def values(b, par, s):
                    pe.wait_ge(probs_ready, NEXP * b + 2 * s + 2)
                    if s == 0:
                        pe.wait_ge(v_staged, b + 1)
                        if not static(b) or b > 0:
                            pe.wait_ge(out_drained, b)
                    for j in range(G0):
                        t, g = j // 2, j % 2
                        mm = pe.matmul(av_ps[32 * j:32 * (j + 1), :], vst[par][:, s, j, :],
                                       probs[2 * (s % 2) + t][:, g, :], start=(s == 0), stop=(s == NT - 1))
                    mm.then_inc(probs_used, 1)

                def turn_out(b, par, jb, j):
                    pe.wait_ge(out_drained, b + 1)
                    ring_free(jb, j)
                    for qs in range(TPC):
                        mm = pe.transpose(ring(j)[:, P * qs:P * (qs + 1)], outT0[par][:, P * qs:P * (qs + 1)],
                                          ident[:, :])
                    mm.then_inc(ring_filled, 1)

                def empty_job(b):
                    pe.wait_ge(ring_drained, JOBS * b + OUT_JOB)
                    pe.sem_inc(ring_filled, 1)

                def body(b, par, k):
                    more = not static(b) or b < NB - 1
                    later = not static(b) or b > 0
                    if more:
                        pe.wait_ge(mops_loaded[1 - par], 8 * 16 * ((k if par == 0 else k + 1) + 1))
                    for s in range(NT):
                        ms = max_range(s) if more else range(0)
                        if s == 0:
                            if later:
                                values(b - 1, 1 - par, NT - 1)
                            max_scores(b + 1, 1 - par, ms)
                            pe.wait_ge(eops_loaded[par], 12 * 16 * (k + 1))
                            scores_T(b, par, s, 0)
                            scores_T(b, par, s, 1)
                            continue
                        max_scores(b + 1, 1 - par, ms[0:1])
                        scores_T(b, par, s, 0)
                        max_scores(b + 1, 1 - par, ms[1:2])
                        scores_T(b, par, s, 1)
                        max_scores(b + 1, 1 - par, ms[2:3])
                        values(b, par, s - 1)
                        max_scores(b + 1, 1 - par, ms[3:])
                        if s == OUT_STEP:
                            if more and later:
                                turn_out(b - 1, 1 - par, b + 1, OUT_JOB)
                            elif more:
                                empty_job(b + 1)
                            else:
                                turn_out(b - 1, 1 - par, NB, 0)
                        if s == MAX_STEPS and more:
                            turn_max(b + 1)

                pe.wait_ge(mops_loaded[0], 8 * 16)
                max_scores(0, 0, range(OUT_JOB))
                empty_job(0)
                max_scores(0, 0, range(OUT_JOB, NMAX))
                turn_max(0)
                for_blocks(pe, body)
                values(NB - 1, 1, NT - 1)
                turn_out(NB - 1, 1, NB, 1)

            @block.scalar
            def _(act):
                def drain_out(b, par):
                    act.wait_ge(probs_used, NT * (b + 1))
                    act.activation(outT0[par], av_ps, ACT.Copy).then_inc(out_drained, 1)

                def body(b, par, k):
                    later = not static(b) or b > 0
                    if later:
                        drain_out(b - 1, 1 - par)
                    for s in range(NT):
                        for t in range(2):
                            act.wait_ge(scores_ready, NEXP * b + 2 * s + t + 1)
                            if s >= 2:
                                act.wait_ge(probs_used, NT * b + s - 1)
                            act.activation(probs[2 * (s % 2) + t], exp_ps[t], ACT.Exp, scale=SC0)\
                               .then_inc(probs_ready, 1)

                for_blocks(act, body)
                drain_out(NB - 1, 1)

            @block.vector
            def _(dve):
                def reduce_tiles(b, ms):
                    for m in ms:
                        g, t, qs, kc = max_tile(m)
                        dve.wait_ge(ring_filled, JOBS * b + max_job(m) + 1)
                        col = (2 * g + t) * TPC + qs
                        dve.tensor_reduce(tile_max[:, col, kc:kc + 1], ring(max_job(m)), AX.X, ALU.max)\
                           .then_inc(ring_drained, 1)

                def join_max(b):
                    dve.wait_ge(ring_drained, JOBS * (b + 1) - 1)
                    dve.tensor_reduce(neg_max[:, :], tile_max[:, :, :], AX.X, ALU.max, negate=True)\
                       .then_inc(max_joined, 1)

                def split_max(b):
                    turned = ring(JOBS - 1)[0:MCOLS, 0:P]
                    dve.wait_ge(ring_filled, JOBS * (b + 1))
                    dve.tensor_copy(max_rows[:, 0, :], turned).then_inc(max_hi, 1)
                    dve.wait_ge(max_hi, b + 1)
                    dve.tensor_tensor(max_rows[:, 1, :], turned, max_rows[:, 0, :], ALU.subtract)\
                       .then_inc(ring_drained, 1)

                def norm_out(b, jb, j):
                    dve.wait_ge(ring_drained, JOBS * jb + j)
                    dve.wait_ge(ring_filled, JOBS * jb + j + 1)
                    sums = ring(j).rearrange("p (a j d) -> p (a j) d", j=G0, d=32)
                    dve.reciprocal(rden0[:, :], sums[:, :, HD0]).then_inc(out_rden, 1)
                    dve.wait_ge(out_rden, b + 1)
                    dve.tensor_tensor(
                        attn_sb[:, ds(b // NG0 * TPC, TPC), ds(b % NG0 * (G0 * HD0), G0 * HD0)]
                        .rearrange("p a (j d) -> p a j d", d=HD0),
                        ring(j).rearrange("p (a j d) -> p a j d", j=G0, d=32)[:, :, :, 0:HD0],
                        rden0[:, :].rearrange("p (a j) -> p a j", j=G0).unsqueeze(3).broadcast_to([P, TPC, G0, HD0]),
                        ALU.mult).then_inc(ring_drained, 1)

                def empty_job(b):
                    dve.wait_ge(ring_filled, JOBS * b + OUT_JOB + 1)
                    dve.sem_inc(ring_drained, 1)

                def body(b, par, k):
                    if static(b) and b == NB - 1:
                        norm_out(b - 1, NB, 0)
                        return
                    reduce_tiles(b + 1, range(OUT_JOB))
                    if static(b):
                        empty_job(b + 1)
                    else:
                        norm_out(b - 1, b + 1, OUT_JOB)
                    reduce_tiles(b + 1, range(OUT_JOB, NMAX))
                    join_max(b + 1)
                    split_max(b + 1)

                reduce_tiles(0, range(OUT_JOB))
                empty_job(0)
                reduce_tiles(0, range(OUT_JOB, NMAX))
                join_max(0)
                split_max(0)
                for_blocks(dve, body)
                norm_out(NB - 1, NB, 1)

        z_sum = sem("z_sum")
        z_exp = sem("z_exp")
        gate0_steps = sem("gate0_steps")
        x1_done = sem("x1_done")
        stats1_done = sem("stats1_done")
        std1_done = sem("std1_done")
        xn1_done = sem("xn1_done")
        turned1 = sem("turned1")
        xT1_done = sem("xT1_done")
        pads_made = sem("pads_made")
        hid_ready = sem("hid_ready")
        hid_done = sem("hid_done")
        mlp_ready = sem("mlp_ready")
        mlp_exp = sem("mlp_exp")
        mlp_done = sem("mlp_done")
        mlp_steps = sem("mlp_steps")
        xn1 = cut(8 * S, S).rearrange("p (t d) -> p t d", d=D)
        ez = cut(11 * S, S)
        gz = cut(12 * S, S)

        def flat(a):
            return a[:, :, :].rearrange("p t d -> p (t d)")

        with nc.Block() as block:
            @block.vector
            def _(dve):
                def chunk(a, c):
                    return a[:, CH * c:CH * (c + 1)]
                z, y, g, xf = flat(attn_sb), flat(y_sb), flat(gate_sb), flat(x_sb)
                for c in range(NC):
                    dve.tensor_tensor(chunk(z, c), chunk(z, c), chunk(g, c), ALU.add).then_inc(z_sum, 1)
                n = 0
                for c in range(NC):
                    dve.wait_ge(z_exp, c + 1)
                    for m, ins in enumerate((
                        lambda: dve.tensor_scalar(chunk(ez, c), chunk(ez, c), 1.0, None, ALU.add),
                        lambda: dve.reciprocal(chunk(ez, c), chunk(ez, c)),
                        lambda: dve.tensor_tensor(chunk(gz, c), chunk(z, c), chunk(y, c), ALU.mult),
                        lambda: dve.tensor_tensor(chunk(gz, c), chunk(gz, c), chunk(ez, c), ALU.mult),
                    )):
                        ins().then_inc(gate0_steps, 1)
                        n += 1
                        dve.wait_ge(gate0_steps, n)
                    dve.tensor_tensor(chunk(xf, c), chunk(xf, c), chunk(gz, c), ALU.add).then_inc(x1_done, 1)
                    dve.wait_ge(x1_done, c + 1)
                    for t in range(TPC * c, TPC * (c + 1)):
                        dve.bn_stats(stats[:, t, :], x_sb[:, t, :]).then_inc(stats1_done, 1)
                dve.wait_ge(stats1_done, NT)
                for t in range(NT):
                    dve.bn_aggr(mv[:, t, :], stats[:, t, :]).then_inc(stats1_done, 1)
                dve.wait_ge(stats1_done, 2 * NT)
                dve.tensor_scalar(var_eps[:, :], mv[:, :, 1], EPS, None, ALU.add).then_inc(stats1_done, 1)
                dve.wait_ge(std1_done, 1)
                dve.reciprocal(rstd[:, :], std[:, :]).then_inc(stats1_done, 1)
                dve.wait_ge(stats1_done, 2 * NT + 2)
                for t in range(NT):
                    dve.tensor_scalar(xn1[:, t, :], x_sb[:, t, :], mv[:, t, 0:1], rstd[:, t:t + 1],
                                      ALU.subtract, ALU.mult).then_inc(xn1_done, 1)
                n = 0
                for c in range(NC):
                    dve.wait_ge(mlp_exp, c + 1)
                    dve.tensor_scalar(chunk(ez, c), chunk(ez, c), 1.0, None, ALU.add).then_inc(mlp_steps, 1)
                    dve.wait_ge(mlp_steps, 2 * c + 1)
                    dve.reciprocal(chunk(ez, c), chunk(ez, c)).then_inc(mlp_steps, 1)
                    dve.wait_ge(mlp_steps, 2 * c + 2)
                    dve.tensor_tensor(chunk(g, c), ps[:, c, :], chunk(ez, c), ALU.mult).then_inc(mlp_done, 1)

            @block.scalar
            def _(act):
                z = flat(attn_sb)
                for c in range(NC):
                    act.wait_ge(z_sum, c + 1)
                    act.activation(ez[:, CH * c:CH * (c + 1)], z[:, CH * c:CH * (c + 1)], ACT.Exp, scale=-1.0)\
                       .then_inc(z_exp, 1)
                act.wait_ge(stats1_done, 2 * NT + 1)
                act.activation(std[:, :], var_eps[:, :], ACT.Sqrt).then_inc(std1_done, 1)
                for c in range(NC):
                    act.wait_ge(turned1, c + 1)
                    act.activation(xT[:, CH * c:CH * (c + 1)], ps[:, c, :], ACT.Copy).then_inc(xT1_done, 1)
                for n in range(NI * NC):
                    i, c = n % NI, n // NI
                    act.wait_ge(hid_ready, n + 1)
                    act.activation(hT[:, i, CH * c:CH * (c + 1)], ps[:, 4 + n % 4, :], ACT.Relu,
                                   bias=b1_sb[:, i:i + 1]).then_inc(hid_done, 1)
                for c in range(NC):
                    act.wait_ge(mlp_ready, c + 1)
                    act.activation(ez[:, CH * c:CH * (c + 1)], ps[:, c, :], ACT.Exp, scale=-1.0).then_inc(mlp_exp, 1)

            @block.gpsimd
            def _(pool):
                pool.memset(k_pad[64:P, 0, :], 0.0).then_inc(pads_made, 1)
                pool.wait_ge(pads_made, 1)
                pool.memset(k_pad[0:64, 1, :], 0.0).then_inc(pads_made, 1)
                pool.wait_ge(pads_made, 2)
                pool.tensor_copy(wst[:, :, :], w1qkv_sb[:, :, 0:P]).then_inc(pads_made, 1)

            @block.tensor
            def _(pe):
                for c in range(NC):
                    for t in range(TPC):
                        pe.wait_ge(xn1_done, TPC * c + t + 1)
                        mm = pe.transpose(ps[:, c, P * t:P * (t + 1)], xn1[:, TPC * c + t, :], ident[:, :])
                    mm.then_inc(turned1, 1)
                for n in range(NI * NC):
                    i, c = n % NI, n // NI
                    pe.wait_ge(xT1_done, c + 1)
                    if n >= 4:
                        pe.wait_ge(hid_done, n - 3)
                    pe.matmul(ps[:, 4 + n % 4, :], W1_sb[:, i:NI * P:NI], xT[:, CH * c:CH * (c + 1)],
                              start=True, stop=True).then_inc(hid_ready, 1)
                for c in range(NC):
                    pe.wait_ge(hid_done, NI * (c + 1))
                    for t in range(TPC):
                        cols = slice(P * t, P * (t + 1))
                        for i in range(NI):
                            pe.matmul(ps[:, c, cols], hT[:, i, CH * c + P * t:CH * c + P * (t + 1)], W2_sb[:, i, :],
                                      start=(i == 0), stop=False)
                        mm = pe.matmul(ps[:, c, cols], ones_row[:, :], b2_sb[:, :], start=False, stop=True)
                    mm.then_inc(mlp_ready, 1)

        wqk_staged = sem("wqk_staged")
        wv_staged = sem("wv_staged")
        qk_filled = sem("qk_filled")
        q_drained = sem("q_drained")
        k_drained = sem("k_drained")
        v_filled = sem("v_filled")
        v_drained = sem("v_drained")
        v2_copied = sem("v2_copied")
        s_filled = sem("s_filled")
        s_masked = sem("s_masked")
        mask_turns = sem("mask_turns")
        exped = sem("exped")
        recips = sem("recips")
        normed = sem("normed")
        pT_filled = sem("pT_filled")
        pT_drained = sem("pT_drained")
        av_done = sem("av_done")
        av_drained = sem("av_drained")
        T_LAG, AV_LAG, OUT_LAG = 3, 4, 5
        VJ = NC + 1

        def width(qb):
            return KW if qb else P

        def for_pairs(eng, body):
            with eng.Fori(0, NP1 - 1) as hp:
                body(hp, True)
            body(NP1 - 1, False)

        with nc.Block() as block:
            @block.gpsimd
            def _(pool):
                def body(hp, more):
                    if more:
                        pool.wait_ge(qk_filled, 2 * NC * (hp + 1))
                        pool.tensor_copy(wst[:, 0:2, :], w1qkv_sb[:, 0:2, ds(P * (hp + 1), P)]).then_inc(wqk_staged, 1)
                        pool.wait_ge(v_filled, VJ * (hp + 1))
                        pool.tensor_copy(wst[:, 2:3, :], w1qkv_sb[:, 2:3, ds(P * (hp + 1), P)]).then_inc(wv_staged, 1)
                    for qb in range(NT):
                        pool.wait_ge(recips, NT * hp + qb + 1)
                        p = p1[:, qb % NSLOT, :, 0:width(qb)]
                        pool.tensor_tensor(p, p, rinv1[:, qb % NSLOT, :].unsqueeze(2).broadcast_to([P, 2, width(qb)]),
                                           ALU.mult).then_inc(normed, 1)

                for_pairs(pool, body)

            @block.sync
            def _(sp):
                def body(hp, more):
                    sp.wait_ge(v_drained, VJ * hp + 1)
                    sp.dma_start(v2[HALF:TAIL, :, :], v1[0:GLOB, 0:1, :].broadcast_to([GLOB, NT - 1, P]))\
                      .then_inc(v2_copied, 16)
                    sp.wait_ge(v_drained, VJ * (hp + 1))
                    sp.dma_start(v2[0:HALF, :, :], v1[0:HALF, 2:NT + 1, :]).then_inc(v2_copied, 16)

                for_pairs(sp, body)

            @block.tensor
            def _(pe):
                def project_qk(n):
                    c, which = n // 2, n % 2
                    pe.matmul(ps[:, n % 4, :], wst[:, which, :], xT[:, CH * c:CH * (c + 1)],
                              start=True, stop=True).then_inc(qk_filled, 1)

                def project_v(hp, n):
                    if n == 0:
                        pe.wait_ge(wv_staged, hp + 1)
                    if n >= 2:
                        pe.wait_ge(v_drained, VJ * hp + n - 1)
                    if n == NC:
                        mm = pe.matmul(ps[0:HALF, 4 + n % 2, 0:P], xT[:, S - HALF:S], wst[:, 2, :], start=True, stop=True)
                    else:
                        for t in range(TPC * n, TPC * (n + 1)):
                            first = P * t - HALF if t else 0
                            mm = pe.matmul(ps[:, 4 + n % 2, P * (t % TPC):P * (t % TPC + 1)], xT[:, first:first + P],
                                           wst[:, 2, :], start=True, stop=True)
                    mm.then_inc(v_filled, 1)

                def scores(hp, qb):
                    if qb >= 4:
                        pe.wait_ge(s_masked, 2 * NT * hp + 2 * (qb - 3))
                    to = ps[:, qb % 4, 0:2 * KW].rearrange("p (g n) -> p g n", g=2)
                    q = qT[:, P * qb:P * (qb + 1)]
                    first, wide = (P * qb - HALF, WIN) if qb else (0, P)
                    mm = pe.matmul(to[:, :, 0:wide], q, k_pad[:, :, first:first + wide], start=True, stop=True)
                    if qb:
                        mm = pe.matmul(to[:, :, WIN:KW], q, k_pad[:, :, 0:GLOB], start=True, stop=True)
                    mm.then_inc(s_filled, 1)

                def turn(hp, qb):
                    pe.wait_ge(normed, NT * hp + qb + 1)
                    if qb >= 2:
                        pe.wait_ge(pT_drained, NT * hp + qb - 1)
                    elif qb == 0:
                        pe.wait_ge(v_drained, VJ * (hp + 1))
                    to = ps[:, 4 + qb % 2, :]
                    for g in range(2):
                        mm = pe.transpose(to[:, P * g:P * (g + 1)], p1[:, qb % NSLOT, g, 0:P], ident[:, :])
                    if qb:
                        for g in range(2):
                            mm = pe.transpose(to[0:TAIL, P * (2 + g):P * (3 + g)],
                                              p1[:, qb % NSLOT, g, P:KW], ident[:, :])
                    mm.then_inc(pT_filled, 1)

                def values(hp, qb):
                    pe.wait_ge(pT_drained, NT * hp + qb + 1)
                    if qb == 1:
                        pe.wait_ge(v2_copied, 32 * (hp + 1))
                    if qb % TPC == 0:
                        pe.wait_ge(av_drained, NC * hp + qb // TPC)
                    to = ps[:, 6 + qb // TPC % 2, P * (qb % TPC):P * (qb % TPC + 1)]
                    for g in range(2):
                        mm = pe.matmul(to[64 * g:64 * (g + 1), :], v1[:, qb, 64 * g:64 * (g + 1)],
                                       pT[:, qb % 4, P * g:P * (g + 1)], start=True, stop=(qb == 0))
                    if qb:
                        for g in range(2):
                            mm = pe.matmul(to[64 * g:64 * (g + 1), :], v2[0:TAIL, qb - 1, 64 * g:64 * (g + 1)],
                                           pT[0:TAIL, qb % 4, P * (2 + g):P * (3 + g)], start=False, stop=True)
                    mm.then_inc(av_done, 1)

                def body(hp, more):
                    for n in range(VJ):
                        project_v(hp, n)
                    pe.wait_ge(q_drained, NC * (hp + 1))
                    pe.wait_ge(k_drained, NC * (hp + 1))
                    for step in range(NT + AV_LAG):
                        if step < NT:
                            scores(hp, step)
                        if 0 <= step - T_LAG < NT:
                            turn(hp, step - T_LAG)
                        if step - AV_LAG >= 0:
                            values(hp, step - AV_LAG)
                        if step >= NT and more:
                            if step == NT:
                                pe.wait_ge(wqk_staged, hp + 1)
                            for n in range(2 * (step - NT), 2 * (step - NT) + 2):
                                if n < 4:
                                    pe.wait_ge(s_masked, 2 * NT * hp + 2 * (NT - 4 + n + 1))
                                else:
                                    pe.wait_ge(k_drained if n % 2 else q_drained, NC * (hp + 1) + n // 2 - 1)
                                project_qk(n)
                    pe.wait_ge(pT_drained, NT * (hp + 1))

                assert AV_LAG == NC
                for n in range(2 * NC):
                    if n >= 4:
                        pe.wait_ge(k_drained if n % 2 else q_drained, n // 2 - 1)
                    project_qk(n)
                for_pairs(pe, body)

            @block.scalar
            def _(act):
                def drain_q(pair, c):
                    act.wait_ge(qk_filled, 2 * NC * pair + 2 * c + 1)
                    act.activation(qT[:, CH * c:CH * (c + 1)], ps[:, 2 * c % 4, :], ACT.Copy).then_inc(q_drained, 1)

                def body(hp, more):
                    for n in range(VJ):
                        act.wait_ge(v_filled, VJ * hp + n + 1)
                        if n == NC:
                            act.activation(v1[0:HALF, NT, :], ps[0:HALF, 4 + n % 2, 0:P], ACT.Copy).then_inc(v_drained, 1)
                        else:
                            act.activation(v1[:, TPC * n:TPC * (n + 1), :],
                                           ps[:, 4 + n % 2, :].rearrange("p (t d) -> p t d", d=P), ACT.Copy)\
                               .then_inc(v_drained, 1)
                    for step in range(NT + AV_LAG):
                        qb = step
                        if qb < NT:
                            for g in range(2):
                                act.wait_ge(s_masked, 2 * NT * hp + 2 * qb + g + 1)
                                p = p1[:, qb % NSLOT, g, 0:width(qb)]
                                act.activation(p, p, ACT.Exp, scale=-1.0, bias=nmax1[:, qb % NSLOT, g:g + 1],
                                               accum_out=rsum1[:, qb % NSLOT, g:g + 1]).then_inc(exped, 1)
                        qb = step - T_LAG
                        if 0 <= qb < NT:
                            act.wait_ge(pT_filled, NT * hp + qb + 1)
                            frm = ps[:, 4 + qb % 2, :]
                            ins = act.activation(pT[:, qb % 4, 0:2 * P], frm[:, 0:2 * P], ACT.Copy)
                            if qb:
                                ins = act.activation(pT[0:TAIL, qb % 4, 2 * P:4 * P], frm[0:TAIL, 2 * P:4 * P], ACT.Copy)
                            ins.then_inc(pT_drained, 1)
                        if step >= NT and more:
                            drain_q(hp + 1, step - NT)

                for c in range(NC):
                    drain_q(0, c)
                for_pairs(act, body)

            @block.vector
            def _(dve):
                def drain_k(pair, c):
                    dve.wait_ge(qk_filled, 2 * NC * pair + 2 * c + 2)
                    for g in range(2):
                        rows = slice(64 * g, 64 * (g + 1))
                        ins = dve.tensor_copy(k_pad[rows, g, CH * c:CH * (c + 1)], ps[rows, (2 * c + 1) % 4, :])
                    ins.then_inc(k_drained, 1)

                def body(hp, more):
                    for step in range(NT + OUT_LAG):
                        qb = step
                        if qb < NT:
                            dve.wait_ge(s_filled, NT * hp + qb + 1)
                            if qb >= NSLOT:
                                dve.wait_ge(pT_filled, NT * hp + qb - NSLOT + 1)
                            dve.sem_inc(mask_turns, 1)
                            for g in range(2):
                                dve.tensor_tensor_reduce(
                                    p1[:, qb % NSLOT, g, 0:width(qb)], ps[:, qb % 4, KW * g:KW * g + width(qb)],
                                    masks[:, :] if qb else mask0[:, :], -SC1, BIG, ALU.add, ALU.min,
                                    nmax1[:, qb % NSLOT, g:g + 1]).then_inc(s_masked, 1)
                        qb = step - 1
                        if 0 <= qb < NT:
                            dve.wait_ge(exped, 2 * NT * hp + 2 * (qb + 1))
                            dve.reciprocal(rinv1[:, qb % NSLOT, :], rsum1[:, qb % NSLOT, :]).then_inc(recips, 1)
                        if NT < step <= NT + NC and more:
                            drain_k(hp + 1, step - NT - 1)
                        qb = step - OUT_LAG
                        if qb >= 0 and qb % TPC == TPC - 1:
                            c = qb // TPC
                            dve.wait_ge(av_done, NT * hp + qb + 1)
                            dve.tensor_copy(outT1[:, ds(hp, 1), CH * c:CH * (c + 1)],
                                            ps[:, 6 + c % 2, :].unsqueeze(1)).then_inc(av_drained, 1)

                dve.sem_inc(av_drained, 1)
                dve.sem_inc(wv_staged, 1)
                for c in range(NC):
                    drain_k(0, c)
                for_pairs(dve, body)

        o_ready = sem("o_ready")
        o_gated = sem("o_gated")
        x2_done = sem("x2_done")
        stored = sem("stored")
        with nc.Block() as block:
            @block.tensor
            def _(pe):
                for c in range(NC):
                    for t in range(TPC):
                        for h in range(NP1):
                            mm = pe.matmul(ps[:, c, P * t:P * (t + 1)],
                                           outT1[:, h, CH * c + P * t:CH * c + P * (t + 1)], wout_sb[:, h, :],
                                           start=(h == 0), stop=(h == NP1 - 1))
                    mm.then_inc(o_ready, 1)

            @block.vector
            def _(dve):
                for c in range(NC):
                    cols = slice(CH * c, CH * (c + 1))
                    dve.wait_ge(o_ready, c + 1)
                    dve.tensor_tensor(tmp[:, c % 2, :], ps[:, c, :], flat(gate_sb)[:, cols], ALU.mult).then_inc(o_gated, 1)
                    dve.wait_ge(o_gated, c + 1)
                    dve.tensor_tensor(flat(x_sb)[:, cols], flat(x_sb)[:, cols], tmp[:, c % 2, :], ALU.add)\
                       .then_inc(x2_done, 1)

            @block.sync
            def _(sp):
                for c in range(NC):
                    sp.wait_ge(x2_done, c + 1)
                    sp.dma_start(out[0, CH * c:CH * (c + 1), :].rearrange("(t p) d -> p t d", p=P),
                                 x_sb[:, TPC * c:TPC * (c + 1), :]).then_inc(stored, 16)
                sp.wait_ge(stored, NC * 16)


_INS = ['L0_attn_x', 'L0_attn_theta_log', 'L0_attn_nu_log', 'L0_attn_gamma_log', 'L0_attn_B_re', 'L0_attn_B_im',
        'L0_attn_C_re', 'L0_attn_C_im', 'L0_attn_D', 'L0_ffn_W_qkv', 'L0_ffn_b_qkv', 'L0_ffn_W_gate',
        'L0_ffn_b_gate', 'L0_ffn_W_experts', 'L0_ffn_b_experts', 'L1_attn_w_qkv', 'L1_attn_w_out',
        'L1_ffn_W1', 'L1_ffn_b1', 'L1_ffn_W2', 'L1_ffn_b2']
_OUTS = [((1, 2048, 128), 'float32')]


def kernel(**inputs):
    import numpy as _np
    import concourse.bacc as _bacc
    from concourse import mybir as _mybir
    from concourse.bass_utils import run_bass_kernel_spmd as _run

    nc = _bacc.Bacc("TRN2", target_bir_lowering=False, num_devices=1)
    arrays, args = {}, []
    for name in _INS:
        a = _np.ascontiguousarray(inputs[name])
        arrays[f"in_{name}_dram"] = a
        args.append(nc.dram_tensor(f"in_{name}_dram", a.shape, _mybir.dt.from_np(a.dtype), kind="ExternalInput").ap())
    for i, (shape, dtype) in enumerate(_OUTS):
        dt = _mybir.dt.from_np(_np.dtype(dtype))
        args.append(nc.dram_tensor(f"out_{i}_dram", shape, dt, kind="ExternalOutput").ap())
    recurrent_moe_sparse_attention_kernel(nc, *args)
    r = _run(nc, [arrays], core_ids=[0])
    got = tuple(r.results[0][f"out_{i}_dram"] for i in range(len(_OUTS)))
    return got[0]
```

```python
import concourse.bass as bass
from concourse import mybir
from contextlib import ExitStack


def recurrent_moe_sparse_attention_kernel(
    nc, x, theta_log, nu_log, gamma_log, B_re, B_im, C_re, C_im, D_skip,
    W_qkv0, b_qkv0, W_gate, b_gate, W_experts, b_experts,
    W_qkv1, W_out1, W1, b1, W2, b2, out,
):
    fp32 = mybir.dt.float32
    bf16 = mybir.dt.bfloat16
    i32 = mybir.dt.int32
    ALU = mybir.AluOpType
    ACT = mybir.ActivationFunctionType
    AX = mybir.AxisListType
    ds = bass.ds

    P = 128
    S, D = x.shape[1], x.shape[2]
    NT = S // P
    CH = 512
    NC = S // CH
    TPC = CH // P
    EPS = 1e-5
    HID = theta_log.shape[0]
    NE = W_gate.shape[1]
    H0 = 16
    HD0 = D // H0
    G0 = 4
    NG0 = H0 // G0
    NB = NC * NG0
    SC0 = float(HD0) ** -0.5
    NPROD = 6
    KR = NPROD * HD0
    H1 = 16
    HD1 = W_out1.shape[0] // H1
    NP1 = H1 // 2
    SC1 = float(HD1) ** -0.5
    HALF = 16
    GLOB = 64
    WIN = P + HALF
    KW = WIN + GLOB
    TAIL = KW - P
    NI = W1.shape[1] // P
    NEG = -1.0e30
    BIG = 3.0e38
    ONES = 1.0 + 0x3F80 / 2.0 ** 23
    TWO_PI_HI = 6.28125
    TWO_PI_LO = 0.0019353071795864769
    PI_2 = 1.5707963267948966

    ctx = ExitStack()
    with ctx:
        def sb(name, shape, dt=fp32):
            return ctx.enter_context(nc.sbuf_tensor(name, shape, dt))

        def sem(name):
            return ctx.enter_context(nc.semaphore(name))

        x_sb = sb("x_sb", [P, NT, D])
        xT = sb("xT", [P, S])
        layer0 = sb("layer0", [P, 3, S])
        y_sb, attn_sb, v_sb = [layer0[:, n, :].rearrange("p (t d) -> p t d", d=D) for n in range(3)]
        gate_sb = sb("gate_sb", [P, NT, D])
        ident = sb("ident", [P, P])
        w1qkv_sb = sb("w1qkv_sb", [P, 3, H1 * HD1])
        wout_sb = sb("wout_sb", [P, NP1, D])
        W1_sb = sb("W1_sb", [P, NI * P])
        W2_sb = sb("W2_sb", [P, NI, D])
        b1_sb = sb("b1_sb", [P, NI])
        b2_all = sb("b2_all", [P, D])
        stats = sb("stats", [P, NT, 6])
        mv = sb("mv", [P, NT, 2])
        var_eps = sb("var_eps", [P, NT])
        std = sb("std", [P, NT])
        rstd = sb("rstd", [P, NT])
        masks = sb("masks", [P, KW])
        mask0 = sb("mask0", [P, P])

        ARENA = 13 * S + 64 * 2
        arena = sb("arena", [P, ARENA])

        def cut(at, words):
            assert at + words <= ARENA
            return arena[:, at:at + words]

        xn_sb = cut(0, S).rearrange("p (t d) -> p t d", d=D)
        cos_t, sin_t, rot_x, state = [cut(S * (n + 1), S) for n in range(4)]
        w_in = state
        st_cos, st_sin = cos_t, sin_t
        partsQ = cut(7 * S, 3 * S // 2).bitcast(bf16).rearrange("p (a n) -> p a n", a=3)
        partsK = cut(7 * S + 3 * S // 2, 3 * S // 2).bitcast(bf16).rearrange("p (a n) -> p a n", a=3)
        rest = cut(10 * S, 4 * CH).rearrange("p (a n) -> p a n", a=4)
        eo = cut(10 * S, 2 * NE * D).rearrange("p (s e d) -> p s e d", s=2, e=NE)
        probs = [cut(2 * CH * n, 2 * CH).rearrange("p (g n) -> p g n", g=2) for n in range(4)]
        outT0 = [cut(2 * S + CH * n, CH) for n in range(2)]
        ez = cut(3 * S, S)
        gz = cut(4 * S, S)
        q_places = cut(5 * S, 2 * S)
        qmax, qexp = [[cut(5 * S + 2 * CH * n + S * m, 2 * CH).bitcast(bf16)
                       .rearrange("p (g t n) -> p g t n", g=2, t=2) for n in range(2)] for m in range(2)]
        k_places = [cut(11 * S, 2 * S), cut(7 * S, 2 * S)]
        kmax, kexp = [[k_places[n][:, S * m:S * (m + 1)].bitcast(bf16).rearrange("p (t n) -> p t n", t=2)
                       for n in range(2)] for m in range(2)]
        v_places = cut(9 * S, 2 * S)
        vst = [v_places[:, S * n:S * (n + 1)].rearrange("p (t j d) -> p t j d", j=G0, d=32) for n in range(2)]
        outT1 = cut(0, NP1 * S).rearrange("p (h n) -> p h n", h=NP1)
        hT = cut(0, NI * S).rearrange("p (i n) -> p i n", i=NI)
        qT = cut(8 * S, S)
        k_pad = cut(9 * S, 2 * S).rearrange("p (g n) -> p g n", g=2)
        v1 = cut(11 * S, S + P).rearrange("p (t d) -> p t d", d=P)
        v2 = cut(12 * S + P, S - P).rearrange("p (t d) -> p t d", d=P)

        prm = sb("prm", [P, 3])
        eprm = sb("eprm", [P, 3])
        r_col = sb("r_col", [P, 1])
        ang = sb("ang", [P, 8])
        ang_i = sb("ang_i", [P, 1], i32)
        pw = sb("pw", [P, 12, 4])
        rot_tmp = sb("rot_tmp", [P, S // 2])
        B_sb = sb("B_sb", [P, 2, D])
        C_sb = sb("C_sb", [P, 2, 2 * HID])
        BT = sb("BT", [P, 2, P])
        CT = sb("CT", [P, 2, D])
        D_col = sb("D_col", [P, 1])
        D_diag = sb("D_diag", [P, P])
        w0_sb = sb("w0_sb", [P, 3, D])
        bqk_col = sb("bqk_col", [P, 2])
        bv_all = sb("bv_all", [P, D])
        wg_sb = sb("wg_sb", [P, NE])
        bg_all = sb("bg_all", [P, NE])
        we_sb = sb("we_sb", [P, NE, D])
        be_sb = sb("be_sb", [NE, D])
        logits = sb("logits", [P, NT, NE])
        gmax = sb("gmax", [P, NT])
        gsum = sb("gsum", [P, NT])
        gates = sb("gates", [P, NT, NE])
        beats = cut(0, NT * NE * NE).rearrange("p (t e j) -> p t e j", e=NE, j=NE)
        ties = cut(NT * NE * NE, NT * NE * NE).rearrange("p (t e j) -> p t e j", e=NE, j=NE)
        lower = sb("lower", [P, NE, NE])
        combT = sb("combT", [NE, S])
        tile_max = sb("tile_max", [P, 2 * TPC * 2, NC])
        neg_max = sb("neg_max", [P, 2 * TPC * 2])
        max_rows = sb("max_rows", [2 * TPC * 2, 2, P], bf16)
        rden0 = sb("rden0", [P, TPC * G0])
        wst = sb("wst", [P, 3, P])
        NSLOT = 8
        p1 = layer0[:, :, :].rearrange("p a n -> p (a n)")[:, 0:NSLOT * 2 * KW]\
            .rearrange("p (s g n) -> p s g n", g=2, n=KW)
        nmax1 = sb("nmax1", [P, NSLOT, 2])
        rsum1 = sb("rsum1", [P, NSLOT, 2])
        rinv1 = sb("rinv1", [P, NSLOT, 2])
        pT = layer0[:, 2, :].rearrange("p (s n) -> p s n", n=CH)
        tmp = rot_tmp[:, :].rearrange("p (s n) -> p s n", n=CH)

        ps = ctx.enter_context(nc.psum_tensor("ps", [P, 8, CH], fp32))

        q_parts = nc.dram_tensor("q_parts", [NPROD, P, S], bf16, kind="Internal").ap()
        k_parts = nc.dram_tensor("k_parts", [NPROD, P, S], bf16, kind="Internal").ap()
        Q_PART = [0, 0, 0, 1, 1, 2]
        K_PART = [0, 1, 2, 0, 1, 0]

        HT = NT // 2
        x_loaded = [sem("x_loaded0"), sem("x_loaded1")]
        prm_loaded = sem("prm_loaded")
        att_loaded = sem("att_loaded")
        gw_loaded = sem("gw_loaded")
        rec_loaded = sem("rec_loaded")
        moe_loaded = sem("moe_loaded")
        l1_loaded = sem("l1_loaded")
        consts_made = sem("consts_made")
        stats_done = sem("stats_done")
        std_done = sem("std_done")
        rstd_done = sem("rstd_done")
        xn_done = sem("xn_done")
        prm_done = sem("prm_done")
        angle_steps = sem("angle_steps")
        sin_done = sem("sin_done")
        filled = sem("filled")
        act_drained = sem("act_drained")
        dve_drained = sem("dve_drained")
        hi_done = sem("hi_done")
        rest_done = sem("rest_done")
        mid_done = sem("mid_done")
        parts_done = sem("parts_done")
        parts_stored = sem("parts_stored")
        table_steps = sem("table_steps")
        long_steps = sem("long_steps")
        rot_done = sem("rot_done")
        scan_done = sem("scan_done")
        back_done = sem("back_done")
        diag_done = sem("diag_done")
        gate_steps = sem("gate_steps")
        gexp_in = sem("gexp_in")
        gexp_done = sem("gexp_done")
        comb_done = sem("comb_done")
        moe_steps = sem("moe_steps")
        sum_steps = sem("sum_steps")
        mops_loaded = [sem("mops_loaded0"), sem("mops_loaded1")]
        eops_loaded = [sem("eops_loaded0"), sem("eops_loaded1")]
        rows_set = sem("rows_set")
        v_staged = sem("v_staged")

        q_src = q_parts.rearrange("r (a x d) (c n) -> a x r d c n", x=G0, d=HD0, n=CH)
        k_src = k_parts.rearrange("r (a x d) n -> a x r d n", x=G0, d=HD0)

        def load_operands(sp, q_to, k_to, b, loaded):
            b = b % NB if isinstance(b, int) else b
            for g in range(2):
                rows = slice(64 * g, 64 * g + KR)
                for t in range(2):
                    sp.dma_start(q_to[rows, g, t, :], q_src[ds(b % NG0, 1), 2 * t + g, :, :, ds(b // NG0 % NC, 1), :])\
                      .then_inc(loaded, 16)
                    sp.dma_start(k_to[rows, t, :], k_src[ds(b % NG0, 1), 2 * t + g, :, :, :]).then_inc(loaded, 16)

        def stage_values(pool, b, par):
            cols = ds(G0 * HD0 * (b % NG0), G0 * HD0)
            pool.tensor_tensor(vst[par][:, :, :, 0:HD0],
                               v_sb[:, :, cols].rearrange("p t (j d) -> p t j d", d=HD0),
                               bv_all[:, cols].rearrange("p (j d) -> p j d", d=HD0).unsqueeze(1)
                               .broadcast_to([P, NT, G0, HD0]), ALU.add).then_inc(v_staged, 1)

        QKV = [("q", 0), ("q", 1), ("v", 0), ("q", 2), ("q", 3), ("v", 1), ("k", 0), ("k", 1), ("k", 2), ("k", 3)]
        LATE_V = [2, 3]
        assert NC == 4
        jobs = [("xT", c, "act") for c in range(NC)]
        jobs += [(k, c, "act" if k == "v" else "dve") for k, c in QKV]
        jobs += [("BT", 0, "act"), ("CT", 0, "act")]
        jobs += [("logits", 0, "dve")]
        jobs += [(k, c, "act") for c in range(NC) for k in ("u", "w")]
        jobs += [("v", c, "act") for c in LATE_V]
        jobs += [("combT", c, "act") for c in range(NC)]
        jobs += [("bias", c, "act") for c in range(NC)]
        LEVELS = S.bit_length() - 1
        assert S == 1 << LEVELS
        POOL_LEVELS = LEVELS - 3
        POOL_STEPS = 4 * LEVELS + 6 * POOL_LEVELS + 2
        SCAN_AT = NT // 2
        HELPED = NT // 4
        OWN_JOBS = 2 * (NT - HELPED)
        EXPERTS = []
        for n in range(0, OWN_JOBS, 4):
            EXPERTS += [("experts", n + k) for k in range(4)]
            if n // 4 < HELPED:
                EXPERTS += [("helped", n // 2), ("helped", n // 2 + 1)]
        jobs += [(k, n, "dve" if k == "experts" else "act") for k, n in EXPERTS]
        nth = {}
        seen = {"act": 0, "dve": 0}
        for n, (kind, c, eng) in enumerate(jobs):
            seen[eng] += 1
            nth[kind, c] = (n, seen[eng])
        drained = {"act": act_drained, "dve": dve_drained}

        def expert_job(n):
            return 2 * (n // 4) + n % 2, n // 2 % 2

        def helped_job(n):
            return NT - HELPED + n // 2, n % 2

        def qk_part(m, part):
            return (partsQ, partsK)[m // NC][:, part, CH * (m % NC):CH * (m % NC + 1)]

        def bank(kind, c):
            return ps[:, nth[kind, c][0] % 8, :]

        def sum_helped(pool, i):
            pool.wait_ge(act_drained, nth["helped", 2 * i + 1][1])
            e, t = eo[:, i % 2, :, :], NT - HELPED + i
            for k, width in enumerate((4, 2, 1)):
                pool.tensor_tensor(e[:, 0:width, :], e[:, 0:width, :], e[:, width:2 * width, :], ALU.add)\
                    .then_inc(sum_steps, 1)
                pool.wait_ge(sum_steps, 4 * i + k + 1)
            pool.tensor_tensor(gate_sb[:, t, :], gate_sb[:, t, :], e[:, 0, :], ALU.add).then_inc(sum_steps, 1)

        with nc.Block() as block:
            @block.sync
            def _(sp):
                for h in range(2):
                    sp.dma_start(x_sb[:, HT * h:HT * (h + 1), :],
                                 x[0, HT * P * h:HT * P * (h + 1), :].rearrange("(t p) d -> p t d", p=P))\
                      .then_inc(x_loaded[h], 16)
                for h in range(2):
                    half = slice(HID * h, HID * (h + 1))
                    sp.dma_start(prm[half, 0:1], theta_log.rearrange("(p a) -> p a", a=1)).then_inc(prm_loaded, 16)
                    sp.dma_start(prm[half, 1:2], nu_log.rearrange("(p a) -> p a", a=1)).then_inc(prm_loaded, 16)
                    sp.dma_start(prm[half, 2:3], gamma_log.rearrange("(p a) -> p a", a=1)).then_inc(prm_loaded, 16)
                sp.dma_start(w0_sb[:, :, :], W_qkv0.rearrange("k (s n) -> k s n", s=3)).then_inc(att_loaded, 16)
                sp.dma_start(bqk_col[:, 0:1], b_qkv0[0:D].rearrange("(p a) -> p a", a=1)).then_inc(att_loaded, 16)
                sp.dma_start(bqk_col[:, 1:2], b_qkv0[D:2 * D].rearrange("(p a) -> p a", a=1)).then_inc(att_loaded, 16)
                sp.dma_start(bv_all[:, :], b_qkv0[2 * D:3 * D].rearrange("(a n) -> a n", a=1).broadcast_to([P, D]))\
                  .then_inc(att_loaded, 16)
                sp.dma_start(wg_sb[:, :], W_gate).then_inc(gw_loaded, 16)
                sp.dma_start(bg_all[:, :], b_gate.rearrange("(a n) -> a n", a=1).broadcast_to([P, NE]))\
                  .then_inc(gw_loaded, 16)
                for h in range(2):
                    half = slice(HID * h, HID * (h + 1))
                    sp.dma_start(B_sb[half, h, :], B_re).then_inc(rec_loaded, 16)
                    sp.dma_start(B_sb[half, 1 - h, :], B_im).then_inc(rec_loaded, 16)
                sp.dma_start(C_sb[:, 0, 0:HID], C_re).then_inc(rec_loaded, 16)
                sp.dma_start(C_sb[:, 0, HID:], C_im).then_inc(rec_loaded, 16)
                sp.dma_start(C_sb[:, 1, 0:HID], C_im).then_inc(rec_loaded, 16)
                sp.dma_start(C_sb[:, 1, HID:], C_re).then_inc(rec_loaded, 16)
                sp.dma_start(D_col[:, :], D_skip.rearrange("(p a) -> p a", a=1)).then_inc(rec_loaded, 16)
                sp.dma_start(we_sb[:, :, :], W_experts.rearrange("e d f -> d e f")).then_inc(moe_loaded, 16)
                sp.dma_start(be_sb[:, :], b_experts).then_inc(moe_loaded, 16)
                for n, (parts, order, dram) in enumerate(((partsQ, Q_PART, q_parts), (partsK, K_PART, k_parts))):
                    sp.wait_ge(parts_done, NC * (n + 1))
                    for r in range(NPROD):
                        sp.dma_start(dram[r], parts[:, order[r], :]).then_inc(parts_stored, 16)
                sp.wait_ge(parts_stored, 2 * NPROD * 16)
                sp.wait_ge(rows_set, 2)
                load_operands(sp, qmax[0], kmax[0], 0, mops_loaded[0])
                load_operands(sp, qexp[0], kexp[0], 0, eops_loaded[0])
                sp.dma_start(w1qkv_sb[:, :, :], W_qkv1.rearrange("k (s n) -> k s n", s=3)).then_inc(l1_loaded, 16)
                sp.dma_start(wout_sb[:, :, :], W_out1.rearrange("(h p) n -> p h n", p=P)).then_inc(l1_loaded, 16)
                sp.dma_start(W1_sb[:, :], W1).then_inc(l1_loaded, 16)
                sp.dma_start(W2_sb[:, :, :], W2.rearrange("(p i) n -> p i n", p=P)).then_inc(l1_loaded, 16)
                sp.dma_start(b1_sb[:, :], b1.rearrange("(p i) -> p i", p=P)).then_inc(l1_loaded, 16)
                sp.dma_start(b2_all[:, :], b2.rearrange("(a n) -> a n", a=1).broadcast_to([P, D])).then_inc(l1_loaded, 16)
                sp.wait_ge(l1_loaded, 6 * 16)

            @block.gpsimd
            def _(pool):
                pool.memset(ident[:, :], 0.0).then_inc(consts_made, 1)
                pool.memset(lower[:, :, :], 1.0).then_inc(consts_made, 1)
                pool.memset(masks[:, :], 0.0).then_inc(consts_made, 1)
                pool.memset(mask0[:, :], 0.0).then_inc(consts_made, 1)
                pool.wait_ge(consts_made, 4)
                pool.affine_select(out=ident[:, :], in_=ident[:, :], compare_op=ALU.not_equal, fill=1.0,
                                   base=0, pattern=[[-1, P]], channel_multiplier=1).then_inc(consts_made, 1)
                pool.affine_select(out=lower[:, :, :], in_=lower[:, :, :], compare_op=ALU.is_gt, fill=0.0,
                                   base=0, pattern=[[1, NE], [-1, NE]], channel_multiplier=0).then_inc(consts_made, 1)
                pool.affine_select(out=masks[:, 0:WIN], in_=masks[:, 0:WIN], compare_op=ALU.is_ge, fill=NEG,
                                   base=0, pattern=[[1, WIN]], channel_multiplier=-1).then_inc(consts_made, 1)
                pool.affine_select(out=mask0[:, GLOB:P], in_=mask0[:, GLOB:P], compare_op=ALU.is_ge, fill=NEG,
                                   base=HALF + GLOB, pattern=[[1, P - GLOB]], channel_multiplier=-1).then_inc(consts_made, 1)
                pool.memset(q_places, 0.0).then_inc(rows_set, 1)
                pool.wait_ge(consts_made, 8)
                pool.affine_select(out=masks[:, 0:WIN], in_=masks[:, 0:WIN], compare_op=ALU.is_ge, fill=NEG,
                                   base=HALF, pattern=[[-1, WIN]], channel_multiplier=1).then_inc(consts_made, 1)
                pool.affine_select(out=mask0[:, :], in_=mask0[:, :], compare_op=ALU.is_ge, fill=NEG,
                                   base=0, pattern=[[-1, P]], channel_multiplier=1).then_inc(consts_made, 1)
                pool.memset(k_places[0], ONES).then_inc(rows_set, 1)
                ts = 0
                def tstep(ins):
                    nonlocal ts
                    ts += 1
                    ins.then_inc(table_steps, 1)
                    return ts
                pool.wait_ge(sin_done, 1)
                sh, chh = ang[:, 4:5], ang[:, 5:6]

                def double(level, s, c):
                    tstep(pool.tensor_tensor(pw[:, level, 2:3], s, s, ALU.mult))
                    n = tstep(pool.tensor_tensor(pw[:, level, 3:4], s, c, ALU.mult))
                    pool.wait_ge(table_steps, n)
                    tstep(pool.tensor_scalar(pw[:, level, 0:1], pw[:, level, 2:3], -2.0, 1.0, ALU.mult, ALU.add))
                    n = tstep(pool.tensor_scalar(pw[:, level, 1:2], pw[:, level, 3:4], 2.0, None, ALU.mult))
                    pool.wait_ge(table_steps, n)

                double(0, sh, chh)
                tstep(pool.memset(cos_t[:, 0:1], 1.0))
                n = tstep(pool.memset(sin_t[:, 0:1], 0.0))
                pool.wait_ge(table_steps, n)
                for level in range(POOL_LEVELS):
                    size = 1 << level
                    c1, s1 = pw[:, level, 0:1], pw[:, level, 1:2]
                    a, b = slice(0, size), slice(size, 2 * size)
                    tstep(pool.tensor_scalar(rot_tmp[:, a], sin_t[:, a], s1, None, ALU.mult))
                    n = tstep(pool.tensor_scalar(cos_t[:, b], cos_t[:, a], c1, None, ALU.mult))
                    pool.wait_ge(table_steps, n)
                    n = tstep(pool.tensor_tensor(cos_t[:, b], cos_t[:, b], rot_tmp[:, a], ALU.subtract))
                    pool.wait_ge(table_steps, n)
                    tstep(pool.tensor_scalar(rot_tmp[:, a], cos_t[:, a], s1, None, ALU.mult))
                    n = tstep(pool.tensor_scalar(sin_t[:, b], sin_t[:, a], c1, None, ALU.mult))
                    pool.wait_ge(table_steps, n)
                    n = tstep(pool.tensor_tensor(sin_t[:, b], sin_t[:, b], rot_tmp[:, a], ALU.add))
                    pool.wait_ge(table_steps, n)
                    double(level + 1, s1, c1)
                for level in range(POOL_LEVELS + 1, LEVELS):
                    double(level, pw[:, level - 1, 1:2], pw[:, level - 1, 0:1])
                for c in range(NC):
                    cols = slice(CH * c, CH * (c + 1))
                    pool.wait_ge(act_drained, nth["w", c][1])
                    long = sum(CH * (c + 1) > 1 << n for n in range(POOL_LEVELS, LEVELS))
                    if long:
                        pool.wait_ge(long_steps, 4 * long)
                    pool.tensor_tensor(rot_x[:, cols], rot_x[:, cols], cos_t[:, cols], ALU.mult).then_inc(rot_done, 1)
                    pool.tensor_tensor(w_in[:, cols], w_in[:, cols], sin_t[:, cols], ALU.mult).then_inc(rot_done, 1)
                    pool.wait_ge(rot_done, 3 * c + 2)
                    pool.tensor_tensor(rot_x[:, cols], rot_x[:, cols], w_in[:, cols], ALU.add).then_inc(rot_done, 1)
                assert NE == 8
                for i in range(HELPED // 2):
                    sum_helped(pool, i)
                pool.wait_ge(scan_done, 1)
                pool.tensor_tensor(st_cos, state, cos_t, ALU.mult).then_inc(back_done, 1)
                pool.tensor_tensor(st_sin, state, sin_t, ALU.mult).then_inc(back_done, 1)
                for i in range(HELPED // 2, HELPED - 1):
                    sum_helped(pool, i)

            @block.scalar
            def _(act):
                act.wait_ge(prm_loaded, 6 * 16)
                act.activation(eprm[:, :], prm[:, :], ACT.Exp).then_inc(prm_done, 1)
                act.wait_ge(prm_done, 1)
                act.activation(r_col[:, :], eprm[:, 1:2], ACT.Exp, scale=-1.0).then_inc(prm_done, 1)
                for h in range(2):
                    half = slice(HT * h, HT * (h + 1))
                    act.wait_ge(stats_done, (2 * HT + 1) * (h + 1))
                    act.activation(std[:, half], var_eps[:, half], ACT.Sqrt).then_inc(std_done, 1)
                act.wait_ge(angle_steps, 7)
                act.activation(ang[:, 4:6], ang[:, 2:4], ACT.Sin).then_inc(sin_done, 1)

                def drain(kind, c, dst, **how):
                    n, k = nth[kind, c]
                    act.wait_ge(filled, n + 1)
                    act.activation(dst, how.pop("src", bank(kind, c)), how.pop("func", ACT.Copy), **how)\
                       .then_inc(act_drained, 1)

                for c in range(NC):
                    drain("xT", c, xT[:, CH * c:CH * (c + 1)])
                act.wait_ge(att_loaded, 4 * 16)

                def middle(m):
                    act.wait_ge(rest_done, m + 1)
                    act.activation(qk_part(m, 1), rest[:, m % 4, :], ACT.Copy).then_inc(mid_done, 1)

                def drain_v(c):
                    drain("v", c, v_sb[:, TPC * c:TPC * (c + 1), :], src=bank("v", c).rearrange("p (t d) -> p t d", d=D))

                for kind, c in QKV:
                    if kind == "v":
                        drain_v(c)
                        continue
                    n = 0 if kind == "q" else 1
                    m = NC * n + c
                    act.wait_ge(filled, nth[kind, c][0] + 1)
                    act.activation(qk_part(m, 0), bank(kind, c), ACT.Identity, bias=bqk_col[:, n:n + 1]).then_inc(hi_done, 1)
                    if m > 0:
                        middle(m - 1)
                middle(2 * NC - 1)
                drain("BT", 0, BT[:, :, :], src=bank("BT", 0)[:, 0:2 * P].rearrange("p (a n) -> p a n", a=2))
                drain("CT", 0, CT[:, :, :], src=bank("CT", 0)[:, 0:2 * P].rearrange("p (a n) -> p a n", a=2))
                act.wait_ge(gexp_in, 1)
                act.activation(gates[:, :, :], logits[:, :, :], ACT.Exp).then_inc(gexp_done, 1)
                for c in range(NC):
                    drain("u", c, rot_x[:, CH * c:CH * (c + 1)])
                    drain("w", c, w_in[:, CH * c:CH * (c + 1)])
                for c in LATE_V:
                    drain_v(c)
                for c in range(NC):
                    drain("combT", c, combT[:, CH * c:CH * (c + 1)], src=bank("combT", c)[0:NE, :])
                for c in range(NC):
                    drain("bias", c, gate_sb[:, TPC * c:TPC * (c + 1), :],
                          src=bank("bias", c).rearrange("p (t d) -> p t d", d=D))
                act.wait_ge(comb_done, 1)
                act.wait_ge(parts_done, 2 * NC)
                for n in range(2 * HELPED):
                    t, half = helped_job(n)
                    if n >= 4:
                        act.wait_ge(sum_steps, 4 * (n // 2 - 1))
                    act.wait_ge(filled, nth["helped", n][0] + 1)
                    for k in range(NE // 2):
                        e = NE // 2 * half + k
                        ins = act.activation(eo[:, n // 2 % 2, e, :], bank("helped", n)[:, P * k:P * (k + 1)],
                                             ACT.Identity, scale=gates[:, t, e:e + 1])
                    ins.then_inc(act_drained, 1)

            @block.tensor
            def _(pe):
                def begin(kind, c):
                    n = nth[kind, c][0]
                    if n >= 8:
                        k, cc, eng = jobs[n - 8]
                        pe.wait_ge(drained[eng], nth[k, cc][1])
                    return bank(kind, c)

                pe.wait_ge(consts_made, 5)
                for c in range(NC):
                    to = begin("xT", c)
                    for t in range(TPC):
                        pe.wait_ge(xn_done, TPC * c + t + 1)
                        mm = pe.transpose(to[:, P * t:P * (t + 1)], xn_sb[:, TPC * c + t, :], ident[:, :])
                    mm.then_inc(filled, 1)
                pe.wait_ge(att_loaded, 4 * 16)

                def project(kind, c):
                    pe.wait_ge(act_drained, nth["xT", c][1])
                    to = begin(kind, c)
                    if kind == "v":
                        for t in range(TPC):
                            mm = pe.matmul(to[:, P * t:P * (t + 1)], xT[:, CH * c + P * t:CH * c + P * (t + 1)],
                                           w0_sb[:, 2, :], start=True, stop=True)
                    else:
                        mm = pe.matmul(to, w0_sb[:, 0 if kind == "q" else 1, :], xT[:, CH * c:CH * (c + 1)],
                                       start=True, stop=True)
                    mm.then_inc(filled, 1)

                for kind, c in QKV:
                    project(kind, c)
                pe.wait_ge(diag_done, 6)
                to = begin("BT", 0)
                for a in range(2):
                    mm = pe.transpose(to[:, P * a:P * (a + 1)], B_sb[:, a, :], ident[:, :])
                mm.then_inc(filled, 1)
                to = begin("CT", 0)
                for a in range(2):
                    mm = pe.transpose(to[:, P * a:P * (a + 1)], C_sb[:, a, :], ident[:, :])
                mm.then_inc(filled, 1)
                pe.wait_ge(gw_loaded, 2 * 16)
                to = begin("logits", 0)
                for t in range(NT):
                    mm = pe.matmul(to[:, NE * t:NE * (t + 1)], xT[:, P * t:P * (t + 1)], wg_sb[:, :],
                                   start=True, stop=True)
                mm.then_inc(filled, 1)
                pe.wait_ge(act_drained, nth["CT", 0][1])
                for c in range(NC):
                    for a, kind in enumerate(("u", "w")):
                        pe.matmul(begin(kind, c), BT[:, a, :], xT[:, CH * c:CH * (c + 1)],
                                  start=True, stop=True).then_inc(filled, 1)
                for c in LATE_V:
                    project("v", c)
                pe.wait_ge(comb_done, 1)
                for c in range(NC):
                    to = begin("combT", c)
                    for t in range(TPC):
                        mm = pe.transpose(to[0:NE, P * t:P * (t + 1)], gates[:, TPC * c + t, :], ident[:, :])
                    mm.then_inc(filled, 1)
                pe.wait_ge(moe_loaded, 2 * 16)
                for c in range(NC):
                    pe.wait_ge(act_drained, nth["combT", c][1])
                    to = begin("bias", c)
                    for t in range(TPC):
                        mm = pe.matmul(to[:, P * t:P * (t + 1)], combT[:, CH * c + P * t:CH * c + P * (t + 1)],
                                       be_sb[:, :], start=True, stop=True)
                    mm.then_inc(filled, 1)
                for kind, n in EXPERTS:
                    t, half = expert_job(n) if kind == "experts" else helped_job(n)
                    pe.matmul(begin(kind, n), xT[:, P * t:P * (t + 1)],
                              we_sb[:, NE // 2 * half:NE // 2 * (half + 1), :].rearrange("p e f -> p (e f)"),
                              start=True, stop=True).then_inc(filled, 1)

            @block.vector
            def _(dve):
                for h in range(2):
                    tiles = range(HT * h, HT * (h + 1))
                    done = (2 * HT + 1) * h
                    dve.wait_ge(x_loaded[h], 16)
                    for t in tiles:
                        dve.bn_stats(stats[:, t, :], x_sb[:, t, :]).then_inc(stats_done, 1)
                    dve.wait_ge(stats_done, done + HT)
                    for t in tiles:
                        dve.bn_aggr(mv[:, t, :], stats[:, t, :]).then_inc(stats_done, 1)
                    dve.wait_ge(stats_done, done + 2 * HT)
                    half = slice(HT * h, HT * (h + 1))
                    dve.tensor_scalar(var_eps[:, half], mv[:, half, 1], EPS, None, ALU.add).then_inc(stats_done, 1)
                def halve_theta():
                    dve.wait_ge(prm_done, 2)
                    th = eprm[:, 0:1]
                    dve.tensor_scalar(ang_i[:, :], th, 1.0 / (TWO_PI_HI + TWO_PI_LO), None, ALU.mult)\
                       .then_inc(angle_steps, 1)
                    dve.wait_ge(angle_steps, 1)
                    dve.tensor_copy(ang[:, 0:1], ang_i[:, :]).then_inc(angle_steps, 1)
                    dve.wait_ge(angle_steps, 2)
                    dve.scalar_tensor_tensor(out=ang[:, 1:2], in0=ang[:, 0:1], scalar=-TWO_PI_HI, in1=th,
                                             op0=ALU.mult, op1=ALU.add).then_inc(angle_steps, 1)
                    dve.wait_ge(angle_steps, 3)
                    dve.scalar_tensor_tensor(out=ang[:, 6:7], in0=ang[:, 0:1], scalar=-TWO_PI_LO, in1=ang[:, 1:2],
                                             op0=ALU.mult, op1=ALU.add).then_inc(angle_steps, 1)
                    dve.wait_ge(angle_steps, 4)
                    dve.tensor_scalar(ang[:, 2:3], ang[:, 6:7], 0.5, None, ALU.mult).then_inc(angle_steps, 1)
                    dve.wait_ge(angle_steps, 5)
                    dve.scalar_tensor_tensor(out=ang[:, 7:8], in0=ang[:, 2:3], scalar=-1.0, in1=ang[:, 2:3],
                                             op0=ALU.mult, op1=ALU.max).then_inc(angle_steps, 1)
                    dve.wait_ge(angle_steps, 6)
                    dve.tensor_scalar(ang[:, 3:4], ang[:, 7:8], -1.0, PI_2, ALU.mult, ALU.add).then_inc(angle_steps, 1)

                for h in range(2):
                    half = slice(HT * h, HT * (h + 1))
                    dve.wait_ge(std_done, h + 1)
                    dve.reciprocal(rstd[:, half], std[:, half]).then_inc(rstd_done, 1)
                    dve.wait_ge(rstd_done, h + 1)
                    for t in range(HT * h, HT * (h + 1)):
                        dve.tensor_scalar(xn_sb[:, t, :], x_sb[:, t, :], mv[:, t, 0:1], rstd[:, t:t + 1],
                                          ALU.subtract, ALU.mult).then_inc(xn_done, 1)
                    if h == 0:
                        halve_theta()
                gam = eprm[:, 2:3]
                lo, hi = slice(0, HID), slice(HID, 2 * HID)
                dve.wait_ge(rec_loaded, 9 * 16)
                dve.tensor_scalar(B_sb[:, 0, :], B_sb[:, 0, :], gam, None, ALU.mult).then_inc(diag_done, 1)
                dve.tensor_scalar(B_sb[lo, 1, :], B_sb[lo, 1, :], gam[lo], None, ALU.mult).then_inc(diag_done, 1)
                dve.tensor_scalar(B_sb[hi, 1, :], B_sb[hi, 1, :], gam[hi], -1.0, ALU.mult, ALU.mult)\
                   .then_inc(diag_done, 1)
                dve.tensor_scalar(C_sb[:, 0, HID:], C_sb[:, 0, HID:], -1.0, None, ALU.mult).then_inc(diag_done, 1)
                dve.tensor_scalar(C_sb[:, 1, :], C_sb[:, 1, :], -1.0, None, ALU.mult).then_inc(diag_done, 1)
                dve.wait_ge(consts_made, 10)
                dve.tensor_scalar(D_diag[:, :], ident[:, :], D_col[:, 0:1], None, ALU.mult).then_inc(diag_done, 1)
                def low(m):
                    dve.wait_ge(mid_done, m + 1)
                    dve.tensor_tensor(qk_part(m, 2), rest[:, m % 4, :], qk_part(m, 1), ALU.subtract).then_inc(parts_done, 1)

                for m in range(2 * NC):
                    n, c = m // NC, m % NC
                    kind = ("q", "k")[n]
                    dve.wait_ge(hi_done, m + 1)
                    if m >= 4:
                        dve.wait_ge(parts_done, m - 3)
                    dve.scalar_tensor_tensor(out=rest[:, m % 4, :], in0=bank(kind, c), scalar=bqk_col[:, n:n + 1],
                                             in1=qk_part(m, 0), op0=ALU.add, op1=ALU.subtract).then_inc(rest_done, 1)
                    dve.wait_ge(rest_done, m + 1)
                    dve.sem_inc(dve_drained, 1)
                    if m > 0:
                        low(m - 1)
                low(2 * NC - 1)
                gs = 0
                def gstep(ins):
                    nonlocal gs
                    gs += 1
                    ins.then_inc(gate_steps, 1)
                    dve.wait_ge(gate_steps, gs)
                dve.wait_ge(filled, nth["logits", 0][0] + 1)
                src = bank("logits", 0)[:, 0:NT * NE].rearrange("p (t e) -> p t e", e=NE)
                dve.wait_ge(gw_loaded, 2 * 16)
                dve.tensor_tensor(logits[:, :, :], src, bg_all[:, :].unsqueeze(1).broadcast_to([P, NT, NE]), ALU.add)\
                   .then_inc(dve_drained, 1)
                dve.wait_ge(dve_drained, nth["logits", 0][1])
                gstep(dve.tensor_reduce(gmax[:, :], logits[:, :, :], AX.X, ALU.max))
                gstep(dve.tensor_tensor(logits[:, :, :], logits[:, :, :], gmax[:, :].unsqueeze(2).broadcast_to([P, NT, NE]),
                                        ALU.subtract))
                dve.sem_inc(gexp_in, 1)
                dve.wait_ge(gexp_done, 1)
                gstep(dve.tensor_reduce(gsum[:, :], gates[:, :, :], AX.X, ALU.add))
                gstep(dve.reciprocal(gmax[:, :], gsum[:, :]))
                gstep(dve.tensor_tensor(gates[:, :, :], gates[:, :, :], gmax[:, :].unsqueeze(2).broadcast_to([P, NT, NE]),
                                        ALU.mult))
                mine = gates[:, :, :].unsqueeze(3).broadcast_to([P, NT, NE, NE])
                other = gates[:, :, :].unsqueeze(2).broadcast_to([P, NT, NE, NE])
                gstep(dve.tensor_tensor(beats[:, :, :, :], other, mine, ALU.is_gt))
                gstep(dve.tensor_tensor(ties[:, :, :, :], other, mine, ALU.is_equal))
                gstep(dve.tensor_tensor(ties[:, :, :, :].rearrange("p t e j -> p t (e j)"),
                                        ties[:, :, :, :].rearrange("p t e j -> p t (e j)"),
                                        lower[:, :, :].rearrange("p e j -> p (e j)").unsqueeze(1).broadcast_to([P, NT, NE * NE]),
                                        ALU.mult))
                gstep(dve.tensor_tensor(beats[:, :, :, :], beats[:, :, :, :], ties[:, :, :, :], ALU.add))
                gstep(dve.tensor_reduce(logits[:, :, :], beats[:, :, :, :], AX.X, ALU.add))
                dve.scalar_tensor_tensor(out=gates[:, :, :], in0=logits[:, :, :], scalar=2.0, in1=gates[:, :, :],
                                         op0=ALU.is_lt, op1=ALU.mult).then_inc(comb_done, 1)
                dve.wait_ge(comb_done, 1)
                dve.wait_ge(table_steps, POOL_STEPS)
                ls = 0
                def lstep(ins):
                    nonlocal ls
                    ls += 1
                    ins.then_inc(long_steps, 1)
                    dve.wait_ge(long_steps, ls)
                for level in range(POOL_LEVELS, LEVELS):
                    size = 1 << level
                    c1, s1 = pw[:, level, 0:1], pw[:, level, 1:2]
                    a, b = slice(0, size), slice(size, 2 * size)
                    lstep(dve.tensor_scalar(rot_tmp[:, a], sin_t[:, a], s1, None, ALU.mult))
                    lstep(dve.scalar_tensor_tensor(out=cos_t[:, b], in0=cos_t[:, a], scalar=c1,
                                                   in1=rot_tmp[:, a], op0=ALU.mult, op1=ALU.subtract))
                    lstep(dve.tensor_scalar(rot_tmp[:, a], cos_t[:, a], s1, None, ALU.mult))
                    lstep(dve.scalar_tensor_tensor(out=sin_t[:, b], in0=sin_t[:, a], scalar=c1,
                                                   in1=rot_tmp[:, a], op0=ALU.mult, op1=ALU.add))
                for n in range(0, OWN_JOBS, 2):
                    if n == SCAN_AT:
                        dve.wait_ge(rot_done, 3 * NC)
                        dve.tensor_tensor_scan(state, r_col[:, 0:1].broadcast_to([P, S]), rot_x, 0.0,
                                               ALU.mult, ALU.add).then_inc(scan_done, 1)
                    for k in range(NE // 2):
                        for m in (n, n + 1):
                            t, half = expert_job(m)
                            e = NE // 2 * half + k
                            if k == 0:
                                dve.wait_ge(filled, nth["experts", m][0] + 1)
                                if half == 0:
                                    dve.wait_ge(act_drained, nth["bias", t // TPC][1])
                                else:
                                    dve.wait_ge(dve_drained, nth["experts", m - 2][1])
                            else:
                                dve.wait_ge(moe_steps, (NE // 2 - 1) * n + 2 * (k - 1) + m - n + 1)
                            dve.scalar_tensor_tensor(
                                out=gate_sb[:, t, :], in0=bank("experts", m)[:, P * k:P * (k + 1)],
                                scalar=gates[:, t, e:e + 1], in1=gate_sb[:, t, :], op0=ALU.mult, op1=ALU.add)\
                               .then_inc(moe_steps if k < NE // 2 - 1 else dve_drained, 1)

        NMAX = 2 * 2 * TPC * NC
        NEXP = 2 * NT
        TURN_STEP = NT - 3
        MAX_COUNTS = [NMAX // NT + (s in (4, 8)) - 2 * (s == TURN_STEP) for s in range(NT)]
        scores_ready = sem("scores_ready")
        probs_ready = sem("probs_ready")
        probs_used = sem("probs_used")
        ring_filled = sem("ring_filled")
        ring_drained = sem("ring_drained")
        max_joined = sem("max_joined")
        max_hi = sem("max_hi")
        out_drained = sem("out_drained")
        out_rden = sem("out_rden")
        y_filled = sem("y_filled")
        y_drained = sem("y_drained")

        exp_ps = [ps[:, 2 * t:2 * t + 2, :] for t in range(2)]
        av_ps = ps[:, 4, :]
        ring_ps = [ps[:, 5 + n, :] for n in range(3)]
        MCOLS = 2 * 2 * TPC

        AHEAD = sum(MAX_COUNTS[TURN_STEP:])

        def max_range(s):
            first = AHEAD + sum(MAX_COUNTS[:s]) if s < TURN_STEP else sum(MAX_COUNTS[TURN_STEP:s])
            return range(first, first + MAX_COUNTS[s])

        OUT_STEP = 2
        OUT_JOB = max_range(OUT_STEP).stop
        JOBS = NMAX + 2
        assert JOBS % len(ring_ps) == 0

        def max_job(m):
            return m + (m >= OUT_JOB)

        def ring(j):
            return ring_ps[j % len(ring_ps)]

        def max_tile(m):
            return m % 2, m // 2 % 2, m // (4 * NC), m // 4 % NC

        def for_blocks(eng, body):
            body(0, 0, 0)
            with eng.Fori(0, NB // 2 - 2) as i:
                body(2 * i + 1, 1, i)
                body(2 * i + 2, 0, i + 1)
            for b in range(NB - 3, NB):
                body(b, b % 2, b // 2)

        def static(b):
            return isinstance(b, int)

        z_sum = sem("z_sum")
        z_exp = sem("z_exp")
        gate0_steps = sem("gate0_steps")
        x1_done = sem("x1_done")
        stats1_done = sem("stats1_done")
        std1_done = sem("std1_done")
        xn1_done = sem("xn1_done")
        turned1 = sem("turned1")
        xT1_done = sem("xT1_done")
        pads_made = sem("pads_made")
        hid_ready = sem("hid_ready")
        hid_done = sem("hid_done")
        mlp_ready = sem("mlp_ready")
        rstd1_done = sem("rstd1_done")
        mlp_done = sem("mlp_done")
        gz_done = sem("gz_done")
        whole = TPC * (NC - 1)
        xn1 = cut(8 * S, S).rearrange("p (t d) -> p t d", d=D)

        def flat(a):
            return a[:, :, :].rearrange("p t d -> p (t d)")

        def chunk(a, c):
            return a[:, CH * c:CH * (c + 1)]

        z_flat, y_flat, gate_flat, x_flat = flat(attn_sb), flat(y_sb), flat(gate_sb), flat(x_sb)

        def sum_z(dve, c):
            dve.tensor_tensor(chunk(z_flat, c), chunk(z_flat, c), chunk(gate_flat, c), ALU.add).then_inc(z_sum, 1)
            dve.wait_ge(z_sum, c + 1)
            dve.tensor_tensor(chunk(gz, c), chunk(z_flat, c), chunk(y_flat, c), ALU.mult).then_inc(gz_done, 1)

        def exp_z(act, c):
            act.wait_ge(z_sum, c + 1)
            act.activation(chunk(ez, c), chunk(z_flat, c), ACT.Exp, scale=-1.0).then_inc(z_exp, 1)

        def end_layer0(dve, c):
            dve.wait_ge(z_exp, c + 1)
            dve.tensor_scalar(chunk(ez, c), chunk(ez, c), 1.0, None, ALU.add).then_inc(gate0_steps, 1)
            dve.wait_ge(gate0_steps, 3 * c + 1)
            dve.reciprocal(chunk(ez, c), chunk(ez, c)).then_inc(gate0_steps, 1)
            dve.wait_ge(gate0_steps, 3 * c + 2)
            dve.wait_ge(gz_done, c + 1)
            dve.tensor_tensor(chunk(gz, c), chunk(gz, c), chunk(ez, c), ALU.mult).then_inc(gate0_steps, 1)
            dve.wait_ge(gate0_steps, 3 * c + 3)
            dve.tensor_tensor(chunk(x_flat, c), chunk(x_flat, c), chunk(gz, c), ALU.add).then_inc(x1_done, 1)
            dve.wait_ge(x1_done, c + 1)
            tiles = range(TPC * c, TPC * (c + 1))
            for t in tiles:
                dve.bn_stats(stats[:, t, :], x_sb[:, t, :]).then_inc(stats1_done, 1)
            dve.wait_ge(stats1_done, (2 * TPC + 1) * c + TPC)
            for t in tiles:
                dve.bn_aggr(mv[:, t, :], stats[:, t, :]).then_inc(stats1_done, 1)
            dve.wait_ge(stats1_done, (2 * TPC + 1) * c + 2 * TPC)
            dve.tensor_scalar(var_eps[:, tiles[0]:tiles[-1] + 1], mv[:, tiles[0]:tiles[-1] + 1, 1], EPS, None, ALU.add)\
               .then_inc(stats1_done, 1)

        with nc.Block() as block:
            @block.sync
            def _(sp):
                def load_max_rows(par):
                    for g in range(2):
                        for a in range(2):
                            row = 64 * g + KR + a
                            sp.dma_start(qexp[par][row:row + 1, g, :, :].rearrange("p t (s q) -> p (t s) q", q=P),
                                         max_rows[2 * TPC * g:2 * TPC * (g + 1), a, :])\
                              .then_inc(eops_loaded[par], 16)

                def body(b, par, k):
                    if not static(b) or b < NB - 1:
                        if not static(b) or b + 2 < NB:
                            sp.wait_ge(ring_filled, JOBS * (b + 1))
                            load_operands(sp, qmax[par], kmax[par], b + 2, mops_loaded[par])
                        if not static(b) or b > 0:
                            sp.wait_ge(scores_ready, NEXP * b)
                        load_operands(sp, qexp[1 - par], kexp[1 - par], b + 1, eops_loaded[1 - par])
                        sp.wait_ge(ring_drained, JOBS * (b + 2))
                        load_max_rows(1 - par)

                sp.wait_ge(rows_set, 3)
                load_operands(sp, qmax[1], kmax[1], 1, mops_loaded[1])
                sp.wait_ge(ring_drained, JOBS)
                load_max_rows(0)
                for_blocks(sp, body)
                for par in range(2):
                    sp.wait_ge(mops_loaded[par], 8 * 16 * (NB // 2))

            @block.gpsimd
            def _(pool):
                def body(b, par, k):
                    if not static(b) or b < NB - 1:
                        if not static(b) or b > 0:
                            pool.wait_ge(probs_used, NT * b)
                        stage_values(pool, b + 1, 1 - par)

                sum_helped(pool, HELPED - 1)
                pool.wait_ge(sum_steps, 4 * HELPED)
                pool.memset(k_places[1], ONES).then_inc(rows_set, 1)
                pool.memset(v_places, 0.0).then_inc(rows_set, 1)
                pool.wait_ge(rows_set, 4)
                for n in range(2):
                    pool.memset(vst[n][:, :, :, HD0:HD0 + 1], 1.0).then_inc(rows_set, 1)
                pool.wait_ge(rows_set, 6)
                stage_values(pool, 0, 0)
                for_blocks(pool, body)

            @block.tensor
            def _(pe):
                def ring_free(b, j):
                    if not static(b) or b > 0 or j >= len(ring_ps):
                        pe.wait_ge(ring_drained, JOBS * b + j - len(ring_ps) + 1)

                def max_scores(b, par, ms):
                    for m in ms:
                        g, t, qs, kc = max_tile(m)
                        ring_free(b, max_job(m))
                        pe.matmul(ring(max_job(m)), qmax[par][:, g, t, P * qs:P * (qs + 1)],
                                  kmax[par][:, t, CH * kc:CH * (kc + 1)], start=True, stop=True)\
                          .then_inc(ring_filled, 1)

                def turn_max(b):
                    pe.wait_ge(max_joined, b + 1)
                    ring_free(b, JOBS - 1)
                    pe.transpose(ring(JOBS - 1)[0:MCOLS, 0:P], neg_max[:, :], ident[:, :]).then_inc(ring_filled, 1)

                def scores_T(b, par, s, t):
                    if not static(b) or b > 0 or s > 0:
                        pe.wait_ge(probs_ready, NEXP * b + 2 * s + t - 1)
                    else:
                        pe.wait_ge(y_drained, NC)
                    for g in range(2):
                        mm = pe.matmul(exp_ps[t][:, g, :], kexp[par][:, t, P * s:P * (s + 1)],
                                       qexp[par][:, g, t, :], start=True, stop=True)
                    mm.then_inc(scores_ready, 1)

                def values(b, par, s):
                    pe.wait_ge(probs_ready, NEXP * b + 2 * s + 2)
                    if s == 0:
                        pe.wait_ge(v_staged, b + 1)
                        if not static(b) or b > 0:
                            pe.wait_ge(out_drained, b)
                    for j in range(G0):
                        t, g = j // 2, j % 2
                        mm = pe.matmul(av_ps[32 * j:32 * (j + 1), :], vst[par][:, s, j, :],
                                       probs[2 * (s % 2) + t][:, g, :], start=(s == 0), stop=(s == NT - 1))
                    mm.then_inc(probs_used, 1)

                def turn_out(b, par, jb, j):
                    pe.wait_ge(out_drained, b + 1)
                    ring_free(jb, j)
                    for qs in range(TPC):
                        mm = pe.transpose(ring(j)[:, P * qs:P * (qs + 1)], outT0[par][:, P * qs:P * (qs + 1)],
                                          ident[:, :])
                    mm.then_inc(ring_filled, 1)

                def empty_job(b):
                    pe.wait_ge(ring_drained, JOBS * b + OUT_JOB)
                    pe.sem_inc(ring_filled, 1)

                def body(b, par, k):
                    more = not static(b) or b < NB - 1
                    later = not static(b) or b > 0
                    more2 = not static(b) or b + 2 < NB
                    for s in range(NT):
                        ms = max_range(s) if (more if s < TURN_STEP else more2) else range(0)
                        if s > TURN_STEP:
                            mb, mpar = b + 2, par
                        else:
                            mb, mpar = b + 1, 1 - par
                        if s == 0:
                            pe.wait_ge(eops_loaded[par], 12 * 16 * (k + 1))
                        if s == TURN_STEP:
                            scores_T(b, par, s, 0)
                            scores_T(b, par, s, 1)
                            if more:
                                turn_max(b + 1)
                            values(b, par, s - 1)
                            if more2:
                                pe.wait_ge(mops_loaded[par], 8 * 16 * (k + 2))
                                max_scores(b + 2, par, ms)
                            continue
                        max_scores(mb, mpar, ms[0:1])
                        scores_T(b, par, s, 0)
                        max_scores(mb, mpar, ms[1:2])
                        scores_T(b, par, s, 1)
                        early = 4 if s == TURN_STEP - 1 else 3
                        max_scores(mb, mpar, ms[2:early])
                        if s > 0:
                            values(b, par, s - 1)
                        elif later:
                            values(b - 1, 1 - par, NT - 1)
                        max_scores(mb, mpar, ms[early:])
                        if s == OUT_STEP:
                            if more and later:
                                turn_out(b - 1, 1 - par, b + 1, OUT_JOB)
                            elif more:
                                empty_job(b + 1)
                            else:
                                turn_out(b - 1, 1 - par, NB, 0)

                pe.wait_ge(mops_loaded[0], 8 * 16)
                assert 3 * NT <= NMAX
                for m in range(NMAX):
                    if m == OUT_JOB:
                        empty_job(0)
                    max_scores(0, 0, range(m, m + 1))
                    if m < 3 * NT:
                        t, part = m // 3, m % 3
                        tok = slice(P * t, P * (t + 1))
                        left, right = ((st_cos, CT[:, 0, :]), (st_sin, CT[:, 1, :]), (xT, D_diag[:, :]))[part]
                        mm = pe.matmul(ps[:, t // TPC, P * (t % TPC):P * (t % TPC + 1)], left[:, tok], right,
                                       start=(part == 0), stop=(part == 2))
                        if part == 2 and t % TPC == TPC - 1:
                            mm.then_inc(y_filled, 1)
                turn_max(0)
                pe.wait_ge(mops_loaded[1], 8 * 16)
                max_scores(1, 1, range(AHEAD))
                for_blocks(pe, body)
                values(NB - 1, 1, NT - 1)
                turn_out(NB - 1, 1, NB, 1)

            @block.scalar
            def _(act):
                def drain_out(b, par):
                    act.wait_ge(probs_used, NT * (b + 1))
                    act.activation(outT0[par], av_ps, ACT.Copy).then_inc(out_drained, 1)

                def body(b, par, k):
                    later = not static(b) or b > 0
                    for s in range(NT):
                        if s == 1 and later:
                            drain_out(b - 1, 1 - par)
                        for t in range(2):
                            act.wait_ge(scores_ready, NEXP * b + 2 * s + t + 1)
                            if s >= 2 or later:
                                act.wait_ge(probs_used, NT * b + s - 1)
                            act.activation(probs[2 * (s % 2) + t], exp_ps[t], ACT.Exp, scale=SC0)\
                               .then_inc(probs_ready, 1)
                        if static(b) and b == NB - 1 and s % 3 == 2 and s // 3 - 1 in range(NC - 1):
                            exp_z(act, s // 3 - 1)

                for c in range(NC):
                    act.wait_ge(y_filled, c + 1)
                    act.activation(chunk(y_flat, c), ps[:, c, :], ACT.Copy).then_inc(y_drained, 1)
                for_blocks(act, body)
                drain_out(NB - 1, 1)
                act.wait_ge(stats1_done, (2 * TPC + 1) * (NC - 1))
                act.activation(std[:, 0:whole], var_eps[:, 0:whole], ACT.Sqrt).then_inc(std1_done, 1)

            @block.vector
            def _(dve):
                def reduce_tiles(b, ms):
                    for m in ms:
                        g, t, qs, kc = max_tile(m)
                        dve.wait_ge(ring_filled, JOBS * b + max_job(m) + 1)
                        col = (2 * g + t) * TPC + qs
                        dve.tensor_reduce(tile_max[:, col, kc:kc + 1], ring(max_job(m)), AX.X, ALU.max)\
                           .then_inc(ring_drained, 1)

                def join_max(b):
                    dve.wait_ge(ring_drained, JOBS * (b + 1) - 1)
                    dve.tensor_reduce(neg_max[:, :], tile_max[:, :, :], AX.X, ALU.max, negate=True)\
                       .then_inc(max_joined, 1)

                def split_max(b):
                    turned = ring(JOBS - 1)[0:MCOLS, 0:P]
                    dve.wait_ge(ring_filled, JOBS * (b + 1))
                    dve.tensor_copy(max_rows[:, 0, :], turned).then_inc(max_hi, 1)
                    dve.wait_ge(max_hi, b + 1)
                    dve.tensor_tensor(max_rows[:, 1, :], turned, max_rows[:, 0, :], ALU.subtract)\
                       .then_inc(ring_drained, 1)

                def norm_out(b, jb, j):
                    dve.wait_ge(ring_drained, JOBS * jb + j)
                    dve.wait_ge(ring_filled, JOBS * jb + j + 1)
                    sums = ring(j).rearrange("p (a j d) -> p (a j) d", j=G0, d=32)
                    dve.reciprocal(rden0[:, :], sums[:, :, HD0]).then_inc(out_rden, 1)
                    dve.wait_ge(out_rden, b + 1)
                    dve.tensor_tensor(
                        attn_sb[:, ds(b // NG0 * TPC, TPC), ds(b % NG0 * (G0 * HD0), G0 * HD0)]
                        .rearrange("p a (j d) -> p a j d", d=HD0),
                        ring(j).rearrange("p (a j d) -> p a j d", j=G0, d=32)[:, :, :, 0:HD0],
                        rden0[:, :].rearrange("p (a j) -> p a j", j=G0).unsqueeze(3).broadcast_to([P, TPC, G0, HD0]),
                        ALU.mult).then_inc(ring_drained, 1)

                def empty_job(b):
                    dve.wait_ge(ring_filled, JOBS * b + OUT_JOB + 1)
                    dve.sem_inc(ring_drained, 1)

                def body(b, par, k):
                    if static(b) and b == NB - 1:
                        norm_out(b - 1, NB, 0)
                        dve.wait_ge(ring_drained, JOBS * NB + 1)
                        for c in range(NC - 1):
                            sum_z(dve, c)
                        for c in range(NC - 1):
                            end_layer0(dve, c)
                        return
                    reduce_tiles(b + 1, range(AHEAD, OUT_JOB))
                    if static(b) and b == 0:
                        empty_job(b + 1)
                    else:
                        norm_out(b - 1, b + 1, OUT_JOB)
                    reduce_tiles(b + 1, range(OUT_JOB, NMAX))
                    join_max(b + 1)
                    split_max(b + 1)
                    if not static(b) or b + 2 < NB:
                        reduce_tiles(b + 2, range(AHEAD))

                reduce_tiles(0, range(OUT_JOB))
                empty_job(0)
                reduce_tiles(0, range(OUT_JOB, NMAX))
                join_max(0)
                split_max(0)
                reduce_tiles(1, range(AHEAD))
                for_blocks(dve, body)
                norm_out(NB - 1, NB, 1)

        with nc.Block() as block:
            @block.vector
            def _(dve):
                def normalise(c):
                    for t in range(TPC * c, TPC * (c + 1)):
                        dve.tensor_scalar(xn1[:, t, :], x_sb[:, t, :], mv[:, t, 0:1], rstd[:, t:t + 1],
                                          ALU.subtract, ALU.mult).then_inc(xn1_done, 1)

                last = NC - 1
                sum_z(dve, last)
                dve.wait_ge(std1_done, 1)
                dve.reciprocal(rstd[:, 0:whole], std[:, 0:whole]).then_inc(rstd1_done, 1)
                dve.wait_ge(rstd1_done, 1)
                for c in range(last):
                    normalise(c)
                end_layer0(dve, last)
                dve.wait_ge(std1_done, 2)
                dve.reciprocal(rstd[:, whole:], std[:, whole:]).then_inc(rstd1_done, 1)
                dve.wait_ge(rstd1_done, 2)
                normalise(last)
                for c in range(NC):
                    dve.wait_ge(mlp_ready, c + 1)
                    dve.tensor_tensor(gate_sb[:, TPC * c:TPC * (c + 1), :],
                                      ps[:, c, :].rearrange("p (t d) -> p t d", d=D),
                                      b2_all[:, :].unsqueeze(1).broadcast_to([P, TPC, D]), ALU.add).then_inc(mlp_done, 1)

            @block.scalar
            def _(act):
                def drain_xT(c):
                    act.wait_ge(turned1, c + 1)
                    act.activation(xT[:, CH * c:CH * (c + 1)], ps[:, c, :], ACT.Copy).then_inc(xT1_done, 1)

                def drain_hidden(c):
                    for n in range(NI * c, NI * (c + 1)):
                        i = n % NI
                        act.wait_ge(hid_ready, n + 1)
                        act.activation(hT[:, i, CH * c:CH * (c + 1)], ps[:, 4 + n % 4, :], ACT.Relu,
                                       bias=b1_sb[:, i:i + 1]).then_inc(hid_done, 1)

                exp_z(act, NC - 1)
                drain_xT(0)
                for c in range(1, NC - 1):
                    drain_xT(c)
                    drain_hidden(c - 1)
                act.wait_ge(stats1_done, (2 * TPC + 1) * NC)
                act.activation(std[:, whole:], var_eps[:, whole:], ACT.Sqrt).then_inc(std1_done, 1)
                drain_xT(NC - 1)
                drain_hidden(NC - 2)
                drain_hidden(NC - 1)

            @block.gpsimd
            def _(pool):
                pool.memset(k_pad[64:P, 0, :], 0.0).then_inc(pads_made, 1)
                pool.wait_ge(pads_made, 1)
                pool.memset(k_pad[0:64, 1, :], 0.0).then_inc(pads_made, 1)
                pool.wait_ge(pads_made, 2)
                pool.tensor_copy(wst[:, :, :], w1qkv_sb[:, :, 0:P]).then_inc(pads_made, 1)

            @block.tensor
            def _(pe):
                def turn(c):
                    for t in range(TPC):
                        pe.wait_ge(xn1_done, TPC * c + t + 1)
                        mm = pe.transpose(ps[:, c, P * t:P * (t + 1)], xn1[:, TPC * c + t, :], ident[:, :])
                    mm.then_inc(turned1, 1)

                def hidden(c):
                    pe.wait_ge(xT1_done, c + 1)
                    for n in range(NI * c, NI * (c + 1)):
                        if n >= 4:
                            pe.wait_ge(hid_done, n - 3)
                        pe.matmul(ps[:, 4 + n % 4, :], W1_sb[:, n % NI:NI * P:NI], xT[:, CH * c:CH * (c + 1)],
                                  start=True, stop=True).then_inc(hid_ready, 1)

                def second(c):
                    pe.wait_ge(hid_done, NI * (c + 1))
                    for t in range(TPC):
                        for i in range(NI):
                            mm = pe.matmul(ps[:, c, P * t:P * (t + 1)], hT[:, i, CH * c + P * t:CH * c + P * (t + 1)],
                                           W2_sb[:, i, :], start=(i == 0), stop=(i == NI - 1))
                    mm.then_inc(mlp_ready, 1)

                turn(0)
                for c in range(1, NC - 1):
                    turn(c)
                    hidden(c - 1)
                second(0)
                turn(NC - 1)
                hidden(NC - 2)
                for c in range(1, NC - 2):
                    second(c)
                hidden(NC - 1)
                second(NC - 2)
                second(NC - 1)

        wqk_staged = sem("wqk_staged")
        wv_staged = sem("wv_staged")
        qk_filled = sem("qk_filled")
        q_drained = sem("q_drained")
        k_drained = sem("k_drained")
        v_filled = sem("v_filled")
        v_drained_act = sem("v_drained_act")
        v_drained_dve = sem("v_drained_dve")
        v2_copied = sem("v2_copied")
        s_filled = sem("s_filled")
        s_masked = sem("s_masked")
        mask_turns = sem("mask_turns")
        exped = sem("exped")
        recips = sem("recips")
        normed = sem("normed")
        pT_filled = sem("pT_filled")
        pT_drained = sem("pT_drained")
        av_done = sem("av_done")
        av_drained = sem("av_drained")
        ez1_done = sem("ez1_done")
        gate1_steps = sem("gate1_steps")
        gate1_done = sem("gate1_done")
        GW = S // NP1
        ez1 = rot_tmp[:, 0:GW]
        GATE_STEP = 4
        T_LAG, AV_LAG, OUT_LAG = 3, 4, 5
        VJ = NC + 1
        VA, VD = (VJ + 1) // 2, VJ // 2

        def width(qb):
            return KW if qb else P

        def for_pairs(eng, body):
            with eng.Fori(0, NP1 - 1) as hp:
                body(hp, True)
            body(NP1 - 1, False)

        with nc.Block() as block:
            @block.gpsimd
            def _(pool):
                def body(hp, more):
                    if more:
                        pool.wait_ge(qk_filled, 2 * NC * (hp + 1))
                        pool.tensor_copy(wst[:, 0:2, :], w1qkv_sb[:, 0:2, ds(P * (hp + 1), P)]).then_inc(wqk_staged, 1)
                        pool.wait_ge(v_filled, VJ * (hp + 1))
                        pool.tensor_copy(wst[:, 2:3, :], w1qkv_sb[:, 2:3, ds(P * (hp + 1), P)]).then_inc(wv_staged, 1)
                    for qb in range(NT):
                        pool.wait_ge(recips, NT * hp + qb + 1)
                        p = p1[:, qb % NSLOT, :, 0:width(qb)]
                        pool.tensor_tensor(p, p, rinv1[:, qb % NSLOT, :].unsqueeze(2).broadcast_to([P, 2, width(qb)]),
                                           ALU.mult).then_inc(normed, 1)

                for_pairs(pool, body)

            @block.sync
            def _(sp):
                def body(hp, more):
                    sp.wait_ge(v_drained_act, VA * hp + 1)
                    sp.dma_start(v2[HALF:TAIL, :, :], v1[0:GLOB, 0:1, :].broadcast_to([GLOB, NT - 1, P]))\
                      .then_inc(v2_copied, 16)
                    sp.wait_ge(v_drained_act, VA * (hp + 1))
                    sp.dma_start(v2[0:HALF, :, :], v1[0:HALF, 2:NT + 1, :]).then_inc(v2_copied, 16)

                for_pairs(sp, body)

            @block.tensor
            def _(pe):
                def project_qk(n):
                    c, which = n // 2, n % 2
                    pe.matmul(ps[:, n % 4, :], wst[:, which, :], xT[:, CH * c:CH * (c + 1)],
                              start=True, stop=True).then_inc(qk_filled, 1)

                def project_v(hp, n):
                    if n == 0:
                        pe.wait_ge(wv_staged, hp + 1)
                    if n >= 2 and n % 2:
                        pe.wait_ge(v_drained_dve, VD * hp + n // 2)
                    elif n >= 2:
                        pe.wait_ge(v_drained_act, VA * hp + n // 2)
                    if n == NC:
                        mm = pe.matmul(ps[0:HALF, 4 + n % 2, 0:P], xT[:, S - HALF:S], wst[:, 2, :], start=True, stop=True)
                    else:
                        for t in range(TPC * n, TPC * (n + 1)):
                            first = P * t - HALF if t else 0
                            mm = pe.matmul(ps[:, 4 + n % 2, P * (t % TPC):P * (t % TPC + 1)], xT[:, first:first + P],
                                           wst[:, 2, :], start=True, stop=True)
                    mm.then_inc(v_filled, 1)

                def scores(hp, qb):
                    if qb >= 4:
                        pe.wait_ge(s_masked, 2 * NT * hp + 2 * (qb - 3))
                    to = ps[:, qb % 4, 0:2 * KW].rearrange("p (g n) -> p g n", g=2)
                    q = qT[:, P * qb:P * (qb + 1)]
                    first, wide = (P * qb - HALF, WIN) if qb else (0, P)
                    mm = pe.matmul(to[:, :, 0:wide], q, k_pad[:, :, first:first + wide], start=True, stop=True)
                    if qb:
                        mm = pe.matmul(to[:, :, WIN:KW], q, k_pad[:, :, 0:GLOB], start=True, stop=True)
                    mm.then_inc(s_filled, 1)

                def turn(hp, qb):
                    pe.wait_ge(normed, NT * hp + qb + 1)
                    if qb >= 2:
                        pe.wait_ge(pT_drained, NT * hp + qb - 1)
                    elif qb == 0:
                        pe.wait_ge(v_drained_act, VA * (hp + 1))
                    to = ps[:, 4 + qb % 2, :]
                    for g in range(2):
                        mm = pe.transpose(to[:, P * g:P * (g + 1)], p1[:, qb % NSLOT, g, 0:P], ident[:, :])
                    if qb:
                        for g in range(2):
                            mm = pe.transpose(to[0:TAIL, P * (2 + g):P * (3 + g)],
                                              p1[:, qb % NSLOT, g, P:KW], ident[:, :])
                    mm.then_inc(pT_filled, 1)

                def values(hp, qb):
                    pe.wait_ge(pT_drained, NT * hp + qb + 1)
                    if qb == 1:
                        pe.wait_ge(v2_copied, 32 * (hp + 1))
                    if qb % TPC == 0:
                        pe.wait_ge(av_drained, NC * hp + qb // TPC)
                    to = ps[:, 6 + qb // TPC % 2, P * (qb % TPC):P * (qb % TPC + 1)]
                    for g in range(2):
                        mm = pe.matmul(to[64 * g:64 * (g + 1), :], v1[:, qb, 64 * g:64 * (g + 1)],
                                       pT[:, qb % 4, P * g:P * (g + 1)], start=True, stop=(qb == 0))
                    if qb:
                        for g in range(2):
                            mm = pe.matmul(to[64 * g:64 * (g + 1), :], v2[0:TAIL, qb - 1, 64 * g:64 * (g + 1)],
                                           pT[0:TAIL, qb % 4, P * (2 + g):P * (3 + g)], start=False, stop=True)
                    mm.then_inc(av_done, 1)

                def body(hp, more):
                    for n in range(VJ):
                        project_v(hp, n)
                    pe.wait_ge(q_drained, NC * (hp + 1))
                    pe.wait_ge(k_drained, NC * (hp + 1))
                    for step in range(NT + AV_LAG):
                        if step < NT:
                            scores(hp, step)
                        if 0 <= step - T_LAG < NT:
                            turn(hp, step - T_LAG)
                        if step - AV_LAG >= 0:
                            values(hp, step - AV_LAG)
                        if step >= NT and more:
                            if step == NT:
                                pe.wait_ge(wqk_staged, hp + 1)
                            for n in range(2 * (step - NT), 2 * (step - NT) + 2):
                                if n < 4:
                                    pe.wait_ge(s_masked, 2 * NT * hp + 2 * (NT - 4 + n + 1))
                                else:
                                    pe.wait_ge(k_drained if n % 2 else q_drained, NC * (hp + 1) + n // 2 - 1)
                                project_qk(n)
                    pe.wait_ge(pT_drained, NT * (hp + 1))

                assert AV_LAG == NC
                for n in range(2 * NC):
                    if n >= 4:
                        pe.wait_ge(k_drained if n % 2 else q_drained, n // 2 - 1)
                    project_qk(n)
                for_pairs(pe, body)

            @block.scalar
            def _(act):
                def drain_q(pair, c):
                    act.wait_ge(qk_filled, 2 * NC * pair + 2 * c + 1)
                    act.activation(qT[:, CH * c:CH * (c + 1)], ps[:, 2 * c % 4, :], ACT.Copy).then_inc(q_drained, 1)

                def body(hp, more):
                    for n in range(0, VJ, 2):
                        act.wait_ge(v_filled, VJ * hp + n + 1)
                        if n == NC:
                            act.wait_ge(v_drained_dve, VD * (hp + 1))
                            act.activation(v1[0:HALF, NT, :], ps[0:HALF, 4 + n % 2, 0:P], ACT.Copy).then_inc(v_drained_act, 1)
                        else:
                            act.activation(v1[:, TPC * n:TPC * (n + 1), :],
                                           ps[:, 4 + n % 2, :].rearrange("p (t d) -> p t d", d=P), ACT.Copy)\
                               .then_inc(v_drained_act, 1)
                    act.wait_ge(gate1_done, hp + 1)
                    act.activation(ez1, gate_flat[:, ds(GW * hp, GW)], ACT.Exp, scale=-1.0).then_inc(ez1_done, 1)
                    for step in range(NT + AV_LAG):
                        qb = step - T_LAG
                        if 0 <= qb < NT:
                            act.wait_ge(pT_filled, NT * hp + qb + 1)
                            frm = ps[:, 4 + qb % 2, :]
                            ins = act.activation(pT[:, qb % 4, 0:2 * P], frm[:, 0:2 * P], ACT.Copy)
                            if qb:
                                ins = act.activation(pT[0:TAIL, qb % 4, 2 * P:4 * P], frm[0:TAIL, 2 * P:4 * P], ACT.Copy)
                            ins.then_inc(pT_drained, 1)
                        qb = step
                        if qb < NT:
                            for g in range(2):
                                act.wait_ge(s_masked, 2 * NT * hp + 2 * qb + g + 1)
                                p = p1[:, qb % NSLOT, g, 0:width(qb)]
                                act.activation(p, p, ACT.Exp, scale=-1.0, bias=nmax1[:, qb % NSLOT, g:g + 1],
                                               accum_out=rsum1[:, qb % NSLOT, g:g + 1]).then_inc(exped, 1)
                        if step >= NT and more:
                            drain_q(hp + 1, step - NT)

                for c in range(NC):
                    drain_q(0, c)
                for_pairs(act, body)

            @block.vector
            def _(dve):
                def drain_k(pair, c):
                    dve.wait_ge(qk_filled, 2 * NC * pair + 2 * c + 2)
                    for g in range(2):
                        rows = slice(64 * g, 64 * (g + 1))
                        ins = dve.tensor_copy(k_pad[rows, g, CH * c:CH * (c + 1)], ps[rows, (2 * c + 1) % 4, :])
                    ins.then_inc(k_drained, 1)

                def body(hp, more):
                    for n in range(1, VJ, 2):
                        dve.wait_ge(v_filled, VJ * hp + n + 1)
                        dve.tensor_copy(v1[:, TPC * n:TPC * (n + 1), :],
                                        ps[:, 4 + n % 2, :].rearrange("p (t d) -> p t d", d=P)).then_inc(v_drained_dve, 1)
                    for step in range(NT + OUT_LAG):
                        qb = step
                        if qb < NT:
                            dve.wait_ge(s_filled, NT * hp + qb + 1)
                            if qb >= NSLOT:
                                dve.wait_ge(pT_filled, NT * hp + qb - NSLOT + 1)
                            dve.sem_inc(mask_turns, 1)
                            for g in range(2):
                                dve.tensor_tensor_reduce(
                                    p1[:, qb % NSLOT, g, 0:width(qb)], ps[:, qb % 4, KW * g:KW * g + width(qb)],
                                    masks[:, :] if qb else mask0[:, :], -SC1, BIG, ALU.add, ALU.min,
                                    nmax1[:, qb % NSLOT, g:g + 1]).then_inc(s_masked, 1)
                        qb = step - 1
                        if 0 <= qb < NT:
                            dve.wait_ge(exped, 2 * NT * hp + 2 * (qb + 1))
                            dve.reciprocal(rinv1[:, qb % NSLOT, :], rsum1[:, qb % NSLOT, :]).then_inc(recips, 1)
                        if step == GATE_STEP:
                            dve.wait_ge(ez1_done, hp + 1)
                            dve.tensor_scalar(ez1, ez1, 1.0, None, ALU.add).then_inc(gate1_steps, 1)
                        for half in range(2):
                            if step == GATE_STEP + 1 + half:
                                dve.wait_ge(gate1_steps, 3 * hp + 1)
                                cols = slice(GW // 2 * half, GW // 2 * (half + 1))
                                dve.reciprocal(ez1[:, cols], ez1[:, cols]).then_inc(gate1_steps, 1)
                        if step == GATE_STEP + 3:
                            dve.wait_ge(gate1_steps, 3 * hp + 3)
                            part = gate_flat[:, ds(GW * hp, GW)]
                            dve.tensor_tensor(part, part, ez1, ALU.mult).then_inc(gate1_done, 1)
                        if NT < step <= NT + NC and more:
                            drain_k(hp + 1, step - NT - 1)
                        qb = step - OUT_LAG
                        if qb >= 0 and qb % TPC == TPC - 1:
                            c = qb // TPC
                            dve.wait_ge(av_done, NT * hp + qb + 1)
                            dve.tensor_copy(outT1[:, ds(hp, 1), CH * c:CH * (c + 1)],
                                            ps[:, 6 + c % 2, :].unsqueeze(1)).then_inc(av_drained, 1)

                dve.sem_inc(gate1_done, 1)
                dve.sem_inc(av_drained, 1)
                dve.sem_inc(wv_staged, 1)
                for c in range(NC):
                    drain_k(0, c)
                for_pairs(dve, body)

        o_ready = sem("o_ready")
        o_gated = sem("o_gated")
        x2_done = sem("x2_done")
        stored = sem("stored")
        parts5 = [(TPC * c, TPC * (c + 1)) for c in range(NC - 1)] + [(NT - TPC, NT - 1), (NT - 1, NT)]
        with nc.Block() as block:
            @block.tensor
            def _(pe):
                for n, (t0, t1) in enumerate(parts5):
                    for t in range(t0, t1):
                        for h in range(NP1):
                            mm = pe.matmul(ps[:, n, P * (t - t0):P * (t - t0 + 1)], outT1[:, h, P * t:P * (t + 1)],
                                           wout_sb[:, h, :], start=(h == 0), stop=(h == NP1 - 1))
                    mm.then_inc(o_ready, 1)

            @block.vector
            def _(dve):
                for n, (t0, t1) in enumerate(parts5):
                    cols, in_bank = slice(P * t0, P * t1), slice(0, P * (t1 - t0))
                    dve.wait_ge(o_ready, n + 1)
                    dve.tensor_tensor(tmp[:, n % 2, in_bank], ps[:, n, in_bank], gate_flat[:, cols], ALU.mult)\
                       .then_inc(o_gated, 1)
                    dve.wait_ge(o_gated, n + 1)
                    dve.tensor_tensor(x_flat[:, cols], x_flat[:, cols], tmp[:, n % 2, in_bank], ALU.add)\
                       .then_inc(x2_done, 1)

            @block.sync
            def _(sp):
                for n, (t0, t1) in enumerate(parts5):
                    sp.wait_ge(x2_done, n + 1)
                    sp.dma_start(out[0, P * t0:P * t1, :].rearrange("(t p) d -> p t d", p=P), x_sb[:, t0:t1, :])\
                      .then_inc(stored, 16)
                sp.wait_ge(stored, len(parts5) * 16)


_INS = ['L0_attn_x', 'L0_attn_theta_log', 'L0_attn_nu_log', 'L0_attn_gamma_log', 'L0_attn_B_re', 'L0_attn_B_im',
        'L0_attn_C_re', 'L0_attn_C_im', 'L0_attn_D', 'L0_ffn_W_qkv', 'L0_ffn_b_qkv', 'L0_ffn_W_gate',
        'L0_ffn_b_gate', 'L0_ffn_W_experts', 'L0_ffn_b_experts', 'L1_attn_w_qkv', 'L1_attn_w_out',
        'L1_ffn_W1', 'L1_ffn_b1', 'L1_ffn_W2', 'L1_ffn_b2']
_OUTS = [((1, 2048, 128), 'float32')]


def kernel(**inputs):
    import numpy as _np
    import concourse.bacc as _bacc
    from concourse import mybir as _mybir
    from concourse.bass_utils import run_bass_kernel_spmd as _run

    nc = _bacc.Bacc("TRN2", target_bir_lowering=False, num_devices=1)
    arrays, args = {}, []
    for name in _INS:
        a = _np.ascontiguousarray(inputs[name])
        arrays[f"in_{name}_dram"] = a
        args.append(nc.dram_tensor(f"in_{name}_dram", a.shape, _mybir.dt.from_np(a.dtype), kind="ExternalInput").ap())
    for i, (shape, dtype) in enumerate(_OUTS):
        dt = _mybir.dt.from_np(_np.dtype(dtype))
        args.append(nc.dram_tensor(f"out_{i}_dram", shape, dt, kind="ExternalOutput").ap())
    recurrent_moe_sparse_attention_kernel(nc, *args)
    r = _run(nc, [arrays], core_ids=[0])
    got = tuple(r.results[0][f"out_{i}_dram"] for i in range(len(_OUTS)))
    return got[0]
```
